# Optimizing a Trainium2 kernel written in Bass

```python
import numpy as np
import jax
import jax.numpy as jnp

def _softmax(x, axis=-1):
    return jax.nn.softmax(x, axis=axis)

def _gelu(x):
    return jax.nn.gelu(x, approximate=True)

def _silu(x):
    return jax.nn.silu(x)

def _sigmoid(x):
    return jax.nn.sigmoid(x)

def _layernorm(x, axis=-1, eps=1e-05):
    m = jnp.mean(x, axis=axis, keepdims=True)
    v = jnp.var(x, axis=axis, keepdims=True)
    return (x - m) / jnp.sqrt(v + eps)

def _scatter_add(tgt, idx, src, axis=0):
    return tgt.at[idx].add(src)

def _segment_sum(src, seg, n):
    return jax.ops.segment_sum(src, seg, n)
kernel_name = 'mk_gnn_resnorm_d4_gnn_r16_6ea98e'

def setup_inputs(seed: int=0):
    np.random.seed(seed)
    _w = jnp.asarray

    def _rec_inputs():
        import jax
        import jax.numpy as jnp
        _gk = jax.random.key(seed)
        x = -0.0002117 + 1 * jax.random.normal(jax.random.fold_in(_gk, 1), (6250, 256), jnp.float32)
        src = jax.random.randint(jax.random.fold_in(_gk, 2), (100000,), 0, 6250, jnp.int32)
        dst = jax.random.randint(jax.random.fold_in(_gk, 3), (100000,), 0, 6250, jnp.int32)
        _o = jnp.argsort(dst, stable=True)
        src = src[_o]
        dst = dst[_o]
        edge_weight = jax.random.uniform(jax.random.fold_in(_gk, 13), (100000,), jnp.float32, 0.0, 1)
        edge_weight1 = jax.random.uniform(jax.random.fold_in(_gk, 14), (100000, 1), jnp.float32, 0.0, 0.999998)
        return (x, src, dst, edge_weight, edge_weight1)
    x, src, dst, edge_weight, edge_weight1 = _rec_inputs()

    def _L0_gnn_setup():
        import jax, jax.numpy as jnp
        import numpy as np
        N = 6250
        E = 200000
        F_IN = 256
        F_OUT = 256
        key = jax.random.key(seed)
        k1, k2, k3, k4, k5 = jax.random.split(key, 5)
        x = jax.random.normal(k1, (N, F_IN), dtype=jnp.float32)
        edge_row = jax.random.randint(k2, (E,), 0, N, dtype=jnp.int32)
        edge_col = jax.random.randint(k3, (E,), 0, N, dtype=jnp.int32)
        edge_val = jax.random.uniform(k4, (E,), dtype=jnp.float32)
        W = jax.random.normal(k5, (2 * F_IN, F_OUT), dtype=jnp.float32) * (1.0 / np.sqrt(2 * F_IN))
        b = jnp.zeros((F_OUT,), dtype=jnp.float32)
        return {'x': x, 'edge_row': edge_row, 'edge_col': edge_col, 'edge_val': edge_val, 'W': W, 'b': b}
    _L0_gnn_all = _L0_gnn_setup()
    _L0_gnn_in = {k: v for k, v in _L0_gnn_all.items() if k in ('W', 'b')}
    del _L0_gnn_all

    def _L1_gnn_setup():
        import jax, jax.numpy as jnp
        import numpy as np
        N = 3125
        E = 50000
        F_IN = 256
        HID = 64
        HEADS = 4

        def _segment_softmax(logits, seg, num_segments):
            m = jax.ops.segment_max(logits, seg, num_segments=num_segments)
            e = jnp.exp(logits - m[seg])
            z = jax.ops.segment_sum(e, seg, num_segments=num_segments)
            return e / z[seg]

        def _gat_layer(x, src, dst, W, a_src, a_dst, b, num_nodes):
            H, C = a_src.shape
            h = (x @ W).reshape(num_nodes, H, C)
            al_s = jnp.einsum('nhc,hc->nh', h, a_src)
            al_d = jnp.einsum('nhc,hc->nh', h, a_dst)
            logits = jax.nn.leaky_relu(al_s[src] + al_d[dst], 0.2)
            alpha = _segment_softmax(logits, dst, num_nodes)
            msg = h[src] * alpha[:, :, None]
            out = jax.ops.segment_sum(msg, dst, num_segments=num_nodes)
            return out.reshape(num_nodes, H * C) + b
        key = jax.random.key(seed)
        ks = jax.random.split(key, 12)
        s = 0.05
        x = jax.random.normal(ks[0], (N, F_IN), dtype=jnp.float32)
        edge_index = jax.random.randint(ks[1], (2, E), 0, N, dtype=jnp.int64)
        W1 = jax.random.normal(ks[2], (F_IN, HEADS * HID), dtype=jnp.float32) * s
        att_src1 = jax.random.normal(ks[3], (HEADS, HID), dtype=jnp.float32) * s
        att_dst1 = jax.random.normal(ks[4], (HEADS, HID), dtype=jnp.float32) * s
        b1 = jnp.zeros((HEADS * HID,), dtype=jnp.float32)
        W2 = jax.random.normal(ks[5], (HEADS * HID, HID), dtype=jnp.float32) * s
        att_src2 = jax.random.normal(ks[6], (1, HID), dtype=jnp.float32) * s
        att_dst2 = jax.random.normal(ks[7], (1, HID), dtype=jnp.float32) * s
        b2 = jnp.zeros((HID,), dtype=jnp.float32)
        Wf = jax.random.normal(ks[8], (HID, F_IN), dtype=jnp.float32) * s
        bf = jnp.zeros((F_IN,), dtype=jnp.float32)
        return {'x': x, 'edge_index': edge_index, 'W1': W1, 'att_src1': att_src1, 'att_dst1': att_dst1, 'b1': b1, 'W2': W2, 'att_src2': att_src2, 'att_dst2': att_dst2, 'b2': b2, 'Wf': Wf, 'bf': bf}
    _L1_gnn_all = _L1_gnn_setup()
    _L1_gnn_in = {k: v for k, v in _L1_gnn_all.items() if k in ('W1', 'att_src1', 'att_dst1', 'b1', 'W2', 'att_src2', 'att_dst2', 'b2', 'Wf', 'bf')}
    del _L1_gnn_all

    def _L2_gnn_setup():
        import jax, jax.numpy as jnp
        import numpy as np
        N_NODES = 6250
        N_EDGES = 200000
        D_IN = 256
        D_OUT = 256
        key = jax.random.key(seed)
        k1, k2, k3, k4, k5 = jax.random.split(key, 5)
        x = jax.random.normal(k1, (N_NODES, D_IN), dtype=jnp.float32)
        limit = float(np.sqrt(6.0 / (D_IN + D_OUT)))
        weight = jax.random.uniform(k2, (D_IN, D_OUT), minval=-limit, maxval=limit, dtype=jnp.float32)
        bias = jnp.zeros((D_OUT,), dtype=jnp.float32)
        edge_src = jax.random.randint(k3, (N_EDGES,), 0, N_NODES, dtype=jnp.int32)
        edge_dst = jax.random.randint(k4, (N_EDGES,), 0, N_NODES, dtype=jnp.int32)
        edge_val = jax.random.uniform(k5, (N_EDGES,), dtype=jnp.float32)
        return {'x': x, 'weight': weight, 'bias': bias, 'edge_src': edge_src, 'edge_dst': edge_dst, 'edge_val': edge_val}
    _L2_gnn_all = _L2_gnn_setup()
    _L2_gnn_in = {k: v for k, v in _L2_gnn_all.items() if k in ('weight', 'bias')}
    del _L2_gnn_all

    def _L3_gnn_setup():
        import jax, jax.numpy as jnp
        import numpy as np
        N_NODES = 3125
        N_EDGES = 50000
        D_IN = 256
        D_HID = 256
        D_OUT = 256

        def _gcn_layer(x, src, dst, ew, W, b, n):
            deg = jax.ops.segment_sum(ew, dst, num_segments=n) + 1.0
            dinv = jax.lax.rsqrt(deg)
            norm = dinv[src] * ew * dinv[dst]
            h = x @ W + b
            agg = jax.ops.segment_sum(h[src] * norm[:, None], dst, num_segments=n)
            return agg + h * (1.0 / deg)[:, None]
        key = jax.random.key(seed)
        ks = jax.random.split(key, 14)
        s = 1.0 / np.sqrt(D_IN)
        inp = {'x': jax.random.normal(ks[0], (N_NODES, D_IN), dtype=jnp.float32), 'edge_index': jax.random.randint(ks[1], (2, N_EDGES), 0, N_NODES, dtype=jnp.int64), 'edge_attr': jax.random.uniform(ks[2], (N_EDGES, 1), dtype=jnp.float32), 'W1': jax.random.normal(ks[3], (D_IN, D_HID), dtype=jnp.float32) * s, 'b1': jnp.zeros((D_HID,), dtype=jnp.float32), 'W2': jax.random.normal(ks[4], (D_HID, D_HID), dtype=jnp.float32) * s, 'b2': jnp.zeros((D_HID,), dtype=jnp.float32), 'W3': jax.random.normal(ks[5], (D_HID, D_OUT), dtype=jnp.float32) * s, 'b3': jnp.zeros((D_OUT,), dtype=jnp.float32), 'mw1': jax.random.normal(ks[6], (1, 8), dtype=jnp.float32), 'mb1': jnp.zeros((8,), dtype=jnp.float32), 'mw2': jax.random.normal(ks[7], (8, 1), dtype=jnp.float32) * (1.0 / np.sqrt(8.0)), 'mb2': jnp.zeros((1,), dtype=jnp.float32)}
        return inp
    _L3_gnn_all = _L3_gnn_setup()
    _L3_gnn_in = {k: v for k, v in _L3_gnn_all.items() if k in ('W1', 'b1', 'W2', 'b2', 'W3', 'b3', 'mw1', 'mb1', 'mw2', 'mb2')}
    del _L3_gnn_all
    return {'x': x, 'src': src, 'dst': dst, 'edge_weight': edge_weight, 'edge_weight1': edge_weight1, 'L0_gnn_W': _L0_gnn_in['W'], 'L0_gnn_b': _L0_gnn_in['b'], 'L1_gnn_W1': _L1_gnn_in['W1'], 'L1_gnn_att_src1': _L1_gnn_in['att_src1'], 'L1_gnn_att_dst1': _L1_gnn_in['att_dst1'], 'L1_gnn_b1': _L1_gnn_in['b1'], 'L1_gnn_W2': _L1_gnn_in['W2'], 'L1_gnn_att_src2': _L1_gnn_in['att_src2'], 'L1_gnn_att_dst2': _L1_gnn_in['att_dst2'], 'L1_gnn_b2': _L1_gnn_in['b2'], 'L1_gnn_Wf': _L1_gnn_in['Wf'], 'L1_gnn_bf': _L1_gnn_in['bf'], 'L2_gnn_weight': _L2_gnn_in['weight'], 'L2_gnn_bias': _L2_gnn_in['bias'], 'L3_gnn_W1': _L3_gnn_in['W1'], 'L3_gnn_b1': _L3_gnn_in['b1'], 'L3_gnn_W2': _L3_gnn_in['W2'], 'L3_gnn_b2': _L3_gnn_in['b2'], 'L3_gnn_W3': _L3_gnn_in['W3'], 'L3_gnn_b3': _L3_gnn_in['b3'], 'L3_gnn_mw1': _L3_gnn_in['mw1'], 'L3_gnn_mb1': _L3_gnn_in['mb1'], 'L3_gnn_mw2': _L3_gnn_in['mw2'], 'L3_gnn_mb2': _L3_gnn_in['mb2']}

def reference(x, src, dst, edge_weight, edge_weight1, L0_gnn_W, L0_gnn_b, L1_gnn_W1, L1_gnn_att_src1, L1_gnn_att_dst1, L1_gnn_b1, L1_gnn_W2, L1_gnn_att_src2, L1_gnn_att_dst2, L1_gnn_b2, L1_gnn_Wf, L1_gnn_bf, L2_gnn_weight, L2_gnn_bias, L3_gnn_W1, L3_gnn_b1, L3_gnn_W2, L3_gnn_b2, L3_gnn_W3, L3_gnn_b3, L3_gnn_mw1, L3_gnn_mb1, L3_gnn_mw2, L3_gnn_mb2):
    import jax
    import jax.numpy as jnp

    def _L0_gnn_ref(x, edge_row, edge_col, edge_val, W, b):
        import jax, jax.numpy as jnp
        import numpy as np
        N = 6250
        E = 200000
        F_IN = 256
        F_OUT = 256
        gathered = edge_val[:, None] * x[edge_col]
        support = jax.ops.segment_sum(gathered, edge_row, num_segments=N)
        h = jnp.concatenate([x, support], axis=1)
        out = h @ W + b
        return jax.nn.relu(out)

    def _L1_gnn_ref(x, edge_index, W1, att_src1, att_dst1, b1, W2, att_src2, att_dst2, b2, Wf, bf):
        import jax, jax.numpy as jnp
        import numpy as np
        N = 3125
        E = 50000
        F_IN = 256
        HID = 64
        HEADS = 4

        def _segment_softmax(logits, seg, num_segments):
            m = jax.ops.segment_max(logits, seg, num_segments=num_segments)
            e = jnp.exp(logits - m[seg])
            z = jax.ops.segment_sum(e, seg, num_segments=num_segments)
            return e / z[seg]

        def _gat_layer(x, src, dst, W, a_src, a_dst, b, num_nodes):
            H, C = a_src.shape
            h = (x @ W).reshape(num_nodes, H, C)
            al_s = jnp.einsum('nhc,hc->nh', h, a_src)
            al_d = jnp.einsum('nhc,hc->nh', h, a_dst)
            logits = jax.nn.leaky_relu(al_s[src] + al_d[dst], 0.2)
            alpha = _segment_softmax(logits, dst, num_nodes)
            msg = h[src] * alpha[:, :, None]
            out = jax.ops.segment_sum(msg, dst, num_segments=num_nodes)
            return out.reshape(num_nodes, H * C) + b
        num_nodes = x.shape[0]
        loop = jnp.arange(num_nodes, dtype=edge_index.dtype)
        src = jnp.concatenate([edge_index[0], loop])
        dst = jnp.concatenate([edge_index[1], loop])
        h = jax.nn.relu(_gat_layer(x, src, dst, W1, att_src1, att_dst1, b1, num_nodes))
        h = _gat_layer(h, src, dst, W2, att_src2, att_dst2, b2, num_nodes)
        return h @ Wf + bf

    def _L2_gnn_ref(x, weight, bias, edge_src, edge_dst, edge_val):
        import jax, jax.numpy as jnp
        import numpy as np
        N_NODES = 6250
        N_EDGES = 200000
        D_IN = 256
        D_OUT = 256
        h = jnp.matmul(x, weight) + bias
        msgs = edge_val[:, None] * h[edge_src]
        out = jax.ops.segment_sum(msgs, edge_dst, num_segments=N_NODES)
        return out

    def _L3_gnn_ref(x, edge_index, edge_attr, W1, b1, W2, b2, W3, b3, mw1, mb1, mw2, mb2):
        import jax, jax.numpy as jnp
        import numpy as np
        N_NODES = 3125
        N_EDGES = 50000
        D_IN = 256
        D_HID = 256
        D_OUT = 256

        def _gcn_layer(x, src, dst, ew, W, b, n):
            deg = jax.ops.segment_sum(ew, dst, num_segments=n) + 1.0
            dinv = jax.lax.rsqrt(deg)
            norm = dinv[src] * ew * dinv[dst]
            h = x @ W + b
            agg = jax.ops.segment_sum(h[src] * norm[:, None], dst, num_segments=n)
            return agg + h * (1.0 / deg)[:, None]
        src, dst = (edge_index[0], edge_index[1])
        h = jax.nn.relu(edge_attr @ mw1 + mb1)
        ew = jax.nn.sigmoid(h @ mw2 + mb2)[:, 0]
        n = x.shape[0]
        x = jax.nn.relu(_gcn_layer(x, src, dst, ew, W1, b1, n))
        x = jax.nn.relu(_gcn_layer(x, src, dst, ew, W2, b2, n))
        x = _gcn_layer(x, src, dst, ew, W3, b3, n)
        return x
    edge_index = jnp.stack([src, dst])
    x = _layernorm(x + _L0_gnn_ref(x, src, dst, edge_weight, L0_gnn_W, L0_gnn_b), axis=-1)
    x = _layernorm(x + _L1_gnn_ref(x, edge_index, L1_gnn_W1, L1_gnn_att_src1, L1_gnn_att_dst1, L1_gnn_b1, L1_gnn_W2, L1_gnn_att_src2, L1_gnn_att_dst2, L1_gnn_b2, L1_gnn_Wf, L1_gnn_bf), axis=-1)
    x = _layernorm(x + _L2_gnn_ref(x, L2_gnn_weight, L2_gnn_bias, src, dst, edge_weight), axis=-1)
    x = _layernorm(x + _L3_gnn_ref(x, edge_index, edge_weight1, L3_gnn_W1, L3_gnn_b1, L3_gnn_W2, L3_gnn_b2, L3_gnn_W3, L3_gnn_b3, L3_gnn_mw1, L3_gnn_mb1, L3_gnn_mw2, L3_gnn_mb2), axis=-1)
    return x

_drawn_inputs = setup_inputs


def setup_inputs(seed=0):
    import zlib

    import numpy as np

    out = dict(_drawn_inputs(seed))
    spreads = {'L0_gnn_b': (0.0, 0.1),
     'L1_gnn_b1': (0.0, 0.1),
     'L1_gnn_b2': (0.0, 0.1),
     'L1_gnn_bf': (0.0, 0.1),
     'L2_gnn_bias': (0.0, 0.1),
     'L3_gnn_b1': (0.0, 0.1),
     'L3_gnn_b2': (0.0, 0.1),
     'L3_gnn_b3': (0.0, 0.1),
     'L3_gnn_mb1': (0.0, 0.8)}
    factors = {'edge_weight1': 6.432,
     'L1_gnn_W1': 2.894,
     'L1_gnn_att_src1': 6.024,
     'L1_gnn_att_dst1': 8.0,
     'L1_gnn_att_src2': 8.0,
     'L1_gnn_att_dst2': 8.0,
     'L3_gnn_mw1': 8.0,
     'L3_gnn_mw2': 8.0}
    for name, (base, spread) in spreads.items():
        noise = np.random.default_rng([zlib.crc32(name.encode()), seed]).standard_normal(out[name].shape)
        drawn = base * np.exp(spread * noise) if base else spread * noise
        out[name] = jnp.asarray(drawn.astype(out[name].dtype))
    for name, factor in factors.items():
        out[name] = (out[name] * factor).astype(out[name].dtype)
    return out
```

```python
import math
from collections import namedtuple
from contextlib import ExitStack, contextmanager

import numpy as np
import concourse.bass as bass
from concourse import mybir

P = 128
RING = 16
HALF = RING // 2
BUFS = 4
COPIES = 4
BIG = 1e30

FP32 = mybir.dt.float32
INT32 = mybir.dt.int32
ALU = mybir.AluOpType
ACT = mybir.ActivationFunctionType
AXX = mybir.AxisListType.X
ENGINES = mybir.ALL_ENGINES


def sizes(nodes, edges):
    tiles = math.ceil(edges / P / RING) * RING
    blocks = 2 * math.ceil((nodes + P) / P / 2)
    return tiles, blocks


class Graph:
    pass


@contextmanager
def phase(nc, *names):
    sems = {n: nc.alloc_semaphore(name=f"{n}_{nc.next_id()}") for n in names}
    with nc.Block() as block:
        yield block, namedtuple("Semaphores", list(sems))(**sems)
    nc.clear_and_free_semaphores(list(sems.values()))
    nc.all_engine_barrier(sem_only=True)


def tiles_of(stack, nc):
    def sbuf(name, shape, dtype=FP32):
        return stack.enter_context(nc.sbuf_tensor(f"{name}_{nc.next_id()}", shape, dtype))

    def psum(name, shape=(P, 512), dtype=FP32):
        return stack.enter_context(nc.psum_tensor(f"{name}_{nc.next_id()}", list(shape), dtype))

    return sbuf, psum


def aggregate(nc, g, table, features, weights, heads, first_pass):
    chunks = math.ceil(features / P)
    width = features // chunks
    share = features // heads
    with ExitStack() as stack:
        sbuf, psum = tiles_of(stack, nc)
        rows = sbuf("rows", [P, RING, features])
        scaled_rows = sbuf("scaled_rows", [P, BUFS, features])
        onehots = sbuf("onehots", [P, BUFS, P])
        index = sbuf("index", [P, RING], INT32)
        sums = [psum(f"sums{n}") for n in range(BUFS)]
        gathered_names = [f"gathered{k}" for k in range(RING)]
        with phase(nc, "index_ready", "issued", "scaled", "onehot_ready", "summed", "added",
                   *gathered_names) as (block, s):
            gathered = s[-RING:]

            @block.gpsimd
            def _(pool):
                with pool.Fori(0, g.tiles // RING) as i:
                    for k in range(RING):
                        if k % HALF == 0:
                            pool.wait_ge(s.index_ready, i * 2 + (k // HALF + 1))
                        pool.wait_ge(s.scaled, i * RING + (k + 1))
                        pool.sem_inc(s.issued, 1)
                        nc.gpsimd.indirect_dma_start(
                            rows[:, k, :], None, table,
                            bass.IndirectOffsetOnAxis(ap=index[:, k:k + 1], axis=0),
                        ).then_inc(gathered[k], 16)

            @block.scalar
            def _(act):
                act.sem_inc(s.scaled, RING)
                for half in range(2):
                    nc.scalar.copy(index[:, half * HALF:(half + 1) * HALF],
                                   g.source[:, half * HALF:(half + 1) * HALF]
                                   ).then_inc(s.index_ready, 1)
                with act.Fori(0, g.tiles // RING) as i:
                    for k in range(RING):
                        act.wait_ge(gathered[k], i * 16 + 16)
                        act.wait_ge(s.summed, i * RING + (k + 1))
                        for h in range(heads):
                            part = slice(h * share, (h + 1) * share)
                            last = nc.scalar.activation(
                                scaled_rows[:, k % BUFS, part], rows[:, k, part], ACT.Copy,
                                scale=weights[:, h, bass.ds(i * RING + k, 1)])
                        last.then_inc(s.scaled, 1)
                        if k % HALF == HALF - 1:
                            half = k // HALF * HALF
                            nc.scalar.copy(index[:, half:half + HALF],
                                           g.source[:, bass.ds(i * RING + (RING + half), HALF)]
                                           ).then_inc(s.index_ready, 1)

            @block.tensor
            def _(pe):
                pe.sem_inc(s.summed, BUFS)
                with pe.Fori(0, g.tiles // RING) as i:
                    for k in range(RING):
                        pe.wait_ge(s.scaled, i * RING + (RING + k + 1))
                        pe.wait_ge(s.onehot_ready, i * RING + (k + 1))
                        pe.wait_ge(s.added, i * RING + (k + 1))
                        b = k % BUFS
                        for c in range(chunks):
                            last = nc.tensor.matmul(
                                sums[b][0:width, c * P:(c + 1) * P],
                                scaled_rows[:, b, c * width:(c + 1) * width], onehots[:, b, :],
                                start=True, stop=True)
                        last.then_inc(s.summed, 1)

            @block.vector
            def _(dve):
                def onehot(slot, column):
                    nc.vector.tensor_scalar(onehots[:, slot, :], g.iota[:], column, None,
                                            ALU.is_equal).then_inc(s.onehot_ready, 1)

                if first_pass:
                    nc.vector.memset(g.acc[0:width, 0:chunks, :], 0.0).then_inc(s.added, BUFS)
                else:
                    dve.sem_inc(s.added, BUFS)
                for k in range(2):
                    onehot(k, g.offset[:, k:k + 1])
                with dve.Fori(0, g.tiles // RING) as i:
                    for k in range(RING):
                        if k % HALF == 0:
                            _, bases = nc.values_load_multi_w_load_instructions(
                                g.base[0:1, bass.ds(i * RING + k, HALF)],
                                engines=[mybir.EngineType.DVE], min_val=0,
                                max_val=(g.blocks - 1) * P,
                                skip_runtime_bounds_check_because="a destination, or clamped")
                            bases = list(bases)
                        onehot((k + 2) % BUFS, g.offset[:, bass.ds(i * RING + (k + 2), 1)])
                        window = bass.ds(bases[k % HALF], P)
                        dve.wait_ge(s.summed, i * RING + (BUFS + k + 1))
                        dve.wait_ge(s.added, i * RING + (BUFS + k))
                        nc.vector.tensor_tensor(
                            g.acc[0:width, 0:chunks, window], g.acc[0:width, 0:chunks, window],
                            sums[k % BUFS][0:width, 0:chunks * P].rearrange("p (c n) -> p c n", c=chunks),
                            ALU.add).then_inc(s.added, 1)


def scatter_by_source(nc, g, support, spare, histogram, first_pass):
    with ExitStack() as stack:
        sbuf, psum = tiles_of(stack, nc)
        zeros = sbuf("zeros", [P, (g.blocks + 1) * P // 2])
        x_window = sbuf("x_window", [P, 2, g.features])
        source_row = sbuf("source_row", [P, 2, HALF, P], INT32)
        values = sbuf("values", [P, 2, HALF, 3])
        onehots = sbuf("onehots", [P, BUFS, P])
        same_source = sbuf("same_source", [P, BUFS, P])
        scrap = sbuf("scrap", [P, HALF, P])
        repeats = sbuf("repeats", [P, 2, HALF])
        moved = sbuf("moved", [P, 2, HALF])
        index = sbuf("index", [P, 2, HALF], INT32)
        cross = sbuf("cross", [P, BUFS, P])
        rows = sbuf("rows", [P, HALF, g.features])
        cross_bank = [psum(f"cross_bank{n}") for n in range(2)]
        rows_bank = [psum(f"rows_bank{n}") for n in range(2)]
        counts_bank = [psum(f"counts_bank{n}") for n in range(2)]
        names = [f"scattered{k}" for k in range(HALF)]
        with phase(nc, "zeroed", "x_loaded0", "x_loaded1", "row_loaded0", "row_loaded1", "own", "index_ready",
                   "issued", "matrices", "crossed", "cross_copied", "multiplied", "rows_ready", "counted",
                   "values_ready", *names) as (block, s):
            scattered = s[-HALF:]
            x_loaded, row_loaded = [s.x_loaded0, s.x_loaded1], [s.row_loaded0, s.row_loaded1]

            @block.gpsimd
            def _(pool):
                pool.wait_ge(s.zeroed, 1)
                for slot in range(HALF):
                    for part in range(2):
                        if first_pass:
                            flat = support[slot % COPIES].rearrange("n f -> (n f)")
                            size = flat.shape[0] // 4
                            quarter = 2 * (slot // COPIES) + part
                            target = flat[quarter * size:(quarter + 1) * size].rearrange("(p z) -> p z", p=P)
                            pool.dma_start(target, zeros[:]).then_inc(scattered[slot], 16)
                        else:
                            pool.dma_start(spare[slot, part], zeros[:, 0:P]).then_inc(scattered[slot], 16)
                for slot in range(HALF):
                    pool.wait_ge(scattered[slot], 32)
                with pool.Fori(0, g.tiles // RING) as i:
                    for k in range(RING):
                        if k % HALF == 0:
                            pool.wait_ge(s.index_ready, i * 2 + (k // HALF + 1))
                        pool.wait_ge(s.rows_ready, i * RING + (k + 3))
                        before = (k - COPIES) % HALF
                        uses = (k - COPIES) // HALF + 1
                        pool.wait_ge(scattered[before], i * 32 + 16 * (uses + 2))
                        pool.sem_inc(s.issued, 1)
                        nc.gpsimd.indirect_dma_start(
                            support[k % COPIES],
                            bass.IndirectOffsetOnAxis(ap=index[:, k // HALF, k % HALF:k % HALF + 1], axis=0),
                            rows[:, k % HALF, :], None, compute_op=ALU.add,
                        ).then_inc(scattered[k % HALF], 16)
                for slot in range(HALF):
                    pool.wait_ge(scattered[slot], 16 * (g.tiles // HALF + 2))

            @block.sync
            def _(sync):
                with sync.Fori(0, g.tiles // RING) as i:
                    for h in range(2):
                        base = sync.value_load(g.half_base[0:1, bass.ds(i * 2 + h, 1)], min_val=0,
                                               max_val=(g.blocks - 1) * P)
                        sync.wait_ge(s.multiplied, i * RING + HALF * (h + 1))
                        sync.dma_start(x_window[:, h, :], g.x_dram[bass.ds(base, P), :]).then_inc(x_loaded[h], 16)
                        sync.wait_ge(s.matrices, i * RING + HALF * (h + 1))
                        sync.dma_start(
                            source_row[:, h, :, :].rearrange("p k e -> p (k e)"),
                            g.source_flat[0:1, bass.ds((i * 2 + h) * (HALF * P), HALF * P)]
                            .to_broadcast([P, HALF * P])).then_inc(row_loaded[h], 16)

            @block.scalar
            def _(act):
                act.sem_inc(s.cross_copied, 2)
                act.sem_inc(s.rows_ready, 2)

                def copy_rows(i, k):
                    act.wait_ge(s.multiplied, i * RING + (RING + k + 1))
                    act.wait_ge(scattered[k % HALF], i * 32 + 16 * (k // HALF + 2))
                    nc.scalar.copy(rows[:, k % HALF, :], rows_bank[k % 2][:, 0:g.features]).then_inc(s.rows_ready, 1)

                with act.Fori(0, g.tiles // RING) as i:
                    for k in range(RING):
                        if k % HALF == 0:
                            nc.scalar.copy(values[:, k // HALF, :, :],
                                           g.edge_values[:, bass.ds(i * RING + k, HALF), :]
                                           ).then_inc(s.values_ready, 1)
                        act.wait_ge(s.crossed, i * RING + (BUFS + k + 1))
                        nc.scalar.copy(cross[:, k % BUFS, :], cross_bank[k % 2][:, 0:P]).then_inc(s.cross_copied, 1)
                        if k > 0:
                            copy_rows(i, k - 1)
                    copy_rows(i, RING - 1)

            @block.tensor
            def _(pe):
                pe.sem_inc(s.crossed, BUFS)
                pe.sem_inc(s.multiplied, RING)

                def multiply(i, k):
                    if k % HALF == 0:
                        pe.wait_ge(x_loaded[k // HALF], i * 16 + 16)
                    pe.wait_ge(s.cross_copied, i * RING + (k + 3))
                    pe.wait_ge(s.rows_ready, i * RING + (k + 1))
                    nc.tensor.matmul(rows_bank[k % 2][:, 0:g.features], cross[:, k % BUFS, :],
                                     x_window[:, k // HALF, :], start=True, stop=True).then_inc(s.multiplied, 1)

                with pe.Fori(0, g.tiles // RING) as i:
                    for k in range(RING):
                        b = k % BUFS
                        pe.wait_ge(s.matrices, i * RING + (RING + k + 1))
                        pe.wait_ge(s.cross_copied, i * RING + (k + 1))
                        nc.tensor.matmul(cross_bank[k % 2][:, 0:P], onehots[:, b, :], same_source[:, b, :],
                                         start=True, stop=True)
                        if k % HALF == 0:
                            pe.wait_ge(s.values_ready, i * 2 + (k // HALF + 1))
                            pe.wait_ge(s.counted, i * 2 + (k // HALF + 1))
                        nc.tensor.matmul(counts_bank[k // HALF][0:3, 0:P], values[:, k // HALF, k % HALF, :],
                                         onehots[:, b, :], start=(k % HALF == 0), stop=(k % HALF == HALF - 1)
                                         ).then_inc(s.crossed, 1)
                        if k > 0:
                            multiply(i, k - 1)
                    multiply(i, RING - 1)

            @block.vector
            def _(dve):
                nc.vector.memset(zeros[:], 0.0).then_inc(s.zeroed, 1)
                if first_pass:
                    nc.vector.memset(histogram[:], 0.0).then_inc(s.counted, 2)
                else:
                    dve.sem_inc(s.counted, 2)
                dve.sem_inc(s.matrices, RING)
                for slot in range(HALF):
                    dve.wait_ge(scattered[slot], 32)
                with dve.Fori(0, g.tiles // RING) as i:
                    for h in range(2):
                        base = dve.value_load(g.half_base[0:1, bass.ds(i * 2 + h, 1)], min_val=0,
                                              max_val=(g.blocks - 1) * P)
                        dve.wait_ge(row_loaded[h], i * 16 + 16)
                        for k in range(HALF):
                            last = nc.vector.scalar_tensor_tensor(
                                scrap[:, k, :], source_row[:, h, k, :],
                                g.source_float[:, bass.ds(i * RING + (h * HALF + k), 1)], g.earlier[:],
                                ALU.is_equal, ALU.mult, accum_out=repeats[:, h, k:k + 1])
                        last.then_inc(s.own, 1)
                        dve.wait_ge(s.own, i * 4 + (2 * h + 1))
                        here = bass.ds(i * RING + h * HALF, HALF)
                        nc.vector.scalar_tensor_tensor(moved[:, h, :], repeats[:, h, :], 0.5, g.to_spare[:, here],
                                                       ALU.is_gt, ALU.mult).then_inc(s.own, 1)
                        dve.wait_ge(s.own, i * 4 + (2 * h + 2))
                        for slot in range(HALF):
                            dve.wait_ge(scattered[slot], i * 32 + 16 * (h + 1))
                        nc.vector.tensor_tensor(index[:, h, :], moved[:, h, :], g.source_float[:, here],
                                                ALU.add).then_inc(s.index_ready, 1)
                        for k in range(HALF):
                            b, tile = k % BUFS, bass.ds(i * RING + (h * HALF + k), 1)
                            dve.wait_ge(s.crossed, i * RING + (h * HALF + k + 1))
                            nc.vector.tensor_scalar(onehots[:, b, :], g.iota[:], g.half_offset[:, tile], None,
                                                    ALU.is_equal)
                            nc.vector.tensor_scalar(same_source[:, b, :], source_row[:, h, k, :],
                                                    g.source_float[:, tile],
                                                    g.edge_values[:, tile, 0:1].rearrange("p a v -> p (a v)"),
                                                    ALU.is_equal, ALU.mult).then_inc(s.matrices, 1)
                        window = bass.ds(base, P)
                        dve.wait_ge(s.crossed, i * RING + (BUFS + HALF * (h + 1)))
                        dve.wait_ge(s.counted, i * 2 + (h + 2))
                        nc.vector.tensor_tensor(histogram[:, window], histogram[:, window],
                                                counts_bank[h][0:3, 0:P], ALU.add).then_inc(s.counted, 1)


def windows(nc, g, one_pass, tables):
    one_pass(True)
    offset, base_float, base, offset_dram, base_float_dram, last_window = tables
    wide = nc.values_load(last_window[0:1, 0:1], engines=ENGINES, min_val=0, max_val=g.blocks - 1,
                          skip_runtime_bounds_check_because="destinations are below blocks * 128")
    with nc.If(wide > 0):
        with nc.Fori(1, wide + 1):
            with phase(nc, "moved") as (block, s):
                @block.vector
                def _(dve):
                    nc.vector.tensor_scalar(offset[:], offset[:], float(P), None, ALU.subtract)
                    nc.vector.tensor_scalar(base_float[:], base_float[:], float(P),
                                            float((g.blocks - 1) * P), ALU.add, ALU.min).then_inc(s.moved, 1)
                    dve.wait_ge(s.moved, 1)
                    nc.vector.tensor_copy(base[:], base_float[:])
            one_pass(False)
        load(nc, (offset[:], offset_dram[:]), (base_float[:], base_float_dram[:]))
        with phase(nc) as (block, s):
            @block.vector
            def _(dve):
                nc.vector.tensor_copy(base[:], base_float[:])


def aggregate_windows(nc, g, table, features, weights, heads):
    windows(nc, g, lambda first: aggregate(nc, g, table, features, weights, heads, first),
            (g.offset, g.base_float, g.base, g.offset_dram, g.base_float_dram, g.last_window))


def linker(engine, sem):
    count = [0]

    def link(instruction):
        count[0] += 1
        instruction.then_inc(sem, 1)
        engine.wait_ge(sem, count[0])

    link.count = count
    return link


def inverse_root(nc, link, value, root, scratch):
    link(nc.vector.reciprocal(root[:], root[:]))
    link(nc.vector.tensor_tensor(scratch[:], root[:], root[:], ALU.mult))
    link(nc.vector.tensor_tensor(scratch[:], scratch[:], value[:], ALU.mult))
    link(nc.vector.tensor_scalar(scratch[:], scratch[:], -0.5, 1.5, ALU.mult, ALU.add))
    link(nc.vector.tensor_tensor(root[:], root[:], scratch[:], ALU.mult))


def set_up(nc, g, t):
    with ExitStack() as stack:
        sbuf, psum = tiles_of(stack, nc)
        iota_int = sbuf("iota_int", [P, P], INT32)
        lane_int = sbuf("lane_int", [P, 1], INT32)
        lane = sbuf("lane", [P, 1])
        dst_int = sbuf("dst_int", [P, g.tiles], INT32)
        base_int = sbuf("base_int", [P, g.tiles], INT32)
        base_all = sbuf("base_all", [P, g.tiles])
        chunk_dst = sbuf("chunk_dst", [P, g.tiles], INT32)
        chunk_before = sbuf("chunk_before", [P, g.tiles], INT32)
        attribute = sbuf("attribute", [P, g.tiles])
        weight = sbuf("weight", [P, g.tiles])
        hidden = sbuf("hidden", [P, 2, g.tiles])
        gate = sbuf("gate", [P, g.tiles])
        mlp = sbuf("mlp", [P, 25])
        widest = sbuf("widest", [1, 2])
        small = sbuf("small", [P, 5])
        turned = psum("turned")
        groups = g.tiles // HALF
        hid = t.L3_gnn_mw2.shape[0]
        with phase(nc, "loaded", "x_loaded", "iota", "own", "relu", "added", "gated", "kept",
                   "turned", "wide", "stored") as (block, s):
            @block.sync
            def _(sync):
                for out, dram in ((g.source[:, 0:g.tiles], t.src_tile),
                                  (g.source_chunk[:, 0:g.tiles], t.src_chunk),
                                  (dst_int[:], t.dst_tile),
                                  (base_int[:], t.dst_tile[0:1, :].to_broadcast([P, g.tiles])),
                                  (g.base[:], t.dst_tile[0:1, :]), (chunk_dst[:], t.dst_chunk),
                                  (chunk_before[:], t.before_chunk), (attribute[:], t.attr_tile),
                                  (weight[:], t.weight_tile)):
                    sync.dma_start(out, dram).then_inc(s.loaded, 16)
                for at, param in ((0, t.L3_gnn_mw1), (hid, t.L3_gnn_mb1), (2 * hid, t.L3_gnn_mw2),
                                  (3 * hid, t.L3_gnn_mb2)):
                    n = hid if at < 3 * hid else 1
                    sync.dma_start(mlp[:, at:at + n], param.rearrange("a b -> (a b)").unsqueeze(0).to_broadcast([P, n])
                                   if len(param.shape) == 2 else param.unsqueeze(0).to_broadcast([P, n])
                                   ).then_inc(s.loaded, 16)
                sync.dma_start(g.x[:], t.x.rearrange("(b p) f -> p b f", p=P)).then_inc(s.x_loaded, 16)
                sync.wait_ge(s.x_loaded, 16)
                sync.wait_ge(s.kept, 1)
                sync.dma_start(g.offset_dram[:], g.offset[:]).then_inc(s.stored, 16)
                sync.dma_start(g.base_float_dram[:], g.base_float[:]).then_inc(s.stored, 16)
                sync.dma_start(g.half_offset_dram[:], g.half_offset[:]).then_inc(s.stored, 16)
                sync.dma_start(g.half_base_float_dram[:], g.half_base_float[:]).then_inc(s.stored, 16)
                sync.wait_ge(s.stored, 64)

            @block.gpsimd
            def _(pool):
                nc.gpsimd.iota(iota_int[:], [[1, P]], base=0, channel_multiplier=0).then_inc(s.iota, 1)
                nc.gpsimd.iota(lane_int[:], [[0, 1]], base=0, channel_multiplier=1).then_inc(s.iota, 1)

            @block.scalar
            def _(act):
                act.wait_ge(s.loaded, 16 * 13)
                for k in range(hid):
                    if k >= 2:
                        act.wait_ge(s.added, k - 1)
                    nc.scalar.activation(hidden[:, k % 2, :], attribute[:], ACT.Relu,
                                         bias=mlp[:, hid + k:hid + k + 1],
                                         scale=mlp[:, k:k + 1]).then_inc(s.relu, 1)
                act.wait_ge(s.added, hid)
                nc.scalar.activation(g.edge_values[:, :, 1], gate[:], ACT.Sigmoid,
                                     bias=mlp[:, 3 * hid:3 * hid + 1]).then_inc(s.gated, 1)
                act.wait_ge(s.gated, 1)

            @block.tensor
            def _(pe):
                pe.wait_ge(s.kept, 1)
                nc.tensor.matmul(turned[0:1, 0:P], small[:, 0:1], g.identity[:], start=True, stop=True)
                nc.tensor.matmul(turned[0:1, 3 * P:4 * P], small[:, 4:5], g.identity[:], start=True, stop=True)
                nc.tensor.matmul(turned[0:8, P:2 * P], small[:, 1:2].to_broadcast([P, 8]), g.identity[:],
                                 start=True, stop=True)
                nc.tensor.matmul(turned[0:8, 2 * P:3 * P], small[:, 2:3].to_broadcast([P, 8]), g.identity[:],
                                 start=True, stop=True).then_inc(s.turned, 1)

            @block.vector
            def _(dve):
                link = linker(dve, s.own)
                nc.vector.memset(g.source[:, g.tiles:], 0)
                nc.vector.memset(g.source_chunk[:, g.tiles:], 0)
                nc.vector.memset(g.offset[:, g.tiles:], -1.0)
                nc.vector.memset(g.edge_values[:, :, 2], 1.0)
                dve.wait_ge(s.iota, 2)
                nc.vector.tensor_copy(lane[:], lane_int[:])
                link(nc.vector.tensor_copy(g.iota[:], iota_int[:]))
                nc.vector.tensor_scalar(g.identity[:], g.iota[:], lane[:], None, ALU.is_equal)
                nc.vector.tensor_scalar(g.earlier[:], g.iota[:], lane[:], None, ALU.is_lt)
                link(nc.vector.tensor_scalar(small[:, 3:4], lane[:], float(g.blocks * P), None, ALU.add))
                dve.wait_ge(s.loaded, 16 * 13)
                nc.vector.tensor_copy(g.offset[:, 0:g.tiles], dst_int[:])
                nc.vector.tensor_copy(g.base_float[:], base_int[0:1, :])
                nc.vector.tensor_copy(g.half_base_float[:], base_int[0:1, ::HALF])
                nc.vector.tensor_copy(g.half_base[:], base_int[0:1, ::HALF])
                link(nc.vector.tensor_copy(g.source_float[:], g.source[:, 0:g.tiles]))
                nc.vector.tensor_scalar(g.to_spare[:], g.source_float[:], small[:, 3:4], -1.0,
                                        ALU.subtract, ALU.mult)
                link(nc.vector.tensor_copy(base_all[:], base_int[:]))
                link(nc.vector.tensor_tensor(
                    g.half_offset[:].rearrange("p (n k) -> p n k", k=HALF),
                    g.offset[:, 0:g.tiles].rearrange("p (n k) -> p n k", k=HALF),
                    base_all[:].rearrange("p (n k) -> p n k", k=HALF)[:, :, 0:1].to_broadcast([P, groups, HALF]),
                    ALU.subtract))
                link(nc.vector.tensor_tensor(g.offset[:, 0:g.tiles], g.offset[:, 0:g.tiles], base_all[:], ALU.subtract))
                nc.vector.tensor_copy(g.edge_values[:, :, 0], weight[:])
                link(nc.vector.tensor_tensor(g.keep[:], chunk_dst[:], chunk_before[:], ALU.is_equal))
                link(nc.vector.tensor_scalar(g.reset[:], g.keep[:], 1.0, BIG, ALU.subtract, ALU.mult))
                nc.vector.tensor_reduce(small[:, 0:1], g.offset[:, 0:g.tiles], AXX, ALU.max)
                nc.vector.tensor_reduce(small[:, 4:5], g.half_offset[:], AXX, ALU.max)
                nc.vector.tensor_reduce(small[:, 1:2], g.keep[:], AXX, ALU.min)
                nc.vector.tensor_reduce(small[:, 2:3], g.reset[:], AXX, ALU.min).then_inc(s.kept, 1)
                dve.wait_ge(s.turned, 1)
                nc.vector.tensor_copy(g.keep_row[:], turned[0:8, P:2 * P])
                nc.vector.tensor_copy(g.reset_row[:], turned[0:8, 2 * P:3 * P])
                nc.vector.tensor_reduce(widest[:, 0:1], turned[0:1, 0:P], AXX, ALU.max)
                link(nc.vector.tensor_reduce(widest[:, 1:2], turned[0:1, 3 * P:4 * P], AXX, ALU.max))
                link(nc.vector.tensor_scalar(widest[:], widest[:], 1.0 / P, 0.5 / P - 0.5, ALU.mult, ALU.add))
                nc.vector.tensor_copy(g.last_window[:], widest[:, 0:1])
                nc.vector.tensor_copy(g.half_last_window[:], widest[:, 1:2])
                for k in range(hid):
                    dve.wait_ge(s.relu, k + 1)
                    if k == 0:
                        nc.vector.tensor_scalar(gate[:], hidden[:, 0, :], mlp[:, 2 * hid:2 * hid + 1], None,
                                                ALU.mult).then_inc(s.added, 1)
                    else:
                        dve.wait_ge(s.added, k)
                        nc.vector.scalar_tensor_tensor(
                            gate[:], hidden[:, k % 2, :], mlp[:, 2 * hid + k:2 * hid + k + 1], gate[:],
                            ALU.mult, ALU.add).then_inc(s.added, 1)


def degrees(nc, g, histogram):
    with ExitStack() as stack:
        sbuf, psum = tiles_of(stack, nc)
        running = sbuf("running", [3, g.blocks * P])
        one = sbuf("one", [3, 1])
        counts = sbuf("counts", [P, g.blocks, 2])
        degree = sbuf("degree", [P, g.blocks])
        scratch = sbuf("scratch", [P, g.blocks])
        values = psum("values")[:, 0:3 * g.blocks].rearrange("p (b v) -> p b v", v=3)
        ends = psum("ends")[:, 0:3 * g.blocks].rearrange("p (b v) -> p b v", v=3)
        with phase(nc, "own", "counted", "turned", "rooted", "degree") as (block, s):
            @block.tensor
            def _(pe):
                pe.wait_ge(s.counted, 1)
                for b in range(g.blocks):
                    nc.tensor.matmul(values[:, b, :], histogram[:, b * P:(b + 1) * P],
                                     g.identity[0:3, 0:3], start=True, stop=True)
                    last = nc.tensor.matmul(ends[:, b, :], running[:, b * P:(b + 1) * P],
                                            g.identity[0:3, 0:3], start=True, stop=True)
                last.then_inc(s.turned, 1)

            @block.scalar
            def _(act):
                act.wait_ge(s.degree, 1)
                nc.scalar.activation(g.root_degree[:], degree[:], ACT.Sqrt).then_inc(s.rooted, 1)

            @block.vector
            def _(dve):
                link = linker(dve, s.own)
                link(nc.vector.memset(one[:], 1.0))
                nc.vector.tensor_tensor_scan(running[:], one[:].to_broadcast([3, g.blocks * P]), histogram[:],
                                             0.0, ALU.mult, ALU.add).then_inc(s.counted, 1)
                dve.wait_ge(s.turned, 1)
                nc.vector.tensor_copy(g.weight_sum[:], values[:, :, 0])
                nc.vector.tensor_scalar(degree[:], values[:, :, 1], 1.0, None, ALU.add).then_inc(s.degree, 1)
                nc.vector.tensor_copy(counts[:, :, 0], values[:, :, 2])
                link(nc.vector.tensor_copy(counts[:, :, 1], ends[:, :, 2]))
                link(nc.vector.tensor_scalar(g.nonempty[:], counts[:, :, 0], 0.5, None, ALU.is_gt))
                nc.vector.tensor_scalar(g.empty[:], counts[:, :, 0], 0.5, None, ALU.is_lt)
                link(nc.vector.tensor_tensor(counts[:, :, 0], counts[:, :, 1], counts[:, :, 0], ALU.subtract))
                link(nc.vector.tensor_scalar(counts[:, :, 1], counts[:, :, 1], 1.0, None, ALU.subtract))
                link(nc.vector.tensor_tensor(counts[:, :, 1], counts[:, :, 1], g.nonempty[:], ALU.mult))
                nc.vector.tensor_copy(g.last_edge[:], counts[:, :, 1])
                link(nc.vector.scalar_tensor_tensor(counts[:, :, 0], g.empty[:], float(2 * g.tiles * P),
                                                    counts[:, :, 0], ALU.mult, ALU.add))
                nc.vector.tensor_copy(g.first_edge[:], counts[:, :, 0])
                dve.wait_ge(s.rooted, 1)
                inverse_root(nc, link, degree, g.root_degree, scratch)


def segmented_scan(nc, g, values, out, columns, largest):
    start = -BIG if largest else 0.0
    first, op0, op1 = (g.reset, ALU.add, ALU.max) if largest else (g.keep, ALU.mult, ALU.add)
    row_first = g.reset_row if largest else g.keep_row
    with ExitStack() as stack:
        sbuf, psum = tiles_of(stack, nc)
        ends = sbuf("ends", [P, columns])
        row = sbuf("row", [columns, P + 1])
        carry = sbuf("carry", [P, columns])
        turned = psum("turned")
        with phase(nc, "own", "ended", "turned", "carried", "returned") as (block, s):
            @block.tensor
            def _(pe):
                pe.wait_ge(s.ended, 1)
                nc.tensor.matmul(turned[0:columns, 0:P], ends[:], g.identity[:], start=True,
                                 stop=True).then_inc(s.turned, 1)
                pe.wait_ge(s.carried, 1)
                nc.tensor.matmul(turned[:, P:P + columns], row[:, 0:P], g.identity[0:columns, 0:columns],
                                 start=True, stop=True).then_inc(s.returned, 1)

            @block.vector
            def _(dve):
                link = linker(dve, s.own)
                nc.vector.memset(row[:, 0:1], start)
                for c in range(columns):
                    last = nc.vector.tensor_tensor_scan(out[:, :, c], first[:], values[:, :, c], start, op0, op1)
                link(last)
                nc.vector.tensor_copy(ends[:], out[:, g.tiles - 1, :]).then_inc(s.ended, 1)
                dve.wait_ge(s.turned, 1)
                nc.vector.tensor_tensor_scan(row[:, 1:P + 1], row_first[0:columns, :], turned[0:columns, 0:P],
                                             start, op0, op1).then_inc(s.carried, 1)
                dve.wait_ge(s.returned, 1)
                link(nc.vector.tensor_copy(carry[:], turned[:, P:P + columns]))
                for c in range(columns):
                    nc.vector.tensor_tensor_scan(out[:, :, c], first[:], values[:, :, c], carry[:, c:c + 1], op0, op1)


def gather_logits(nc, g, table, heads, out):
    with ExitStack() as stack:
        sbuf, _ = tiles_of(stack, nc)
        rows = sbuf("rows", [P, RING, heads])
        index = sbuf("index", [P, RING], INT32)
        with phase(nc, "index_ready", "issued", "copied", "gathered0", "gathered1") as (block, s):
            gathered = [s.gathered0, s.gathered1]

            @block.gpsimd
            def _(pool):
                with pool.Fori(0, g.tiles // RING) as i:
                    for k in range(RING):
                        if k % HALF == 0:
                            pool.wait_ge(s.index_ready, i * 2 + (k // HALF + 1))
                            pool.sem_inc(s.issued, 1)
                        nc.gpsimd.indirect_dma_start(
                            rows[:, k, :], None, table,
                            bass.IndirectOffsetOnAxis(ap=index[:, k:k + 1], axis=0),
                        ).then_inc(gathered[k // HALF], 16)

            @block.vector
            def _(dve):
                for half in range(2):
                    nc.vector.tensor_copy(index[:, half * HALF:(half + 1) * HALF],
                                          g.source_chunk[:, half * HALF:(half + 1) * HALF]
                                          ).then_inc(s.index_ready, 1)
                with dve.Fori(0, g.tiles // RING) as i:
                    for half in range(2):
                        at = half * HALF
                        dve.wait_ge(gathered[half], i * (16 * HALF) + 16 * HALF)
                        nc.vector.tensor_copy(out[:, bass.ds(i * RING + at, HALF), :],
                                              rows[:, at:at + HALF, :])
                        nc.vector.tensor_copy(index[:, at:at + HALF],
                                              g.source_chunk[:, bass.ds(i * RING + (RING + at), HALF)]
                                              ).then_inc(s.index_ready, 1)


def store_edges(nc, g, pairs):
    with phase(nc, "stored") as (block, s):
        @block.sync
        def _(sync):
            for dram, tile in pairs:
                sync.dma_start(dram, tile, allow_slow_non_contiguous=True).then_inc(s.stored, 16)
            sync.wait_ge(s.stored, 16 * len(pairs))


def at_last_edges(nc, g, edges, out, heads):
    with phase(nc, "gathered") as (block, s):
        @block.gpsimd
        def _(pool):
            for b in range(g.blocks):
                nc.gpsimd.indirect_dma_start(
                    out[:, b, :], None, edges,
                    bass.IndirectOffsetOnAxis(ap=g.last_edge[:, b:b + 1], axis=0)).then_inc(s.gathered, 16)
            pool.wait_ge(s.gathered, 16 * g.blocks)


def to_edges(nc, g, values, columns, scratch, spread, out):
    with phase(nc, "scattered", "loaded") as (block, s):
        @block.gpsimd
        def _(pool):
            for b in range(g.blocks):
                nc.gpsimd.indirect_dma_start(
                    scratch, bass.IndirectOffsetOnAxis(ap=g.first_edge[:, b:b + 1], axis=0),
                    values[:, b, :], None, bounds_check=g.tiles * P - 1, oob_is_err=False,
                ).then_inc(s.scattered, 16)
            pool.wait_ge(s.scattered, 16 * g.blocks)
            pool.dma_start(spread[:], scratch.rearrange("(p i) v -> p i v", p=P)).then_inc(s.loaded, 16)
            pool.wait_ge(s.loaded, 16)
    segmented_scan(nc, g, spread, out, columns, False)


def attention(nc, g, table, heads, scratch_sums, scratch_pair, scratch_one, scratch_planes):
    both = 2 * heads
    with ExitStack() as stack:
        sbuf, psum = tiles_of(stack, nc)
        logit = sbuf("logit", [P, g.tiles, heads])
        best = sbuf("best", [P, g.tiles, heads])
        spread = sbuf("spread", [P, g.tiles, both])
        pair = sbuf("pair", [P, g.tiles, both])
        node = sbuf("node", [P, g.blocks, heads])
        node_self = sbuf("node_self", [P, g.blocks, heads])
        node_pair = sbuf("node_pair", [P, g.blocks, both])
        node_one = sbuf("node_one", [P, g.blocks, heads])
        mask = g.nonempty[:].unsqueeze(2).to_broadcast([P, g.blocks, heads])
        mask_empty = g.empty[:].unsqueeze(2).to_broadcast([P, g.blocks, heads])
        a_src, a_dst = g.self_logits[:, :, 0:heads], g.self_logits[:, :, heads:both]
        d_node, m_node = node_pair[:, :, 0:heads], node_pair[:, :, heads:both]

        gather_logits(nc, g, table, heads, logit)
        segmented_scan(nc, g, logit, best, heads, True)
        store_edges(nc, g, [(scratch_sums.rearrange("(p i) v -> p i v", p=P), best[:])])
        at_last_edges(nc, g, scratch_sums, node, heads)
        with phase(nc, "own") as (block, s):
            @block.vector
            def _(dve):
                link = linker(dve, s.own)
                link(nc.vector.tensor_tensor(node[:], node[:], mask, ALU.mult))
                link(nc.vector.tensor_tensor(node_self[:], a_src, mask_empty, ALU.mult))
                link(nc.vector.tensor_tensor(node[:], node[:], node_self[:], ALU.add))
                link(nc.vector.tensor_tensor(node[:], node[:], a_src, ALU.max))
                link(nc.vector.tensor_tensor(node[:], node[:], a_dst, ALU.add))
                nc.vector.tensor_copy(d_node, a_dst)
                link(nc.vector.scalar_tensor_tensor(m_node, node[:], 0.2, node[:], ALU.mult, ALU.max))
                link(nc.vector.tensor_tensor(node_self[:], a_src, a_dst, ALU.add))
                link(nc.vector.scalar_tensor_tensor(node_self[:], node_self[:], 0.2, node_self[:], ALU.mult, ALU.max))
                link(nc.vector.tensor_tensor(node_self[:], node_self[:], m_node, ALU.subtract))
        to_edges(nc, g, node_pair, both, scratch_pair, spread, pair)
        with phase(nc, "own", "logits", "exponents") as (block, s):
            @block.vector
            def _(dve):
                link = linker(dve, s.own)
                link(nc.vector.tensor_tensor(logit[:], logit[:], pair[:, :, 0:heads], ALU.add))
                link(nc.vector.scalar_tensor_tensor(logit[:], logit[:], 0.2, logit[:], ALU.mult, ALU.max))
                nc.vector.tensor_tensor(logit[:], logit[:], pair[:, :, heads:both], ALU.subtract
                                        ).then_inc(s.logits, 1)

            @block.scalar
            def _(act):
                nc.scalar.activation(node_self[:], node_self[:], ACT.Exp)
                act.wait_ge(s.logits, 1)
                nc.scalar.activation(logit[:], logit[:], ACT.Exp).then_inc(s.exponents, 1)
        segmented_scan(nc, g, logit, best, heads, False)
        store_edges(nc, g, [(scratch_sums.rearrange("(p i) v -> p i v", p=P), best[:])])
        at_last_edges(nc, g, scratch_sums, node, heads)
        with phase(nc, "own") as (block, s):
            @block.vector
            def _(dve):
                link = linker(dve, s.own)
                link(nc.vector.tensor_tensor(node[:], node[:], mask, ALU.mult))
                link(nc.vector.tensor_tensor(node[:], node[:], node_self[:], ALU.add))
                link(nc.vector.reciprocal(node_one[:], node[:]))
                link(nc.vector.tensor_tensor(g.alpha_self[:, :, 0:heads], node_self[:], node_one[:], ALU.mult))
        to_edges(nc, g, node_one, heads, scratch_one, best, pair[:, :, 0:heads])
        lay_out_weights(nc, g, logit, pair[:, :, 0:heads], spread, heads, scratch_planes)


def lay_out_weights(nc, g, exponents, inverse, spare, heads, planes):
    rows = max(r for r in range(1, P + 1) if g.tiles % r == 0)
    groups = g.tiles // rows
    spare = spare[:].rearrange("p i v -> p (i v)")
    product = spare[:, 0:heads * g.tiles].rearrange("p (h i) -> p h i", h=heads)
    with ExitStack() as stack:
        sbuf, psum = tiles_of(stack, nc)
        by_tile = sbuf("by_tile", [rows, heads, groups, P])
        turned = [psum(f"turned{n}") for n in range(BUFS)]
        with phase(nc, "product", "stored", "loaded", "turned", "copied") as (block, s):
            jobs = [(h, n) for h in range(heads) for n in range(groups)]

            @block.sync
            def _(sync):
                sync.wait_ge(s.product, 1)
                for h in range(heads):
                    sync.dma_start(planes[h].rearrange("(p i) -> p i", p=P), product[:, h, :]).then_inc(s.stored, 16)
                sync.wait_ge(s.stored, 16 * heads)
                for h in range(heads):
                    sync.dma_start(by_tile[:, h, :, :],
                                   planes[h].rearrange("(n r p) -> r n p", r=rows, p=P)).then_inc(s.loaded, 16)

            @block.tensor
            def _(pe):
                pe.wait_ge(s.loaded, 16 * heads)
                for n, (h, k) in enumerate(jobs):
                    if n >= BUFS:
                        pe.wait_ge(s.copied, n - BUFS + 1)
                    nc.tensor.matmul(turned[n % BUFS][:, 0:rows], by_tile[:, h, k, :],
                                     g.identity[0:rows, 0:rows], start=True, stop=True).then_inc(s.turned, 1)

            @block.vector
            def _(dve):
                nc.vector.tensor_tensor(product, exponents[:].rearrange("p i h -> p h i"),
                                        inverse.rearrange("p i h -> p h i"), ALU.mult).then_inc(s.product, 1)
                for n, (h, k) in enumerate(jobs):
                    dve.wait_ge(s.turned, n + 1)
                    nc.vector.tensor_copy(g.alpha[:, h, k * rows:(k + 1) * rows],
                                          turned[n % BUFS][:, 0:rows]).then_inc(s.copied, 1)


def combine(nc, g, spec):
    chunks = math.ceil(spec.features / P)
    width = spec.features // chunks
    own_rows = spec.own is not None and spec.own != "x"
    turn = spec.own is not None and spec.finish != "last"
    copies = not turn or spec.own == "x"
    residual = spec.finish in ("relu", "add", "weight_sum", "last")
    columns = spec.columns
    chain_length = {"relu": 2, "add": 2, "weight_sum": 2, "last": 2, "scale": 1, "logits": 0}[spec.finish]
    pairs = g.blocks // 2

    def nodes(i, j):
        return bass.ds(i * (2 * P) + j * P, P)

    def blk(i, j):
        return bass.ds(i * 2 + j, 1)

    with ExitStack() as stack:
        sbuf, psum = tiles_of(stack, nc)
        rows = sbuf("rows", [P, 2, spec.features])
        own_scaled = sbuf("own_scaled", [P, 2, spec.features])
        sums = sbuf("sums", [width, 2, chunks, P])
        left = sbuf("left", [width, 2, chunks, P])
        aggregate_left = sbuf("aggregate_left", [width, 2, chunks, P])
        if spec.own == "x":
            support_rows = sbuf("support_rows", [P, 2, COPIES, spec.features])
            support = [psum(f"support{n}") for n in range(2)]
        out = sbuf("out", [P, 2, columns])
        turned = [psum(f"turned{n}") for n in range(2)]
        product = [psum(f"product{n}") for n in range(2)]

        def view(tile):
            return tile[0:width, 0:chunks * P].rearrange("p (c n) -> p c n", c=chunks)

        with phase(nc, "own", "issued", "loaded0", "loaded1", "scaled", "copied", "turned", "summed", "left_ready",
                   "support_turned", "multiplied", "finished", "out_free", "stored0", "stored1") as (block, s):
            loaded, stored = [s.loaded0, s.loaded1], [s.stored0, s.stored1]

            if spec.own == "x":
                @block.sync
                def _(sync):
                    with sync.Fori(0, pairs) as i:
                        for j in range(2):
                            sync.wait_ge(s.finished, i * 2 + (j + 1))
                            for q in range(COPIES):
                                sync.dma_start(support_rows[:, j, q, :], spec.support[q][nodes(i, j), :]
                                               ).then_inc(loaded[j], 16)

            if own_rows or not residual:
                @block.sync
                def _(sync):
                    if not residual:
                        sync.sem_inc(s.out_free, 2)
                    with sync.Fori(0, pairs) as i:
                        for j in range(2):
                            if own_rows:
                                sync.wait_ge(s.finished, i * 2 + (j + 1))
                                sync.dma_start(rows[:, j, :], spec.own[nodes(i, j), :]).then_inc(loaded[j], 16)
                        if not residual:
                            for j in range(2):
                                sync.wait_ge(s.finished, i * 2 + (j + 3))
                                sync.dma_start(spec.store[nodes(i, j), :], out[:, j, 0:spec.stored_columns]
                                               ).then_inc(stored[j], 16)
                            for j in range(2):
                                sync.wait_ge(stored[j], i * 16 + 16)
                                sync.sem_inc(s.out_free, 1)

            @block.scalar
            def _(act):
                with act.Fori(0, pairs) as i:
                    if copies and spec.own != "x":
                        for j in range(2):
                            act.wait_ge(s.finished, i * 2 + (j + 1))
                            nc.scalar.copy(aggregate_left[:, j, :, :], g.acc[0:width, 0:chunks, nodes(i, j)]
                                           ).then_inc(s.copied, 1)
                    if spec.own == "x":
                        for j in range(2):
                            nc.scalar.copy(own_scaled[:, j, :], g.x[:, blk(i, j), :].rearrange("p a f -> p (a f)")
                                           ).then_inc(s.scaled, 1)
                        for j in range(2):
                            act.wait_ge(s.support_turned, i * 2 + (j + 1))
                            nc.scalar.copy(aggregate_left[:, j, :, :], view(support[j])).then_inc(s.copied, 1)
                    if spec.heads:
                        share = spec.features // spec.heads
                        for j in range(2):
                            act.wait_ge(loaded[j], i * 16 + 16)
                            for h in range(spec.heads):
                                part = slice(h * share, (h + 1) * share)
                                last = nc.scalar.activation(
                                    own_scaled[:, j, part], rows[:, j, part], ACT.Copy,
                                    scale=g.alpha_self[:, blk(i, j), h:h + 1].rearrange("p a b -> p (a b)"))
                            last.then_inc(s.scaled, 1)
                    if turn:
                        for j in range(2):
                            if spec.own == "x":
                                act.wait_ge(s.turned, i * 2 + (j + 1))
                                nc.scalar.copy(left[:, j, :, :], view(turned[j])).then_inc(s.left_ready, 1)
                                continue
                            act.wait_ge(s.summed, i * 2 + (j + 1))
                            for c in range(chunks):
                                bias = spec.feature_bias[:, c:c + 1] if spec.feature_bias is not None else 0.0
                                last = nc.scalar.activation(left[:, j, c, :], sums[:, j, c, :],
                                                            ACT.Relu if spec.rectify else ACT.Identity, bias=bias)
                            last.then_inc(s.left_ready, 1)

            @block.tensor
            def _(pe):
                with pe.Fori(0, pairs) as i:
                    if spec.own == "x":
                        for j in range(2):
                            pe.wait_ge(loaded[j], i * (16 * COPIES) + 16 * COPIES)
                            pe.wait_ge(s.finished, i * 2 + (j + 1))
                            for c in range(chunks):
                                for q in range(COPIES):
                                    last = nc.tensor.matmul(
                                        support[j][:, c * P:(c + 1) * P],
                                        support_rows[:, j, q, c * P:(c + 1) * P], g.identity[:],
                                        start=(q == 0), stop=(q == COPIES - 1))
                            last.then_inc(s.support_turned, 1)
                    if turn:
                        for j in range(2):
                            if spec.heads or spec.own == "x":
                                pe.wait_ge(s.scaled, i * 2 + (j + 1))
                            elif own_rows:
                                pe.wait_ge(loaded[j], i * 16 + 16)
                            pe.wait_ge(s.finished, i * 2 + (j + 1))
                            for c in range(chunks):
                                part = slice(c * width, (c + 1) * width)
                                source = (own_scaled if spec.heads or spec.own == "x" else rows)[:, j, part]
                                last = nc.tensor.matmul(turned[j][0:width, c * P:(c + 1) * P], source,
                                                        g.identity[:], start=True, stop=True)
                            last.then_inc(s.turned, 1)
                    for j in range(2):
                        if turn:
                            pe.wait_ge(s.left_ready, i * 2 + (j + 1))
                        if copies:
                            pe.wait_ge(s.copied, i * 2 + (j + 1))
                        pe.wait_ge(s.finished, i * 2 + (j + 1))
                        if spec.finish == "last":
                            for c in range(chunks):
                                last = nc.tensor.matmul(product[j][:, c * P:(c + 1) * P],
                                                        aggregate_left[:, j, c, :], g.identity[:],
                                                        start=True, stop=True)
                        else:
                            factors = []
                            if turn:
                                factors += [(left[:, j, c, :], spec.factor[0], c) for c in range(chunks)]
                            if copies:
                                factors += [(aggregate_left[:, j, c, :], spec.factor[-1], c)
                                            for c in range(chunks)]
                            for n, (lhs, matrix, c) in enumerate(factors):
                                last = nc.tensor.matmul(product[j][:, 0:columns], lhs, matrix[:, c, 0:columns],
                                                        start=(n == 0), stop=(n == len(factors) - 1))
                        last.then_inc(s.multiplied, 1)

            @block.vector
            def _(dve):
                dve.sem_inc(s.finished, 2)
                with dve.Fori(0, pairs) as i:
                    done = [0]

                    def link(instruction):
                        done[0] += 1
                        instruction.then_inc(s.own, 1)
                        dve.wait_ge(s.own, i * (2 * chain_length) + done[0])

                    if turn and spec.own != "x":
                        for j in range(2):
                            dve.wait_ge(s.turned, i * 2 + (j + 1))
                            nc.vector.tensor_tensor(sums[:, j, :, :], g.acc[0:width, 0:chunks, nodes(i, j)],
                                                    view(turned[j]), ALU.add).then_inc(s.summed, 1)
                    if spec.finish == "last":
                        for j in range(2):
                            dve.wait_ge(loaded[j], i * 16 + 16)
                    for j in range(2):
                        dve.wait_ge(s.multiplied, i * 2 + (j + 1))
                        got, to = product[j][:, 0:columns], out[:, j, :]
                        x = g.x[:, blk(i, j), :].rearrange("p a f -> p (a f)")
                        if residual:
                            if spec.finish == "relu":
                                link(nc.vector.tensor_tensor(to, got, spec.bias[:], ALU.add))
                                link(nc.vector.scalar_tensor_tensor(x, to, 0.0, x, ALU.max, ALU.add))
                            elif spec.finish == "add":
                                link(nc.vector.tensor_tensor(to, got, spec.bias[:], ALU.add))
                                link(nc.vector.tensor_tensor(x, x, to, ALU.add))
                            elif spec.finish == "weight_sum":
                                link(nc.vector.scalar_tensor_tensor(to, spec.bias[:], g.weight_sum[:, blk(i, j)],
                                                                    got, ALU.mult, ALU.add))
                                link(nc.vector.tensor_tensor(x, x, to, ALU.add))
                            else:
                                link(nc.vector.tensor_tensor(to, got, rows[:, j, :], ALU.add))
                                link(nc.vector.scalar_tensor_tensor(x, to, g.root_degree[:, blk(i, j)], x,
                                                                    ALU.mult, ALU.add))
                            dve.sem_inc(s.issued, 1)
                            nc.vector.bn_stats(g.stats[:, blk(i, j), :].rearrange("p a v -> p (a v)"), x
                                               ).then_inc(s.finished, 1)
                        elif spec.finish == "scale":
                            dve.wait_ge(s.out_free, i * 2 + (j + 1))
                            link(nc.vector.scalar_tensor_tensor(to, got, g.root_degree[:, blk(i, j)],
                                                                spec.bias[:], ALU.mult, ALU.add))
                            nc.vector.tensor_scalar(to, to, g.root_degree[:, blk(i, j)], None, ALU.mult
                                                    ).then_inc(s.finished, 1)
                        else:
                            dve.wait_ge(s.out_free, i * 2 + (j + 1))
                            n = spec.stored_columns
                            nc.vector.tensor_copy(
                                g.self_logits[:, blk(i, j), 0:columns - n].rearrange("p a v -> p (a v)"), got[:, n:])
                            nc.vector.tensor_copy(to[:, 0:n], got[:, 0:n]).then_inc(s.finished, 1)


def project(nc, g, spec):
    chunks = g.features // P
    columns = spec.columns
    pairs = g.blocks // 2
    product_of = spec.finish != "norm"

    def nodes(i, j):
        return bass.ds(i * (2 * P) + j * P, P)

    def blk(i, j):
        return bass.ds(i * 2 + j, 1)

    with ExitStack() as stack:
        sbuf, psum = tiles_of(stack, nc)
        left = sbuf("left", [P, 2, chunks, P])
        normal = sbuf("normal", [P, 2, g.features])
        out = sbuf("out", [P, 2, columns])
        mean = sbuf("mean", [P, g.blocks])
        variance = sbuf("variance", [P, g.blocks])
        spread = sbuf("spread", [P, g.blocks])
        root = sbuf("root", [P, g.blocks])
        turned = [psum(f"turned{n}") for n in range(2)]
        product = [psum(f"product{n}") for n in range(2)]
        with phase(nc, "own", "variance_ready", "root_ready", "normed", "kept", "turned", "left_ready", "multiplied", "finished",
                   "out_free", "stored0", "stored1") as (block, s):
            stored = [s.stored0, s.stored1]

            @block.sync
            def _(sync):
                if not product_of:
                    for n, (dram, tile, b) in enumerate(spec.norm_stores):
                        sync.wait_ge(s.normed, b)
                        sync.dma_start(dram, tile).then_inc(stored[0], 16)
                    sync.wait_ge(stored[0], 16 * len(spec.norm_stores))
                    return
                sync.sem_inc(s.out_free, 2)
                with sync.Fori(0, pairs) as i:
                    for j in range(2):
                        sync.wait_ge(s.finished, i * 2 + (j + 3))
                        sync.dma_start(spec.store[nodes(i, j), :], out[:, j, 0:spec.stored_columns]
                                       ).then_inc(stored[j], 16)
                    for j in range(2):
                        sync.wait_ge(stored[j], i * 16 + 16)
                        sync.sem_inc(s.out_free, 1)

            @block.scalar
            def _(act):
                act.wait_ge(s.variance_ready, 1)
                nc.scalar.activation(root[:], variance[:], ACT.Sqrt).then_inc(s.root_ready, 1)
                if product_of:
                    with act.Fori(0, pairs) as i:
                        for j in range(2):
                            act.wait_ge(s.normed, i * 2 + (j + 1))
                            nc.scalar.copy(g.x[:, blk(i, j), :].rearrange("p a f -> p (a f)"), normal[:, j, :]
                                           ).then_inc(s.kept, 1)
                        for j in range(2):
                            act.wait_ge(s.turned, i * 2 + (j + 1))
                            nc.scalar.copy(left[:, j, :, :],
                                           turned[j][:, 0:chunks * P].rearrange("p (c n) -> p c n", c=chunks)
                                           ).then_inc(s.left_ready, 1)

            if product_of:
                @block.tensor
                def _(pe):
                    with pe.Fori(0, pairs) as i:
                        for j in range(2):
                            pe.wait_ge(s.normed, i * 2 + (j + 1))
                            pe.wait_ge(s.finished, i * 2 + (j + 1))
                            for c in range(chunks):
                                last = nc.tensor.matmul(
                                    turned[j][:, c * P:(c + 1) * P],
                                    normal[:, j, c * P:(c + 1) * P],
                                    g.identity[:], start=True, stop=True)
                            last.then_inc(s.turned, 1)
                        for j in range(2):
                            pe.wait_ge(s.left_ready, i * 2 + (j + 1))
                            for c in range(chunks):
                                last = nc.tensor.matmul(product[j][:, 0:columns], left[:, j, c, :],
                                                        spec.factor[:, c, 0:columns],
                                                        start=(c == 0), stop=(c == chunks - 1))
                            last.then_inc(s.multiplied, 1)

            @block.vector
            def _(dve):
                link = linker(dve, s.own)
                mean_even, mean_odd = g.stats[:, :, 1], g.stats[:, :, 4]
                link(nc.vector.tensor_tensor(mean[:], mean_even, mean_odd, ALU.add))
                link(nc.vector.tensor_scalar(mean[:], mean[:], 0.5, None, ALU.mult))
                link(nc.vector.tensor_tensor(spread[:], mean_even, mean_odd, ALU.subtract))
                link(nc.vector.scalar_tensor_tensor(spread[:], spread[:], 0.25, spread[:], ALU.mult, ALU.mult))
                link(nc.vector.tensor_tensor(variance[:], g.stats[:, :, 2], g.stats[:, :, 5], ALU.add))
                link(nc.vector.scalar_tensor_tensor(variance[:], variance[:], 1.0 / g.features, spread[:],
                                                    ALU.mult, ALU.add))
                link(nc.vector.tensor_scalar(variance[:], variance[:], 1e-5, None, ALU.add))
                dve.sem_inc(s.variance_ready, 1)
                dve.wait_ge(s.root_ready, 1)
                inverse_root(nc, link, variance, root, spread)
                dve.sem_inc(s.finished, 2)
                dve.sem_inc(s.kept, 2)
                with dve.Fori(0, pairs) as i:
                    for j in range(2):
                        x = g.x[:, blk(i, j), :].rearrange("p a f -> p (a f)")
                        if product_of:
                            dve.wait_ge(s.kept, i * 2 + (j + 1))
                        nc.vector.tensor_scalar(normal[:, j, :] if product_of else x, x, mean[:, blk(i, j)],
                                                root[:, blk(i, j)], ALU.subtract, ALU.mult
                                                ).then_inc(s.normed, 1)
                    if product_of:
                        for j in range(2):
                            dve.wait_ge(s.multiplied, i * 2 + (j + 1))
                            dve.wait_ge(s.out_free, i * 2 + (j + 1))
                            got, to = product[j][:, 0:columns], out[:, j, :]
                            if spec.finish == "scale":
                                nc.vector.tensor_tensor(to, got, spec.bias[:], ALU.add).then_inc(s.own, 1)
                                dve.wait_ge(s.own, i * 2 + (j + 1 + link.count[0]))
                                nc.vector.tensor_scalar(to, to, g.root_degree[:, blk(i, j)], None, ALU.mult
                                                        ).then_inc(s.finished, 1)
                            else:
                                n = spec.stored_columns
                                nc.vector.tensor_copy(
                                    g.self_logits[:, blk(i, j), 0:columns - n].rearrange("p a v -> p (a v)"),
                                    got[:, n:])
                                nc.vector.tensor_copy(to[:, 0:n], got[:, 0:n]).then_inc(s.finished, 1)


def load(nc, *pairs):
    with phase(nc, "loaded") as (block, s):
        @block.sync
        def _(sync):
            for tile, dram in pairs:
                sync.dma_start(tile, dram, allow_slow_non_contiguous=True).then_inc(s.loaded, 16)
            sync.wait_ge(s.loaded, 16 * len(pairs))


def by_rows(weight):
    return weight.rearrange("(c p) n -> p c n", p=min(P, weight.shape[0]))


def on_all(bias):
    return bias.unsqueeze(0).to_broadcast([P, bias.shape[0]])


def attention_factor(nc, factor, weight, att_src, att_dst, stack):
    heads, share = att_src.shape
    n = heads * share
    sbuf, _ = tiles_of(stack, nc)
    with ExitStack() as inner:
        sbuf, _ = tiles_of(inner, nc)
        att = sbuf("att", [P, 2, n])
        each = sbuf("each", [P, 2, n])
        with phase(nc, "own", "loaded") as (block, s):
            @block.sync
            def _(sync):
                sync.dma_start(factor[:, :, 0:n], by_rows(weight)).then_inc(s.loaded, 16)
                for k, a in enumerate((att_src, att_dst)):
                    sync.dma_start(att[:, k, :], a.rearrange("h c -> (h c)").unsqueeze(0).to_broadcast([P, n])
                                   ).then_inc(s.loaded, 16)

            @block.vector
            def _(dve):
                link = linker(dve, s.own)
                dve.wait_ge(s.loaded, 48)
                for c in range(2):
                    for k in range(2):
                        link(nc.vector.tensor_tensor(each[:, c, :], factor[:, c, 0:n], att[:, k, :], ALU.mult))
                        link(nc.vector.tensor_reduce(factor[:, c, n + k * heads:n + (k + 1) * heads],
                                                     each[:, c, :].rearrange("p (h v) -> p h v", h=heads),
                                                     AXX, ALU.add))


def build_program(nc, t, output):
    nodes, features, edges = t.nodes, t.x.shape[1], t.edges
    tiles, blocks = sizes(nodes, edges)
    g = Graph()
    g.nodes, g.features, g.tiles, g.blocks = nodes, features, tiles, blocks
    padded, slots = blocks * P, tiles * P
    heads, hidden = t.L1_gnn_att_src1.shape

    def dram(name, shape):
        return nc.dram_tensor(name, shape, FP32, kind="Internal").ap()

    g.offset_dram = dram("offset_dram", [P, tiles + 2])
    g.base_float_dram = dram("base_float_dram", [1, tiles])
    g.half_offset_dram = dram("half_offset_dram", [P, tiles])
    g.half_base_float_dram = dram("half_base_float_dram", [1, tiles // HALF])
    g.source_flat, g.x_dram = t.src_flat, t.x
    support = [dram(f"support{n}", [padded + P, features]) for n in range(COPIES)]
    spare = dram("spare", [HALF, 2, P, P])
    rows1, rows2 = dram("gat_rows1", [padded, features]), dram("gat_rows2", [padded, hidden])
    logits1, logits2 = dram("gat_logits1", [padded, heads]), dram("gat_logits2", [padded, 1])
    norm2 = dram("norm2", [padded, features])
    gcn = [dram(f"gcn_rows{n}", [padded, features]) for n in range(3)]
    scratch = {n: dram(f"scratch{n}", [slots, n]) for n in (2 * heads, heads, 2, 1)}
    segment = {n: dram(f"segment{n}", [slots, n]) for n in (heads, 1)}
    planes = dram("planes", [heads, slots])

    with ExitStack() as stack:
        sbuf, _ = tiles_of(stack, nc)
        g.source = sbuf("source", [P, tiles + RING], INT32)
        g.source_chunk = sbuf("source_chunk", [P, tiles + RING], INT32)
        g.offset = sbuf("offset", [P, tiles + 2])
        g.base = sbuf("base", [1, tiles], INT32)
        g.base_float = sbuf("base_float", [1, tiles])
        g.last_window = sbuf("last_window", [1, 1], INT32)
        g.edge_values = sbuf("edge_values", [P, tiles, 3])
        g.half_base = sbuf("half_base", [1, tiles // HALF], INT32)
        g.half_base_float = sbuf("half_base_float", [1, tiles // HALF])
        g.half_last_window = sbuf("half_last_window", [1, 1], INT32)
        g.half_offset = sbuf("half_offset", [P, tiles])
        g.source_float = sbuf("source_float", [P, tiles])
        g.to_spare = sbuf("to_spare", [P, tiles])
        g.earlier = sbuf("earlier", [P, P])
        g.keep = sbuf("keep", [P, tiles])
        g.reset = sbuf("reset", [P, tiles])
        g.keep_row = sbuf("keep_row", [8, P])
        g.reset_row = sbuf("reset_row", [8, P])
        g.iota = sbuf("iota", [P, P])
        g.identity = sbuf("identity", [P, P])
        g.x = sbuf("x", [P, blocks, features])
        g.stats = sbuf("stats", [P, blocks, 6])
        g.weight_sum = sbuf("weight_sum", [P, blocks])
        g.root_degree = sbuf("root_degree", [P, blocks])
        g.nonempty = sbuf("nonempty", [P, blocks])
        g.empty = sbuf("empty", [P, blocks])
        g.first_edge = sbuf("first_edge", [P, blocks], INT32)
        g.last_edge = sbuf("last_edge", [P, blocks], INT32)
        g.self_logits = sbuf("self_logits", [P, blocks, 2 * heads])
        g.alpha_self = sbuf("alpha_self", [P, blocks, heads])
        edge_weight = g.edge_values[:, :, 0:1].rearrange("p i a -> p a i")
        gate = g.edge_values[:, :, 1:2].rearrange("p i a -> p a i")

        def scoped():
            inner = ExitStack()
            return inner, tiles_of(inner, nc)[0]

        def spec(**fields):
            base = dict(features=features, own=None, heads=0, factor=None, feature_bias=None, rectify=False,
                        columns=features, bias=None, store=None, stored_columns=features)
            base.update(fields)
            return namedtuple("Spec", list(base))(**base)

        set_up(nc, g, t)
        zero_scratch(nc, g, scratch)

        inner, part = scoped()
        with inner:
            with ExitStack() as first:
                histogram = tiles_of(first, nc)[0]("histogram", [3, padded])
                windows(nc, g, lambda first: scatter_by_source(nc, g, support, spare, histogram, first),
                        (g.half_offset, g.half_base_float, g.half_base, g.half_offset_dram,
                         g.half_base_float_dram, g.half_last_window))
                degrees(nc, g, histogram)
            top, bottom = part("top", [P, 2, features]), part("bottom", [P, 2, features])
            bias = part("bias", [P, features])
            load(nc, (top[:], by_rows(t.L0_gnn_W[0:features, :])), (bottom[:], by_rows(t.L0_gnn_W[features:, :])),
                 (bias[:], on_all(t.L0_gnn_b)))
            combine(nc, g, spec(own="x", support=support, factor=[top, bottom], bias=bias, finish="relu"))
        g.alpha = sbuf("alpha", [P, heads, tiles])

        inner, part = scoped()
        with inner as held:
            factor = part("factor", [P, 2, features + 2 * heads])
            attention_factor(nc, factor, t.L1_gnn_W1, t.L1_gnn_att_src1, t.L1_gnn_att_dst1, held)
            project(nc, g, spec(factor=factor, columns=features + 2 * heads, store=rows1, finish="logits"))
        store_edges(nc, g, [(logits1.rearrange("(b p) h -> p b h", p=P), g.self_logits[:, :, 0:heads])])
        attention(nc, g, logits1, heads, segment[heads], scratch[2 * heads], scratch[heads], planes)
        inner, part = scoped()
        with inner as held:
            g.acc = part("acc", [P, 2, padded])
            aggregate_windows(nc, g, rows1, features, g.alpha, heads)
            factor = part("factor", [P, 2, hidden + 2])
            attention_factor(nc, factor, t.L1_gnn_W2, t.L1_gnn_att_src2, t.L1_gnn_att_dst2, held)
            bias = part("bias", [P, 2])
            load(nc, *((bias[:, c:c + 1], t.L1_gnn_b1[c * P:(c + 1) * P].unsqueeze(1)) for c in range(2)))
            combine(nc, g, spec(own=rows1, heads=heads, factor=[factor], feature_bias=bias, rectify=True,
                                columns=hidden + 2, store=rows2, stored_columns=hidden, finish="logits"))

        store_edges(nc, g, [(logits2.rearrange("(b p) h -> p b h", p=P), g.self_logits[:, :, 0:1])])
        attention(nc, g, logits2, 1, segment[1], scratch[2], scratch[1], planes)
        inner, part = scoped()
        with inner:
            g.acc = part("acc", [P, 2, padded])
            aggregate_windows(nc, g, rows2, hidden, g.alpha, 1)
            factor = part("factor", [hidden, 1, features])
            feature_bias, bias = part("feature_bias", [hidden, 1]), part("bias", [P, features])
            load(nc, (factor[:], by_rows(t.L1_gnn_Wf)), (feature_bias[:], t.L1_gnn_b2.unsqueeze(1)),
                 (bias[:], on_all(t.L1_gnn_bf)))
            combine(nc, g, spec(own=rows2, features=hidden, heads=1, factor=[factor], feature_bias=feature_bias,
                                bias=bias, finish="add"))
        norm_store = [(norm2.rearrange("(b p) f -> p b f", p=P)[:, b:min(b + 10, blocks), :],
                       g.x[:, b:min(b + 10, blocks), :], min(b + 10, blocks)) for b in range(0, blocks, 10)]
        project(nc, g, spec(finish="norm", norm_stores=norm_store))

        inner, part = scoped()
        with inner:
            g.acc = part("acc", [P, 2, padded])
            aggregate_windows(nc, g, norm2, features, edge_weight, 1)
            factor, bias = part("factor", [P, 2, features]), part("bias", [P, features])
            load(nc, (factor[:], by_rows(t.L2_gnn_weight)), (bias[:], on_all(t.L2_gnn_bias)))
            combine(nc, g, spec(factor=[factor], bias=bias, finish="weight_sum"))

        inner, part = scoped()
        with inner:
            factor, bias = part("factor", [P, 2, features]), part("bias", [P, features])
            g.acc = part("acc", [P, 2, padded])
            load(nc, (factor[:], by_rows(t.L3_gnn_W1)), (bias[:], on_all(t.L3_gnn_b1)))
            project(nc, g, spec(factor=factor, bias=bias, store=gcn[0], finish="scale"))
            for n, (w, b) in enumerate(((t.L3_gnn_W2, t.L3_gnn_b2), (t.L3_gnn_W3, t.L3_gnn_b3))):
                aggregate_windows(nc, g, gcn[n], features, gate, 1)
                load(nc, (factor[:], by_rows(w)), (bias[:], on_all(b)))
                combine(nc, g, spec(own=gcn[n], factor=[factor], bias=bias, rectify=True, store=gcn[n + 1],
                                    finish="scale"))
            aggregate_windows(nc, g, gcn[2], features, gate, 1)
            combine(nc, g, spec(own=gcn[2], finish="last"))
        full, rest = nodes // P, nodes % P
        out_stores = [(output[b * P:min(b + 8, full) * P, :].rearrange("(b p) f -> p b f", p=P),
                       g.x[:, b:min(b + 8, full), :], min(b + 8, full)) for b in range(0, full, 8)]
        if rest:
            out_stores.append((output[full * P:nodes, :], g.x[0:rest, full, :], full + 1))
        project(nc, g, spec(finish="norm", norm_stores=out_stores))


def zero_scratch(nc, g, scratch):
    with ExitStack() as stack:
        sbuf, _ = tiles_of(stack, nc)
        most = max(scratch)
        zeros = sbuf("zeros", [P, g.tiles * most])
        with phase(nc, "zeroed", "stored") as (block, s):
            @block.vector
            def _(dve):
                nc.vector.memset(zeros[:], 0.0).then_inc(s.zeroed, 1)

            @block.sync
            def _(sync):
                sync.wait_ge(s.zeroed, 1)
                for n, dram in scratch.items():
                    sync.dma_start(dram.rearrange("(p i) v -> p (i v)", p=P), zeros[:, 0:g.tiles * n]
                                   ).then_inc(s.stored, 16)
                sync.wait_ge(s.stored, 16 * len(scratch))


_PLAIN = ["L0_gnn_W", "L0_gnn_b", "L1_gnn_W1", "L1_gnn_att_src1", "L1_gnn_att_dst1", "L1_gnn_b1",
          "L1_gnn_W2", "L1_gnn_att_src2", "L1_gnn_att_dst2", "L1_gnn_b2", "L1_gnn_Wf", "L1_gnn_bf",
          "L2_gnn_weight", "L2_gnn_bias", "L3_gnn_W1", "L3_gnn_b1", "L3_gnn_W2", "L3_gnn_b2", "L3_gnn_W3",
          "L3_gnn_b3", "L3_gnn_mw1", "L3_gnn_mb1", "L3_gnn_mw2", "L3_gnn_mb2"]


def lay_out(inputs):
    nodes, edges = inputs["x"].shape[0], inputs["src"].shape[0]
    tiles, blocks = sizes(nodes, edges)

    def pad(a, value, front=0):
        a = np.asarray(a).reshape(-1)
        whole = np.full(tiles * P + front, value, a.dtype)
        whole[front:front + edges] = a
        return whole[:tiles * P]

    def by_tile(a):
        return np.ascontiguousarray(a.reshape(tiles, P).T)

    src, dst = pad(inputs["src"], 0), pad(inputs["dst"], nodes)
    before = np.concatenate([np.full(1, -1, dst.dtype), dst[:-1]])
    arrays = {n: np.ascontiguousarray(inputs[n]) for n in _PLAIN}
    x = np.zeros((blocks * P, inputs["x"].shape[1]), np.float32)
    x[:nodes] = inputs["x"]
    arrays.update(x=x, src_flat=src.reshape(1, -1), src_tile=by_tile(src), src_chunk=src.reshape(P, tiles), dst_tile=by_tile(dst),
                  dst_chunk=dst.reshape(P, tiles), before_chunk=before.reshape(P, tiles),
                  weight_tile=by_tile(pad(inputs["edge_weight"], 0)),
                  attr_tile=by_tile(pad(inputs["edge_weight1"], 0)))
    return arrays


def kernel(**inputs):
    import concourse.bacc as bacc
    from concourse.bass_utils import run_bass_kernel_spmd

    arrays = lay_out(inputs)
    nc = bacc.Bacc("TRN2", target_bir_lowering=False, num_devices=1)
    t = {n: nc.dram_tensor(f"in_{n}", a.shape, mybir.dt.from_np(a.dtype), kind="ExternalInput").ap()
         for n, a in arrays.items()}
    t.update(nodes=inputs["x"].shape[0], edges=inputs["src"].shape[0])
    output = nc.dram_tensor("out", inputs["x"].shape, FP32, kind="ExternalOutput").ap()
    build_program(nc, namedtuple("Tensors", list(t))(**t), output)
    result = run_bass_kernel_spmd(nc, [{f"in_{n}": a for n, a in arrays.items()}], core_ids=[0])
    return result.results[0]["out"]
```

```python
import math
from collections import namedtuple
from contextlib import ExitStack, contextmanager

import numpy as np
import concourse.bass as bass
from concourse import mybir

P = 128
RING = 16
HALF = RING // 2
BUFS = 4
COPIES = 4
BIG = 1e30

FP32 = mybir.dt.float32
INT32 = mybir.dt.int32
ALU = mybir.AluOpType
ACT = mybir.ActivationFunctionType
AXX = mybir.AxisListType.X
ENGINES = mybir.ALL_ENGINES


def sizes(nodes, edges):
    tiles = math.ceil(edges / P / RING) * RING
    blocks = 2 * math.ceil((nodes + P) / P / 2)
    return tiles, blocks


class Graph:
    pass


@contextmanager
def phase(nc, *names):
    sems = {n: nc.alloc_semaphore(name=f"{n}_{nc.next_id()}") for n in names}
    with nc.Block() as block:
        yield block, namedtuple("Semaphores", list(sems))(**sems)
    nc.clear_and_free_semaphores(list(sems.values()))
    nc.all_engine_barrier(sem_only=True)


def tiles_of(stack, nc):
    def sbuf(name, shape, dtype=FP32):
        return stack.enter_context(nc.sbuf_tensor(f"{name}_{nc.next_id()}", shape, dtype))

    def psum(name, shape=(P, 512), dtype=FP32):
        return stack.enter_context(nc.psum_tensor(f"{name}_{nc.next_id()}", list(shape), dtype))

    return sbuf, psum


def aggregate(nc, g, table, features, weights, heads, first_pass):
    chunks = math.ceil(features / P)
    width = features // chunks
    share = features // heads
    with ExitStack() as stack:
        sbuf, psum = tiles_of(stack, nc)
        rows = sbuf("rows", [P, RING, features])
        scaled_rows = sbuf("scaled_rows", [P, BUFS, features])
        onehots = sbuf("onehots", [P, BUFS, P])
        index = sbuf("index", [P, RING], INT32)
        sums = [psum(f"sums{n}") for n in range(BUFS)]
        gathered_names = [f"gathered{k}" for k in range(RING)]
        with phase(nc, "index_ready", "issued", "scaled", "onehot_ready", "summed", "added",
                   *gathered_names) as (block, s):
            gathered = s[-RING:]

            @block.gpsimd
            def _(pool):
                with pool.Fori(0, g.tiles // RING) as i:
                    for k in range(RING):
                        if k % HALF == 0:
                            pool.wait_ge(s.index_ready, i * 2 + (k // HALF + 1))
                        pool.wait_ge(s.scaled, i * RING + (k + 1))
                        pool.sem_inc(s.issued, 1)
                        nc.gpsimd.indirect_dma_start(
                            rows[:, k, :], None, table,
                            bass.IndirectOffsetOnAxis(ap=index[:, k:k + 1], axis=0),
                        ).then_inc(gathered[k], 16)

            @block.scalar
            def _(act):
                act.sem_inc(s.scaled, RING)
                for half in range(2):
                    nc.scalar.copy(index[:, half * HALF:(half + 1) * HALF],
                                   g.source[:, half * HALF:(half + 1) * HALF]
                                   ).then_inc(s.index_ready, 1)
                with act.Fori(0, g.tiles // RING) as i:
                    for k in range(RING):
                        act.wait_ge(gathered[k], i * 16 + 16)
                        act.wait_ge(s.summed, i * RING + (k + 1))
                        for h in range(heads):
                            part = slice(h * share, (h + 1) * share)
                            last = nc.scalar.activation(
                                scaled_rows[:, k % BUFS, part], rows[:, k, part], ACT.Copy,
                                scale=weights[:, h, bass.ds(i * RING + k, 1)])
                        last.then_inc(s.scaled, 1)
                        if k % HALF == HALF - 1:
                            half = k // HALF * HALF
                            nc.scalar.copy(index[:, half:half + HALF],
                                           g.source[:, bass.ds(i * RING + (RING + half), HALF)]
                                           ).then_inc(s.index_ready, 1)

            @block.tensor
            def _(pe):
                pe.sem_inc(s.summed, BUFS)
                with pe.Fori(0, g.tiles // RING) as i:
                    for k in range(RING):
                        pe.wait_ge(s.scaled, i * RING + (RING + k + 1))
                        pe.wait_ge(s.onehot_ready, i * RING + (k + 1))
                        pe.wait_ge(s.added, i * RING + (k + 1))
                        b = k % BUFS
                        for c in range(chunks):
                            last = nc.tensor.matmul(
                                sums[b][0:width, c * P:(c + 1) * P],
                                scaled_rows[:, b, c * width:(c + 1) * width], onehots[:, b, :],
                                start=True, stop=True)
                        last.then_inc(s.summed, 1)

            @block.vector
            def _(dve):
                def onehot(slot, column):
                    nc.vector.tensor_scalar(onehots[:, slot, :], g.iota[:], column, None,
                                            ALU.is_equal).then_inc(s.onehot_ready, 1)

                if first_pass:
                    nc.vector.memset(g.acc[0:width, 0:chunks, :], 0.0).then_inc(s.added, BUFS)
                else:
                    dve.sem_inc(s.added, BUFS)
                for k in range(2):
                    onehot(k, g.offset[:, k:k + 1])
                with dve.Fori(0, g.tiles // RING) as i:
                    for k in range(RING):
                        if k % HALF == 0:
                            _, bases = nc.values_load_multi_w_load_instructions(
                                g.base[0:1, bass.ds(i * RING + k, HALF)],
                                engines=[mybir.EngineType.DVE], min_val=0,
                                max_val=(g.blocks - 1) * P,
                                skip_runtime_bounds_check_because="a destination, or clamped")
                            bases = list(bases)
                        onehot((k + 2) % BUFS, g.offset[:, bass.ds(i * RING + (k + 2), 1)])
                        window = bass.ds(bases[k % HALF], P)
                        dve.wait_ge(s.summed, i * RING + (BUFS + k + 1))
                        dve.wait_ge(s.added, i * RING + (BUFS + k))
                        nc.vector.tensor_tensor(
                            g.acc[0:width, 0:chunks, window], g.acc[0:width, 0:chunks, window],
                            sums[k % BUFS][0:width, 0:chunks * P].rearrange("p (c n) -> p c n", c=chunks),
                            ALU.add).then_inc(s.added, 1)


def scatter_by_source(nc, g, support, spare, histogram, first_pass):
    with ExitStack() as stack:
        sbuf, psum = tiles_of(stack, nc)
        parts = 2 * HALF // COPIES
        zeros = sbuf("zeros", [P, (g.blocks + 1) * g.features // parts])
        x_window = sbuf("x_window", [P, 2, g.features])
        source_row = sbuf("source_row", [P, 2, HALF, P], INT32)
        values = sbuf("values", [P, 2, HALF, 3])
        onehots = sbuf("onehots", [P, BUFS, P])
        same_source = sbuf("same_source", [P, BUFS, P])
        scrap = sbuf("scrap", [P, HALF, P])
        repeats = sbuf("repeats", [P, 2, HALF])
        moved = sbuf("moved", [P, 2, HALF])
        index = sbuf("index", [P, 2, HALF], INT32)
        cross = sbuf("cross", [P, BUFS, P])
        rows = sbuf("rows", [P, HALF, g.features])
        cross_bank = [psum(f"cross_bank{n}") for n in range(2)]
        rows_bank = [psum(f"rows_bank{n}") for n in range(2)]
        counts_bank = [psum(f"counts_bank{n}") for n in range(2)]
        names = [f"scattered{k}" for k in range(HALF)]
        with phase(nc, "zeroed", "x_loaded0", "x_loaded1", "row_loaded0", "row_loaded1", "own", "index_ready",
                   "issued", "matrices", "crossed", "cross_copied", "multiplied", "rows_ready", "counted",
                   "values_ready", *names) as (block, s):
            scattered = s[-HALF:]
            x_loaded, row_loaded = [s.x_loaded0, s.x_loaded1], [s.row_loaded0, s.row_loaded1]

            @block.gpsimd
            def _(pool):
                pool.wait_ge(s.zeroed, 1)
                for slot in range(HALF):
                    for part in range(2):
                        if first_pass:
                            flat = support[slot % COPIES].rearrange("n f -> (n f)")
                            size = flat.shape[0] // parts
                            at = (2 * (slot // COPIES) + part) * size
                            target = flat[at:at + size].rearrange("(p z) -> p z", p=P)
                            pool.dma_start(target, zeros[:]).then_inc(scattered[slot], 16)
                        else:
                            pool.dma_start(spare[slot, part], zeros[:, 0:P]).then_inc(scattered[slot], 16)
                for slot in range(HALF):
                    pool.wait_ge(scattered[slot], 32)
                with pool.Fori(0, g.tiles // RING) as i:
                    for k in range(RING):
                        if k % HALF == 0:
                            pool.wait_ge(s.index_ready, i * 2 + (k // HALF + 1))
                        pool.wait_ge(s.rows_ready, i * RING + (k + 3))
                        before = (k - COPIES) % HALF
                        uses = (k - COPIES) // HALF + 1
                        pool.wait_ge(scattered[before], i * 32 + 16 * (uses + 2))
                        pool.sem_inc(s.issued, 1)
                        nc.gpsimd.indirect_dma_start(
                            support[k % COPIES],
                            bass.IndirectOffsetOnAxis(ap=index[:, k // HALF, k % HALF:k % HALF + 1], axis=0),
                            rows[:, k % HALF, :], None, compute_op=ALU.add,
                        ).then_inc(scattered[k % HALF], 16)
                for slot in range(HALF):
                    pool.wait_ge(scattered[slot], 16 * (g.tiles // HALF + 2))
                pool.wait_ge(s.index_ready, g.tiles // HALF + 1)

            @block.sync
            def _(sync):
                with sync.Fori(0, g.tiles // RING) as i:
                    for h in range(2):
                        base = sync.value_load(g.half_base[0:1, bass.ds(i * 2 + h, 1)], min_val=0,
                                               max_val=(g.blocks - 1) * P)
                        sync.wait_ge(s.multiplied, i * RING + HALF * (h + 1))
                        sync.dma_start(x_window[:, h, :], g.x_dram[bass.ds(base, P), :]).then_inc(x_loaded[h], 16)
                        sync.wait_ge(s.matrices, i * RING + HALF * (h + 1))
                        sync.dma_start(
                            source_row[:, h, :, :].rearrange("p k e -> p (k e)"),
                            g.source_flat[0:1, bass.ds((i * 2 + h) * (HALF * P), HALF * P)]
                            .to_broadcast([P, HALF * P])).then_inc(row_loaded[h], 16)
                sync.wait_ge(s.matrices, g.tiles + HALF)
                sync.dma_start(source_row[:, 0, :, :].rearrange("p k e -> p (k e)"),
                               g.source_flat[0:1, 0:HALF * P].to_broadcast([P, HALF * P])
                               ).then_inc(row_loaded[0], 16)

            @block.scalar
            def _(act):
                act.sem_inc(s.cross_copied, 2)
                act.sem_inc(s.rows_ready, 2)

                def copy_rows(i, k):
                    act.wait_ge(s.multiplied, i * RING + (RING + k + 1))
                    act.wait_ge(scattered[k % HALF], i * 32 + 16 * (k // HALF + 2))
                    nc.scalar.copy(rows[:, k % HALF, :], rows_bank[k % 2][:, 0:g.features]).then_inc(s.rows_ready, 1)

                with act.Fori(0, g.tiles // RING) as i:
                    for k in range(RING):
                        if k % HALF == 0:
                            nc.scalar.copy(values[:, k // HALF, :, :],
                                           g.edge_values[:, bass.ds(i * RING + k, HALF), :]
                                           ).then_inc(s.values_ready, 1)
                        act.wait_ge(s.crossed, i * RING + (BUFS + k + 1))
                        nc.scalar.copy(cross[:, k % BUFS, :], cross_bank[k % 2][:, 0:P]).then_inc(s.cross_copied, 1)
                        if k > 0:
                            copy_rows(i, k - 1)
                    copy_rows(i, RING - 1)

            @block.tensor
            def _(pe):
                pe.sem_inc(s.crossed, BUFS)
                pe.sem_inc(s.multiplied, RING)

                def multiply(i, k):
                    if k % HALF == 0:
                        pe.wait_ge(x_loaded[k // HALF], i * 16 + 16)
                    pe.wait_ge(s.cross_copied, i * RING + (k + 3))
                    pe.wait_ge(s.rows_ready, i * RING + (k + 1))
                    nc.tensor.matmul(rows_bank[k % 2][:, 0:g.features], cross[:, k % BUFS, :],
                                     x_window[:, k // HALF, :], start=True, stop=True).then_inc(s.multiplied, 1)

                with pe.Fori(0, g.tiles // RING) as i:
                    for k in range(RING):
                        b = k % BUFS
                        pe.wait_ge(s.matrices, i * RING + (RING + k + 1))
                        pe.wait_ge(s.cross_copied, i * RING + (k + 1))
                        nc.tensor.matmul(cross_bank[k % 2][:, 0:P], onehots[:, b, :], same_source[:, b, :],
                                         start=True, stop=True)
                        if k % HALF == 0:
                            pe.wait_ge(s.values_ready, i * 2 + (k // HALF + 1))
                            pe.wait_ge(s.counted, i * 2 + (k // HALF + 1))
                        nc.tensor.matmul(counts_bank[k // HALF][0:3, 0:P], values[:, k // HALF, k % HALF, :],
                                         onehots[:, b, :], start=(k % HALF == 0), stop=(k % HALF == HALF - 1)
                                         ).then_inc(s.crossed, 1)
                        if k > 0:
                            multiply(i, k - 1)
                    multiply(i, RING - 1)

            @block.vector
            def _(dve):
                nc.vector.memset(zeros[:], 0.0).then_inc(s.zeroed, 1)
                if first_pass:
                    nc.vector.memset(histogram[:], 0.0).then_inc(s.counted, 2)
                else:
                    dve.sem_inc(s.counted, 2)
                dve.sem_inc(s.matrices, RING)
                for slot in range(HALF):
                    dve.wait_ge(scattered[slot], 32)

                def index_half(i, h, ahead):
                    dve.wait_ge(row_loaded[h], i * 16 + 16 * (ahead + 1))
                    for k in range(HALF):
                        last = nc.vector.scalar_tensor_tensor(
                            scrap[:, k, :], source_row[:, h, k, :],
                            g.source_float[:, bass.ds(i * RING + (ahead * RING + h * HALF + k), 1)], g.earlier[:],
                            ALU.is_equal, ALU.mult, accum_out=repeats[:, h, k:k + 1])
                    last.then_inc(s.own, 1)
                    halves = 2 * ahead + h
                    dve.wait_ge(s.own, i * 4 + (2 * halves + 1))
                    here = bass.ds(i * RING + halves * HALF, HALF)
                    nc.vector.scalar_tensor_tensor(moved[:, h, :], repeats[:, h, :], 0.5, g.to_spare[:, here],
                                                   ALU.is_gt, ALU.mult).then_inc(s.own, 1)
                    dve.wait_ge(s.own, i * 4 + (2 * halves + 2))
                    for slot in range(HALF):
                        dve.wait_ge(scattered[slot], i * 32 + 16 * (halves + 1))
                    nc.vector.tensor_tensor(index[:, h, :], moved[:, h, :], g.source_float[:, here],
                                            ALU.add).then_inc(s.index_ready, 1)

                index_half(0, 0, 0)
                with dve.Fori(0, g.tiles // RING) as i:
                    for h in range(2):
                        base = dve.value_load(g.half_base[0:1, bass.ds(i * 2 + h, 1)], min_val=0,
                                              max_val=(g.blocks - 1) * P)
                        for k in range(HALF):
                            b, tile = k % BUFS, bass.ds(i * RING + (h * HALF + k), 1)
                            dve.wait_ge(s.crossed, i * RING + (h * HALF + k + 1))
                            nc.vector.tensor_scalar(onehots[:, b, :], g.iota[:], g.half_offset[:, tile], None,
                                                    ALU.is_equal)
                            nc.vector.tensor_scalar(same_source[:, b, :], source_row[:, h, k, :],
                                                    g.source_float[:, tile],
                                                    g.edge_values[:, tile, 0:1].rearrange("p a v -> p (a v)"),
                                                    ALU.is_equal, ALU.mult).then_inc(s.matrices, 1)
                        index_half(i, 1 - h, h)
                        window = bass.ds(base, P)
                        dve.wait_ge(s.crossed, i * RING + (BUFS + HALF * (h + 1)))
                        dve.wait_ge(s.counted, i * 2 + (h + 2))
                        nc.vector.tensor_tensor(histogram[:, window], histogram[:, window],
                                                counts_bank[h][0:3, 0:P], ALU.add).then_inc(s.counted, 1)


def windows(nc, g, one_pass, tables):
    one_pass(True)
    offset, base_float, base, offset_dram, base_float_dram, last_window = tables
    wide = nc.values_load(last_window[0:1, 0:1], engines=ENGINES, min_val=0, max_val=g.blocks - 1,
                          skip_runtime_bounds_check_because="destinations are below blocks * 128")
    with nc.If(wide > 0):
        with nc.Fori(1, wide + 1):
            with phase(nc, "moved") as (block, s):
                @block.vector
                def _(dve):
                    nc.vector.tensor_scalar(offset[:], offset[:], float(P), None, ALU.subtract)
                    nc.vector.tensor_scalar(base_float[:], base_float[:], float(P),
                                            float((g.blocks - 1) * P), ALU.add, ALU.min).then_inc(s.moved, 1)
                    dve.wait_ge(s.moved, 1)
                    nc.vector.tensor_copy(base[:], base_float[:])
            one_pass(False)
        load(nc, (offset[:], offset_dram[:]), (base_float[:], base_float_dram[:]))
        with phase(nc) as (block, s):
            @block.vector
            def _(dve):
                nc.vector.tensor_copy(base[:], base_float[:])


def aggregate_windows(nc, g, table, features, weights, heads):
    windows(nc, g, lambda first: aggregate(nc, g, table, features, weights, heads, first),
            (g.offset, g.base_float, g.base, g.offset_dram, g.base_float_dram, g.last_window))


def linker(engine, sem):
    count = [0]

    def link(instruction):
        count[0] += 1
        instruction.then_inc(sem, 1)
        engine.wait_ge(sem, count[0])

    link.count = count
    return link


def inverse_root(nc, link, value, root, scratch):
    link(nc.vector.reciprocal(root[:], root[:]))
    link(nc.vector.tensor_tensor(scratch[:], root[:], root[:], ALU.mult))
    link(nc.vector.tensor_tensor(scratch[:], scratch[:], value[:], ALU.mult))
    link(nc.vector.tensor_scalar(scratch[:], scratch[:], -0.5, 1.5, ALU.mult, ALU.add))
    link(nc.vector.tensor_tensor(root[:], root[:], scratch[:], ALU.mult))


def set_up(nc, g, t):
    with ExitStack() as stack:
        sbuf, psum = tiles_of(stack, nc)
        iota_int = sbuf("iota_int", [P, P], INT32)
        lane_int = sbuf("lane_int", [P, 1], INT32)
        lane = sbuf("lane", [P, 1])
        dst_int = sbuf("dst_int", [P, g.tiles], INT32)
        base_int = sbuf("base_int", [P, g.tiles], INT32)
        base_all = sbuf("base_all", [P, g.tiles])
        chunk_dst = sbuf("chunk_dst", [P, g.tiles], INT32)
        chunk_before = sbuf("chunk_before", [P, g.tiles], INT32)
        attribute = sbuf("attribute", [P, g.tiles])
        weight = sbuf("weight", [P, g.tiles])
        hidden = sbuf("hidden", [P, 2, g.tiles])
        gate = sbuf("gate", [P, g.tiles])
        mlp = sbuf("mlp", [P, 25])
        widest = sbuf("widest", [1, 2])
        small = sbuf("small", [P, 5])
        turned = psum("turned")
        groups = g.tiles // HALF
        hid = t.L3_gnn_mw2.shape[0]
        with phase(nc, "loaded", "x_loaded", "iota", "own", "relu", "added", "gated", "kept",
                   "turned", "wide", "stored") as (block, s):
            @block.sync
            def _(sync):
                for out, dram in ((g.source[:, 0:g.tiles], t.src_tile),
                                  (g.source_chunk[:, 0:g.tiles], t.src_chunk),
                                  (dst_int[:], t.dst_tile),
                                  (base_int[:], t.dst_tile[0:1, :].to_broadcast([P, g.tiles])),
                                  (g.base[:], t.dst_tile[0:1, :]), (chunk_dst[:], t.dst_chunk),
                                  (chunk_before[:], t.before_chunk), (attribute[:], t.attr_tile),
                                  (weight[:], t.weight_tile)):
                    sync.dma_start(out, dram).then_inc(s.loaded, 16)
                for at, param in ((0, t.L3_gnn_mw1), (hid, t.L3_gnn_mb1), (2 * hid, t.L3_gnn_mw2),
                                  (3 * hid, t.L3_gnn_mb2)):
                    n = hid if at < 3 * hid else 1
                    sync.dma_start(mlp[:, at:at + n], param.rearrange("a b -> (a b)").unsqueeze(0).to_broadcast([P, n])
                                   if len(param.shape) == 2 else param.unsqueeze(0).to_broadcast([P, n])
                                   ).then_inc(s.loaded, 16)
                sync.dma_start(g.x[:], t.x.rearrange("(b p) f -> p b f", p=P)).then_inc(s.x_loaded, 16)
                sync.wait_ge(s.x_loaded, 16)
                sync.wait_ge(s.kept, 1)
                sync.dma_start(g.offset_dram[:], g.offset[:]).then_inc(s.stored, 16)
                sync.dma_start(g.base_float_dram[:], g.base_float[:]).then_inc(s.stored, 16)
                sync.dma_start(g.half_offset_dram[:], g.half_offset[:]).then_inc(s.stored, 16)
                sync.dma_start(g.half_base_float_dram[:], g.half_base_float[:]).then_inc(s.stored, 16)
                sync.wait_ge(s.stored, 64)

            @block.gpsimd
            def _(pool):
                nc.gpsimd.iota(iota_int[:], [[1, P]], base=0, channel_multiplier=0).then_inc(s.iota, 1)
                nc.gpsimd.iota(lane_int[:], [[0, 1]], base=0, channel_multiplier=1).then_inc(s.iota, 1)

            @block.scalar
            def _(act):
                act.wait_ge(s.loaded, 16 * 13)
                for k in range(hid):
                    if k >= 2:
                        act.wait_ge(s.added, k - 1)
                    nc.scalar.activation(hidden[:, k % 2, :], attribute[:], ACT.Relu,
                                         bias=mlp[:, hid + k:hid + k + 1],
                                         scale=mlp[:, k:k + 1]).then_inc(s.relu, 1)
                act.wait_ge(s.added, hid)
                nc.scalar.activation(g.edge_values[:, :, 1], gate[:], ACT.Sigmoid,
                                     bias=mlp[:, 3 * hid:3 * hid + 1]).then_inc(s.gated, 1)
                act.wait_ge(s.gated, 1)

            @block.tensor
            def _(pe):
                pe.wait_ge(s.kept, 1)
                nc.tensor.matmul(turned[0:1, 0:P], small[:, 0:1], g.identity[:], start=True, stop=True)
                nc.tensor.matmul(turned[0:1, 3 * P:4 * P], small[:, 4:5], g.identity[:], start=True, stop=True)
                nc.tensor.matmul(turned[0:8, P:2 * P], small[:, 1:2].to_broadcast([P, 8]), g.identity[:],
                                 start=True, stop=True)
                nc.tensor.matmul(turned[0:8, 2 * P:3 * P], small[:, 2:3].to_broadcast([P, 8]), g.identity[:],
                                 start=True, stop=True).then_inc(s.turned, 1)

            @block.vector
            def _(dve):
                link = linker(dve, s.own)
                nc.vector.memset(g.source[:, g.tiles:], 0)
                nc.vector.memset(g.source_chunk[:, g.tiles:], 0)
                nc.vector.memset(g.offset[:, g.tiles:], -1.0)
                nc.vector.memset(g.edge_values[:, :, 2], 1.0)
                dve.wait_ge(s.iota, 2)
                nc.vector.tensor_copy(lane[:], lane_int[:])
                link(nc.vector.tensor_copy(g.iota[:], iota_int[:]))
                nc.vector.tensor_scalar(g.identity[:], g.iota[:], lane[:], None, ALU.is_equal)
                nc.vector.tensor_scalar(g.earlier[:], g.iota[:], lane[:], None, ALU.is_lt)
                link(nc.vector.tensor_scalar(small[:, 3:4], lane[:], float(g.blocks * P), None, ALU.add))
                dve.wait_ge(s.loaded, 16 * 13)
                nc.vector.tensor_copy(g.offset[:, 0:g.tiles], dst_int[:])
                nc.vector.tensor_copy(g.base_float[:], base_int[0:1, :])
                nc.vector.tensor_copy(g.half_base_float[:], base_int[0:1, ::HALF])
                nc.vector.tensor_copy(g.half_base[:], base_int[0:1, ::HALF])
                link(nc.vector.tensor_copy(g.source_float[:], g.source[:, 0:g.tiles + HALF]))
                nc.vector.tensor_scalar(g.to_spare[:], g.source_float[:], small[:, 3:4], -1.0,
                                        ALU.subtract, ALU.mult)
                link(nc.vector.tensor_copy(base_all[:], base_int[:]))
                link(nc.vector.tensor_tensor(
                    g.half_offset[:].rearrange("p (n k) -> p n k", k=HALF),
                    g.offset[:, 0:g.tiles].rearrange("p (n k) -> p n k", k=HALF),
                    base_all[:].rearrange("p (n k) -> p n k", k=HALF)[:, :, 0:1].to_broadcast([P, groups, HALF]),
                    ALU.subtract))
                link(nc.vector.tensor_tensor(g.offset[:, 0:g.tiles], g.offset[:, 0:g.tiles], base_all[:], ALU.subtract))
                nc.vector.tensor_copy(g.edge_values[:, :, 0], weight[:])
                link(nc.vector.tensor_tensor(g.keep[:], chunk_dst[:], chunk_before[:], ALU.is_equal))
                link(nc.vector.tensor_scalar(g.reset[:], g.keep[:], 1.0, BIG, ALU.subtract, ALU.mult))
                nc.vector.tensor_reduce(small[:, 0:1], g.offset[:, 0:g.tiles], AXX, ALU.max)
                nc.vector.tensor_reduce(small[:, 4:5], g.half_offset[:], AXX, ALU.max)
                nc.vector.tensor_reduce(small[:, 1:2], g.keep[:], AXX, ALU.min)
                nc.vector.tensor_reduce(small[:, 2:3], g.reset[:], AXX, ALU.min).then_inc(s.kept, 1)
                dve.wait_ge(s.turned, 1)
                nc.vector.tensor_copy(g.keep_row[:], turned[0:8, P:2 * P])
                nc.vector.tensor_copy(g.reset_row[:], turned[0:8, 2 * P:3 * P])
                nc.vector.tensor_reduce(widest[:, 0:1], turned[0:1, 0:P], AXX, ALU.max)
                link(nc.vector.tensor_reduce(widest[:, 1:2], turned[0:1, 3 * P:4 * P], AXX, ALU.max))
                link(nc.vector.tensor_scalar(widest[:], widest[:], 1.0 / P, 0.5 / P - 0.5, ALU.mult, ALU.add))
                nc.vector.tensor_copy(g.last_window[:], widest[:, 0:1])
                nc.vector.tensor_copy(g.half_last_window[:], widest[:, 1:2])
                for k in range(hid):
                    dve.wait_ge(s.relu, k + 1)
                    if k == 0:
                        nc.vector.tensor_scalar(gate[:], hidden[:, 0, :], mlp[:, 2 * hid:2 * hid + 1], None,
                                                ALU.mult).then_inc(s.added, 1)
                    else:
                        dve.wait_ge(s.added, k)
                        nc.vector.scalar_tensor_tensor(
                            gate[:], hidden[:, k % 2, :], mlp[:, 2 * hid + k:2 * hid + k + 1], gate[:],
                            ALU.mult, ALU.add).then_inc(s.added, 1)


def degrees(nc, g, histogram):
    with ExitStack() as stack:
        sbuf, psum = tiles_of(stack, nc)
        running = sbuf("running", [3, g.blocks * P])
        one = sbuf("one", [3, 1])
        counts = sbuf("counts", [P, g.blocks, 2])
        degree = sbuf("degree", [P, g.blocks])
        scratch = sbuf("scratch", [P, g.blocks])
        values = psum("values")[:, 0:3 * g.blocks].rearrange("p (b v) -> p b v", v=3)
        ends = psum("ends")[:, 0:3 * g.blocks].rearrange("p (b v) -> p b v", v=3)
        with phase(nc, "own", "counted", "turned", "rooted", "degree") as (block, s):
            @block.tensor
            def _(pe):
                pe.wait_ge(s.counted, 1)
                for b in range(g.blocks):
                    nc.tensor.matmul(values[:, b, :], histogram[:, b * P:(b + 1) * P],
                                     g.identity[0:3, 0:3], start=True, stop=True)
                    last = nc.tensor.matmul(ends[:, b, :], running[:, b * P:(b + 1) * P],
                                            g.identity[0:3, 0:3], start=True, stop=True)
                last.then_inc(s.turned, 1)

            @block.scalar
            def _(act):
                act.wait_ge(s.degree, 1)
                nc.scalar.activation(g.root_degree[:], degree[:], ACT.Sqrt).then_inc(s.rooted, 1)

            @block.vector
            def _(dve):
                link = linker(dve, s.own)
                link(nc.vector.memset(one[:], 1.0))
                nc.vector.tensor_tensor_scan(running[:], one[:].to_broadcast([3, g.blocks * P]), histogram[:],
                                             0.0, ALU.mult, ALU.add).then_inc(s.counted, 1)
                dve.wait_ge(s.turned, 1)
                nc.vector.tensor_copy(g.weight_sum[:], values[:, :, 0])
                nc.vector.tensor_scalar(degree[:], values[:, :, 1], 1.0, None, ALU.add).then_inc(s.degree, 1)
                nc.vector.tensor_copy(counts[:, :, 0], values[:, :, 2])
                link(nc.vector.tensor_copy(counts[:, :, 1], ends[:, :, 2]))
                link(nc.vector.tensor_scalar(g.nonempty[:], counts[:, :, 0], 0.5, None, ALU.is_gt))
                nc.vector.tensor_scalar(g.empty[:], counts[:, :, 0], 0.5, None, ALU.is_lt)
                link(nc.vector.tensor_tensor(counts[:, :, 0], counts[:, :, 1], counts[:, :, 0], ALU.subtract))
                link(nc.vector.tensor_scalar(counts[:, :, 1], counts[:, :, 1], 1.0, None, ALU.subtract))
                link(nc.vector.tensor_tensor(counts[:, :, 1], counts[:, :, 1], g.nonempty[:], ALU.mult))
                nc.vector.tensor_copy(g.last_edge[:], counts[:, :, 1])
                link(nc.vector.scalar_tensor_tensor(counts[:, :, 0], g.empty[:], float(2 * g.tiles * P),
                                                    counts[:, :, 0], ALU.mult, ALU.add))
                nc.vector.tensor_copy(g.first_edge[:], counts[:, :, 0])
                dve.wait_ge(s.rooted, 1)
                inverse_root(nc, link, degree, g.root_degree, scratch)


def segmented_scan(nc, g, values, out, columns, largest):
    start = -BIG if largest else 0.0
    first, op0, op1 = (g.reset, ALU.add, ALU.max) if largest else (g.keep, ALU.mult, ALU.add)
    row_first = g.reset_row if largest else g.keep_row
    with ExitStack() as stack:
        sbuf, psum = tiles_of(stack, nc)
        ends = sbuf("ends", [P, columns])
        row = sbuf("row", [columns, P + 1])
        carry = sbuf("carry", [P, columns])
        turned = psum("turned")
        with phase(nc, "own", "ended", "turned", "carried", "returned") as (block, s):
            @block.tensor
            def _(pe):
                pe.wait_ge(s.ended, 1)
                nc.tensor.matmul(turned[0:columns, 0:P], ends[:], g.identity[:], start=True,
                                 stop=True).then_inc(s.turned, 1)
                pe.wait_ge(s.carried, 1)
                nc.tensor.matmul(turned[:, P:P + columns], row[:, 0:P], g.identity[0:columns, 0:columns],
                                 start=True, stop=True).then_inc(s.returned, 1)

            @block.vector
            def _(dve):
                link = linker(dve, s.own)
                nc.vector.memset(row[:, 0:1], start)
                for c in range(columns):
                    last = nc.vector.tensor_tensor_scan(out[:, :, c], first[:], values[:, :, c], start, op0, op1)
                link(last)
                nc.vector.tensor_copy(ends[:], out[:, g.tiles - 1, :]).then_inc(s.ended, 1)
                dve.wait_ge(s.turned, 1)
                nc.vector.tensor_tensor_scan(row[:, 1:P + 1], row_first[0:columns, :], turned[0:columns, 0:P],
                                             start, op0, op1).then_inc(s.carried, 1)
                dve.wait_ge(s.returned, 1)
                link(nc.vector.tensor_copy(carry[:], turned[:, P:P + columns]))
                for c in range(columns):
                    nc.vector.tensor_tensor_scan(out[:, :, c], first[:], values[:, :, c], carry[:, c:c + 1], op0, op1)


def gather_logits(nc, g, table, heads, out):
    with ExitStack() as stack:
        sbuf, _ = tiles_of(stack, nc)
        rows = sbuf("rows", [P, RING, heads])
        index = sbuf("index", [P, RING], INT32)
        with phase(nc, "index_ready", "issued", "copied", "gathered0", "gathered1") as (block, s):
            gathered = [s.gathered0, s.gathered1]

            @block.gpsimd
            def _(pool):
                with pool.Fori(0, g.tiles // RING) as i:
                    for k in range(RING):
                        if k % HALF == 0:
                            pool.wait_ge(s.index_ready, i * 2 + (k // HALF + 1))
                            pool.sem_inc(s.issued, 1)
                        nc.gpsimd.indirect_dma_start(
                            rows[:, k, :], None, table,
                            bass.IndirectOffsetOnAxis(ap=index[:, k:k + 1], axis=0),
                        ).then_inc(gathered[k // HALF], 16)

            @block.vector
            def _(dve):
                for half in range(2):
                    nc.vector.tensor_copy(index[:, half * HALF:(half + 1) * HALF],
                                          g.source_chunk[:, half * HALF:(half + 1) * HALF]
                                          ).then_inc(s.index_ready, 1)
                with dve.Fori(0, g.tiles // RING) as i:
                    for half in range(2):
                        at = half * HALF
                        dve.wait_ge(gathered[half], i * (16 * HALF) + 16 * HALF)
                        nc.vector.tensor_copy(out[:, bass.ds(i * RING + at, HALF), :],
                                              rows[:, at:at + HALF, :])
                        nc.vector.tensor_copy(index[:, at:at + HALF],
                                              g.source_chunk[:, bass.ds(i * RING + (RING + at), HALF)]
                                              ).then_inc(s.index_ready, 1)


def store_edges(nc, g, pairs):
    with phase(nc, "stored") as (block, s):
        @block.sync
        def _(sync):
            for dram, tile in pairs:
                sync.dma_start(dram, tile, allow_slow_non_contiguous=True).then_inc(s.stored, 16)
            sync.wait_ge(s.stored, 16 * len(pairs))


def at_last_edges(nc, g, edges, out, heads):
    with phase(nc, "gathered") as (block, s):
        @block.gpsimd
        def _(pool):
            for b in range(g.blocks):
                nc.gpsimd.indirect_dma_start(
                    out[:, b, :], None, edges,
                    bass.IndirectOffsetOnAxis(ap=g.last_edge[:, b:b + 1], axis=0)).then_inc(s.gathered, 16)
            pool.wait_ge(s.gathered, 16 * g.blocks)


def to_edges(nc, g, values, columns, scratch, spread, out):
    with phase(nc, "scattered", "loaded") as (block, s):
        @block.gpsimd
        def _(pool):
            for b in range(g.blocks):
                nc.gpsimd.indirect_dma_start(
                    scratch, bass.IndirectOffsetOnAxis(ap=g.first_edge[:, b:b + 1], axis=0),
                    values[:, b, :], None, bounds_check=g.tiles * P - 1, oob_is_err=False,
                ).then_inc(s.scattered, 16)
            pool.wait_ge(s.scattered, 16 * g.blocks)
            pool.dma_start(spread[:], scratch.rearrange("(p i) v -> p i v", p=P)).then_inc(s.loaded, 16)
            pool.wait_ge(s.loaded, 16)
    segmented_scan(nc, g, spread, out, columns, False)


def attention(nc, g, table, heads, scratch_sums, scratch_pair, scratch_one, scratch_planes):
    both = 2 * heads
    with ExitStack() as stack:
        sbuf, psum = tiles_of(stack, nc)
        logit = sbuf("logit", [P, g.tiles, heads])
        best = sbuf("best", [P, g.tiles, heads])
        spread = sbuf("spread", [P, g.tiles, both])
        pair = sbuf("pair", [P, g.tiles, both])
        node = sbuf("node", [P, g.blocks, heads])
        node_self = sbuf("node_self", [P, g.blocks, heads])
        node_pair = sbuf("node_pair", [P, g.blocks, both])
        node_one = sbuf("node_one", [P, g.blocks, heads])
        mask = g.nonempty[:].unsqueeze(2).to_broadcast([P, g.blocks, heads])
        mask_empty = g.empty[:].unsqueeze(2).to_broadcast([P, g.blocks, heads])
        a_src, a_dst = g.self_logits[:, :, 0:heads], g.self_logits[:, :, heads:both]
        d_node, m_node = node_pair[:, :, 0:heads], node_pair[:, :, heads:both]

        gather_logits(nc, g, table, heads, logit)
        segmented_scan(nc, g, logit, best, heads, True)
        store_edges(nc, g, [(scratch_sums.rearrange("(p i) v -> p i v", p=P), best[:])])
        at_last_edges(nc, g, scratch_sums, node, heads)
        with phase(nc, "own") as (block, s):
            @block.vector
            def _(dve):
                link = linker(dve, s.own)
                link(nc.vector.tensor_tensor(node[:], node[:], mask, ALU.mult))
                link(nc.vector.tensor_tensor(node_self[:], a_src, mask_empty, ALU.mult))
                link(nc.vector.tensor_tensor(node[:], node[:], node_self[:], ALU.add))
                link(nc.vector.tensor_tensor(node[:], node[:], a_src, ALU.max))
                link(nc.vector.tensor_tensor(node[:], node[:], a_dst, ALU.add))
                nc.vector.tensor_copy(d_node, a_dst)
                link(nc.vector.scalar_tensor_tensor(m_node, node[:], 0.2, node[:], ALU.mult, ALU.max))
                link(nc.vector.tensor_tensor(node_self[:], a_src, a_dst, ALU.add))
                link(nc.vector.scalar_tensor_tensor(node_self[:], node_self[:], 0.2, node_self[:], ALU.mult, ALU.max))
                link(nc.vector.tensor_tensor(node_self[:], node_self[:], m_node, ALU.subtract))
        to_edges(nc, g, node_pair, both, scratch_pair, spread, pair)
        with phase(nc, "own", "logits", "exponents") as (block, s):
            @block.vector
            def _(dve):
                link = linker(dve, s.own)
                link(nc.vector.tensor_tensor(logit[:], logit[:], pair[:, :, 0:heads], ALU.add))
                link(nc.vector.scalar_tensor_tensor(logit[:], logit[:], 0.2, logit[:], ALU.mult, ALU.max))
                nc.vector.tensor_tensor(logit[:], logit[:], pair[:, :, heads:both], ALU.subtract
                                        ).then_inc(s.logits, 1)

            @block.scalar
            def _(act):
                nc.scalar.activation(node_self[:], node_self[:], ACT.Exp)
                act.wait_ge(s.logits, 1)
                nc.scalar.activation(logit[:], logit[:], ACT.Exp).then_inc(s.exponents, 1)
        segmented_scan(nc, g, logit, best, heads, False)
        store_edges(nc, g, [(scratch_sums.rearrange("(p i) v -> p i v", p=P), best[:])])
        at_last_edges(nc, g, scratch_sums, node, heads)
        with phase(nc, "own") as (block, s):
            @block.vector
            def _(dve):
                link = linker(dve, s.own)
                link(nc.vector.tensor_tensor(node[:], node[:], mask, ALU.mult))
                link(nc.vector.tensor_tensor(node[:], node[:], node_self[:], ALU.add))
                link(nc.vector.reciprocal(node_one[:], node[:]))
                link(nc.vector.tensor_tensor(g.alpha_self[:, :, 0:heads], node_self[:], node_one[:], ALU.mult))
        to_edges(nc, g, node_one, heads, scratch_one, best, pair[:, :, 0:heads])
        lay_out_weights(nc, g, logit, pair[:, :, 0:heads], spread, heads, scratch_planes)


def lay_out_weights(nc, g, exponents, inverse, spare, heads, planes):
    rows = max(r for r in range(1, P + 1) if g.tiles % r == 0)
    groups = g.tiles // rows
    spare = spare[:].rearrange("p i v -> p (i v)")
    product = spare[:, 0:heads * g.tiles].rearrange("p (h i) -> p h i", h=heads)
    with ExitStack() as stack:
        sbuf, psum = tiles_of(stack, nc)
        by_tile = sbuf("by_tile", [rows, heads, groups, P])
        turned = [psum(f"turned{n}") for n in range(BUFS)]
        with phase(nc, "product", "stored", "loaded", "turned", "copied") as (block, s):
            jobs = [(h, n) for h in range(heads) for n in range(groups)]

            @block.sync
            def _(sync):
                sync.wait_ge(s.product, 1)
                for h in range(heads):
                    sync.dma_start(planes[h].rearrange("(p i) -> p i", p=P), product[:, h, :]).then_inc(s.stored, 16)
                sync.wait_ge(s.stored, 16 * heads)
                for h in range(heads):
                    sync.dma_start(by_tile[:, h, :, :],
                                   planes[h].rearrange("(n r p) -> r n p", r=rows, p=P)).then_inc(s.loaded, 16)

            @block.tensor
            def _(pe):
                pe.wait_ge(s.loaded, 16 * heads)
                for n, (h, k) in enumerate(jobs):
                    if n >= BUFS:
                        pe.wait_ge(s.copied, n - BUFS + 1)
                    nc.tensor.matmul(turned[n % BUFS][:, 0:rows], by_tile[:, h, k, :],
                                     g.identity[0:rows, 0:rows], start=True, stop=True).then_inc(s.turned, 1)

            @block.vector
            def _(dve):
                nc.vector.tensor_tensor(product, exponents[:].rearrange("p i h -> p h i"),
                                        inverse.rearrange("p i h -> p h i"), ALU.mult).then_inc(s.product, 1)
                for n, (h, k) in enumerate(jobs):
                    dve.wait_ge(s.turned, n + 1)
                    nc.vector.tensor_copy(g.alpha[:, h, k * rows:(k + 1) * rows],
                                          turned[n % BUFS][:, 0:rows]).then_inc(s.copied, 1)


def steps(blocks):
    return max(n for n in range(2, 12, 2) if blocks % n == 0)


def combine(nc, g, spec):
    chunks = math.ceil(spec.features / P)
    width = spec.features // chunks
    both = spec.own == "x"
    own_rows = spec.own is not None and not both
    turn = spec.own is not None and spec.finish != "last"
    residual = spec.finish in ("relu", "add", "weight_sum", "last")
    columns = spec.columns
    chain_length = {"relu": 2, "add": 2, "weight_sum": 2, "last": 2, "scale": 1, "logits": 0}[spec.finish]
    body = steps(g.blocks)
    group = body // 2

    def nodes(i, j, count=1):
        return bass.ds(i * (body * P) + j * P, count * P)

    def blk(i, j):
        return bass.ds(i * body + j, 1)

    with ExitStack() as stack:
        sbuf, psum = tiles_of(stack, nc)
        if both:
            support_rows = sbuf("support_rows", [P, 2, group, COPIES, spec.features])
            two_sums = sbuf("two_sums", [P, 2, 2, spec.features])
            support_sum = sbuf("support_sum", [P, 2, spec.features])
            support_bank = [psum(f"support_bank{n}") for n in range(2)]
            x_rows = sbuf("x_rows", [P, 2, spec.features])
        if own_rows:
            rows = sbuf("rows", [P, body, spec.features])
        if spec.heads:
            own_scaled = sbuf("own_scaled", [P, 2, spec.features])
        sums = sbuf("sums", [width, 2, chunks, P])
        left = sbuf("left", [width, 2, chunks, P])
        aggregate_left = sbuf("aggregate_left", [width, 2, chunks, P])
        out = sbuf("out", [P, body, columns])
        turned = [psum(f"turned{n}") for n in range(2)]
        product = [psum(f"product{n}") for n in range(2)]

        def view(tile):
            return tile[0:width, 0:chunks * P].rearrange("p (c n) -> p c n", c=chunks)

        with phase(nc, "own", "issued", "loaded0", "loaded1", "scaled", "copied", "turned", "summed", "left_ready",
                   "pairs_added", "support_summed", "support_turned", "multiplied", "finished", "out_free",
                   "stored0", "stored1") as (block, s):
            loaded, stored = [s.loaded0, s.loaded1], [s.stored0, s.stored1]
            transfers = COPIES if both else 1

            if both or own_rows:
                @block.sync
                def _(sync):
                    with sync.Fori(0, g.blocks // body) as i:
                        for h in range(2):
                            sync.wait_ge(s.finished, i * body + (h + 1) * group)
                            for q in range(transfers):
                                table = spec.support[q] if both else spec.own
                                to = (support_rows[:, h, :, q, :] if both
                                      else rows[:, h * group:(h + 1) * group, :])
                                sync.dma_start(to, table[nodes(i, h * group, group), :]
                                               .rearrange("(b p) f -> p b f", p=P)).then_inc(loaded[h], 16)

            if not residual:
                @block.gpsimd
                def _(pool):
                    pool.sem_inc(s.out_free, body)
                    with pool.Fori(0, g.blocks // body) as i:
                        for h in range(2):
                            pool.wait_ge(s.finished, i * body + (body + (h + 1) * group))
                            pool.dma_start(
                                spec.store[nodes(i, h * group, group), :].rearrange("(b p) f -> p b f", p=P),
                                out[:, h * group:(h + 1) * group, 0:spec.stored_columns]
                            ).then_inc(stored[h], 16)
                        for h in range(2):
                            pool.wait_ge(stored[h], i * 16 + 16)
                            pool.sem_inc(s.out_free, group)

            def wait_loaded(engine, i, j):
                if j % group == 0:
                    engine.wait_ge(loaded[j // group], i * (16 * transfers) + 16 * transfers)

            @block.scalar
            def _(act):
                act.sem_inc(s.left_ready, 2)
                act.sem_inc(s.copied, 2)

                def first_stage(i, j):
                    b = j % 2
                    if both:
                        act.wait_ge(s.turned, i * body + (j + 1))
                        nc.scalar.copy(x_rows[:, b, :], g.x[:, blk(i, j), :].rearrange("p a f -> p (a f)")
                                       ).then_inc(s.scaled, 1)
                    elif not turn:
                        act.wait_ge(s.multiplied, i * body + (j + 1))
                        nc.scalar.copy(aggregate_left[:, b, :, :], g.acc[0:width, 0:chunks, nodes(i, j)]
                                       ).then_inc(s.copied, 1)
                    elif spec.heads:
                        share = spec.features // spec.heads
                        wait_loaded(act, i, j)
                        act.wait_ge(s.turned, i * body + (j + 1))
                        for h in range(spec.heads):
                            part = slice(h * share, (h + 1) * share)
                            last = nc.scalar.activation(
                                own_scaled[:, b, part], rows[:, j, part], ACT.Copy,
                                scale=g.alpha_self[:, blk(i, j), h:h + 1].rearrange("p a b -> p (a b)"))
                        last.then_inc(s.scaled, 1)

                def second_stage(i, j):
                    b = j % 2
                    if both:
                        act.wait_ge(s.turned, i * body + (j + 3))
                        act.wait_ge(s.multiplied, i * body + (j + 1))
                        nc.scalar.copy(left[:, b, :, :], view(turned[b])).then_inc(s.left_ready, 1)
                        act.wait_ge(s.support_turned, i * body + (j + 1))
                        nc.scalar.copy(aggregate_left[:, b, :, :], view(support_bank[b])).then_inc(s.copied, 1)
                    elif turn:
                        act.wait_ge(s.summed, i * body + (j + 3))
                        act.wait_ge(s.multiplied, i * body + (j + 1))
                        for c in range(chunks):
                            bias = spec.feature_bias[:, c:c + 1] if spec.feature_bias is not None else 0.0
                            last = nc.scalar.activation(left[:, b, c, :], sums[:, b, c, :],
                                                        ACT.Relu if spec.rectify else ACT.Identity, bias=bias)
                        last.then_inc(s.left_ready, 1)

                with act.Fori(0, g.blocks // body) as i:
                    first_stage(i, 0)
                    for j in range(body):
                        if j + 1 < body:
                            first_stage(i, j + 1)
                        second_stage(i, j)

            @block.tensor
            def _(pe):
                pe.sem_inc(s.turned, 2)
                pe.sem_inc(s.multiplied, 2)

                def turn_rows(i, j):
                    b = j % 2
                    if not turn:
                        return
                    if spec.heads or both:
                        pe.wait_ge(s.scaled, i * body + (j + 1))
                    else:
                        wait_loaded(pe, i, j)
                    if both:
                        pe.wait_ge(s.left_ready, i * body + (j + 1))
                    else:
                        pe.wait_ge(s.summed, i * body + (j + 1))
                    for c in range(chunks):
                        part = slice(c * width, (c + 1) * width)
                        if both:
                            source = x_rows[:, b, part]
                        else:
                            source = own_scaled[:, b, part] if spec.heads else rows[:, j, part]
                        last = nc.tensor.matmul(turned[b][0:width, c * P:(c + 1) * P], source,
                                                g.identity[:], start=True, stop=True)
                    last.then_inc(s.turned, 1)
                    if both:
                        pe.wait_ge(s.support_summed, i * body + (j + 3))
                        pe.wait_ge(s.copied, i * body + (j + 1))
                        for c in range(chunks):
                            last = nc.tensor.matmul(support_bank[b][:, c * P:(c + 1) * P],
                                                    support_sum[:, b, c * P:(c + 1) * P], g.identity[:],
                                                    start=True, stop=True)
                        last.then_inc(s.support_turned, 1)

                def multiply(i, j):
                    b = j % 2
                    if turn:
                        pe.wait_ge(s.left_ready, i * body + (j + 3))
                    if both or not turn:
                        pe.wait_ge(s.copied, i * body + (j + 3))
                    pe.wait_ge(s.finished, i * body + (body + j - 1))
                    if spec.finish == "last":
                        for c in range(chunks):
                            last = nc.tensor.matmul(product[b][:, c * P:(c + 1) * P],
                                                    aggregate_left[:, b, c, :], g.identity[:],
                                                    start=True, stop=True)
                    else:
                        factors = []
                        if turn:
                            factors += [(left[:, b, c, :], spec.factor[0], c) for c in range(chunks)]
                        if both or not turn:
                            factors += [(aggregate_left[:, b, c, :], spec.factor[-1], c)
                                        for c in range(chunks)]
                        for n, (lhs, matrix, c) in enumerate(factors):
                            last = nc.tensor.matmul(product[b][:, 0:columns], lhs, matrix[:, c, 0:columns],
                                                    start=(n == 0), stop=(n == len(factors) - 1))
                    last.then_inc(s.multiplied, 1)

                with pe.Fori(0, g.blocks // body) as i:
                    turn_rows(i, 0)
                    for j in range(body):
                        if j + 1 < body:
                            turn_rows(i, j + 1)
                        multiply(i, j)

            @block.vector
            def _(dve):
                dve.sem_inc(s.finished, body)
                dve.sem_inc(s.summed, 2)
                dve.sem_inc(s.support_summed, 2)

                def add_own(i, j):
                    b = j % 2
                    if both:
                        wait_loaded(dve, i, j)
                        here = support_rows[:, j // group, j % group, :, :]
                        nc.vector.tensor_tensor(two_sums[:, b, :, :], here[:, 0:2, :], here[:, 2:4, :], ALU.add
                                                ).then_inc(s.pairs_added, 1)
                        dve.wait_ge(s.pairs_added, i * body + (j + 1))
                        dve.wait_ge(s.multiplied, i * body + (j + 1))
                        nc.vector.tensor_tensor(support_sum[:, b, :], two_sums[:, b, 0, :], two_sums[:, b, 1, :],
                                                ALU.add).then_inc(s.support_summed, 1)
                    elif turn:
                        dve.wait_ge(s.turned, i * body + (j + 3))
                        dve.wait_ge(s.left_ready, i * body + (j + 1))
                        nc.vector.tensor_tensor(sums[:, b, :, :], g.acc[0:width, 0:chunks, nodes(i, j)],
                                                view(turned[b]), ALU.add).then_inc(s.summed, 1)

                with dve.Fori(0, g.blocks // body) as i:
                    done = [0]

                    def link(instruction):
                        done[0] += 1
                        instruction.then_inc(s.own, 1)
                        dve.wait_ge(s.own, i * (body * chain_length) + done[0])

                    add_own(i, 0)
                    for j in range(body):
                        if j + 1 < body:
                            add_own(i, j + 1)
                        if spec.finish == "last":
                            wait_loaded(dve, i, j)
                        dve.wait_ge(s.multiplied, i * body + (j + 3))
                        got, to = product[j % 2][:, 0:columns], out[:, j, :]
                        x = g.x[:, blk(i, j), :].rearrange("p a f -> p (a f)")
                        if residual:
                            if spec.finish == "relu":
                                link(nc.vector.tensor_tensor(to, got, spec.bias[:], ALU.add))
                                link(nc.vector.scalar_tensor_tensor(x, to, 0.0, x, ALU.max, ALU.add))
                            elif spec.finish == "add":
                                link(nc.vector.tensor_tensor(to, got, spec.bias[:], ALU.add))
                                link(nc.vector.tensor_tensor(x, x, to, ALU.add))
                            elif spec.finish == "weight_sum":
                                link(nc.vector.scalar_tensor_tensor(to, spec.bias[:], g.weight_sum[:, blk(i, j)],
                                                                    got, ALU.mult, ALU.add))
                                link(nc.vector.tensor_tensor(x, x, to, ALU.add))
                            else:
                                link(nc.vector.tensor_tensor(to, got, rows[:, j, :], ALU.add))
                                link(nc.vector.scalar_tensor_tensor(x, to, g.root_degree[:, blk(i, j)], x,
                                                                    ALU.mult, ALU.add))
                            dve.sem_inc(s.issued, 1)
                            nc.vector.bn_stats(g.stats[:, blk(i, j), :].rearrange("p a v -> p (a v)"), x
                                               ).then_inc(s.finished, 1)
                            continue
                        if j % group == 0:
                            dve.wait_ge(s.out_free, i * body + (j + group))
                        if spec.finish == "scale":
                            link(nc.vector.scalar_tensor_tensor(to, got, g.root_degree[:, blk(i, j)],
                                                                spec.bias[:], ALU.mult, ALU.add))
                            nc.vector.tensor_scalar(to, to, g.root_degree[:, blk(i, j)], None, ALU.mult
                                                    ).then_inc(s.finished, 1)
                        else:
                            n = spec.stored_columns
                            nc.vector.tensor_copy(
                                g.self_logits[:, blk(i, j), 0:columns - n].rearrange("p a v -> p (a v)"), got[:, n:])
                            nc.vector.tensor_copy(to[:, 0:n], got[:, 0:n]).then_inc(s.finished, 1)


def project(nc, g, spec):
    chunks = g.features // P
    columns = spec.columns
    product_of = spec.finish != "norm"
    body = steps(g.blocks)
    group = body // 2

    def nodes(i, j, count=1):
        return bass.ds(i * (body * P) + j * P, count * P)

    def blk(i, j):
        return bass.ds(i * body + j, 1)

    with ExitStack() as stack:
        sbuf, psum = tiles_of(stack, nc)
        if product_of:
            left = sbuf("left", [P, 2, chunks, P])
            normal = sbuf("normal", [P, 2, g.features])
            out = sbuf("out", [P, body, columns])
        mean = sbuf("mean", [P, g.blocks])
        variance = sbuf("variance", [P, g.blocks])
        spread = sbuf("spread", [P, g.blocks])
        root = sbuf("root", [P, g.blocks])
        turned = [psum(f"turned{n}") for n in range(2)]
        product = [psum(f"product{n}") for n in range(2)]
        with phase(nc, "own", "variance_ready", "root_ready", "normed", "kept", "turned", "left_ready",
                   "multiplied", "biased", "finished", "out_free", "stored0", "stored1") as (block, s):
            stored = [s.stored0, s.stored1]

            @block.sync
            def _(sync):
                if not product_of:
                    for n, (dram, tile, b) in enumerate(spec.norm_stores):
                        sync.wait_ge(s.normed, b)
                        sync.dma_start(dram, tile).then_inc(stored[0], 16)
                    sync.wait_ge(stored[0], 16 * len(spec.norm_stores))
                    return
                sync.sem_inc(s.out_free, body)
                with sync.Fori(0, g.blocks // body) as i:
                    for h in range(2):
                        sync.wait_ge(s.finished, i * body + ((h + 1) * group + 2))
                        sync.dma_start(
                            spec.store[nodes(i, h * group, group), :].rearrange("(b p) f -> p b f", p=P),
                            out[:, h * group:(h + 1) * group, 0:spec.stored_columns]).then_inc(stored[h], 16)
                    for h in range(2):
                        sync.wait_ge(stored[h], i * 16 + 16)
                        sync.sem_inc(s.out_free, group)

            @block.scalar
            def _(act):
                act.wait_ge(s.variance_ready, 1)
                nc.scalar.activation(root[:], variance[:], ACT.Sqrt).then_inc(s.root_ready, 1)
                if not product_of:
                    return
                act.sem_inc(s.left_ready, 2)
                act.sem_inc(s.kept, 2)

                def keep(i, j):
                    act.wait_ge(s.normed, i * body + (j + 1))
                    nc.scalar.copy(g.x[:, blk(i, j), :].rearrange("p a f -> p (a f)"), normal[:, j % 2, :]
                                   ).then_inc(s.kept, 1)

                with act.Fori(0, g.blocks // body) as i:
                    keep(i, 0)
                    for j in range(body):
                        if j + 1 < body:
                            keep(i, j + 1)
                        act.wait_ge(s.turned, i * body + (j + 3))
                        act.wait_ge(s.multiplied, i * body + (j + 1))
                        nc.scalar.copy(left[:, j % 2, :, :],
                                       turned[j % 2][:, 0:chunks * P].rearrange("p (c n) -> p c n", c=chunks)
                                       ).then_inc(s.left_ready, 1)

            if product_of:
                @block.tensor
                def _(pe):
                    pe.sem_inc(s.turned, 2)
                    pe.sem_inc(s.multiplied, 2)

                    def turn_rows(i, j):
                        pe.wait_ge(s.normed, i * body + (j + 1))
                        pe.wait_ge(s.left_ready, i * body + (j + 1))
                        for c in range(chunks):
                            last = nc.tensor.matmul(turned[j % 2][:, c * P:(c + 1) * P],
                                                    normal[:, j % 2, c * P:(c + 1) * P],
                                                    g.identity[:], start=True, stop=True)
                        last.then_inc(s.turned, 1)

                    with pe.Fori(0, g.blocks // body) as i:
                        turn_rows(i, 0)
                        for j in range(body):
                            if j + 1 < body:
                                turn_rows(i, j + 1)
                            pe.wait_ge(s.left_ready, i * body + (j + 3))
                            pe.wait_ge(s.finished, i * body + (j + 1))
                            for c in range(chunks):
                                last = nc.tensor.matmul(product[j % 2][:, 0:columns], left[:, j % 2, c, :],
                                                        spec.factor[:, c, 0:columns],
                                                        start=(c == 0), stop=(c == chunks - 1))
                            last.then_inc(s.multiplied, 1)

            @block.vector
            def _(dve):
                link = linker(dve, s.own)
                mean_even, mean_odd = g.stats[:, :, 1], g.stats[:, :, 4]
                link(nc.vector.tensor_tensor(mean[:], mean_even, mean_odd, ALU.add))
                link(nc.vector.tensor_scalar(mean[:], mean[:], 0.5, None, ALU.mult))
                link(nc.vector.tensor_tensor(spread[:], mean_even, mean_odd, ALU.subtract))
                link(nc.vector.scalar_tensor_tensor(spread[:], spread[:], 0.25, spread[:], ALU.mult, ALU.mult))
                link(nc.vector.tensor_tensor(variance[:], g.stats[:, :, 2], g.stats[:, :, 5], ALU.add))
                link(nc.vector.scalar_tensor_tensor(variance[:], variance[:], 1.0 / g.features, spread[:],
                                                    ALU.mult, ALU.add))
                link(nc.vector.tensor_scalar(variance[:], variance[:], 1e-5, None, ALU.add))
                dve.sem_inc(s.variance_ready, 1)
                dve.wait_ge(s.root_ready, 1)
                inverse_root(nc, link, variance, root, spread)
                dve.sem_inc(s.finished, 2)

                def normalise(i, j):
                    x = g.x[:, blk(i, j), :].rearrange("p a f -> p (a f)")
                    if product_of:
                        dve.wait_ge(s.kept, i * body + (j + 1))
                        dve.wait_ge(s.turned, i * body + (j + 1))
                    nc.vector.tensor_scalar(normal[:, j % 2, :] if product_of else x, x, mean[:, blk(i, j)],
                                            root[:, blk(i, j)], ALU.subtract, ALU.mult).then_inc(s.normed, 1)

                with dve.Fori(0, g.blocks // body) as i:
                    normalise(i, 0)
                    for j in range(body):
                        if j + 1 < body:
                            normalise(i, j + 1)
                        if not product_of:
                            continue
                        dve.wait_ge(s.multiplied, i * body + (j + 3))
                        if j % group == 0:
                            dve.wait_ge(s.out_free, i * body + (j + group))
                        got, to = product[j % 2][:, 0:columns], out[:, j, :]
                        if spec.finish == "scale":
                            nc.vector.tensor_tensor(to, got, spec.bias[:], ALU.add).then_inc(s.biased, 1)
                            dve.wait_ge(s.biased, i * body + (j + 1))
                            nc.vector.tensor_scalar(to, to, g.root_degree[:, blk(i, j)], None, ALU.mult
                                                    ).then_inc(s.finished, 1)
                        else:
                            n = spec.stored_columns
                            nc.vector.tensor_copy(
                                g.self_logits[:, blk(i, j), 0:columns - n].rearrange("p a v -> p (a v)"), got[:, n:])
                            nc.vector.tensor_copy(to[:, 0:n], got[:, 0:n]).then_inc(s.finished, 1)


def load(nc, *pairs):
    with phase(nc, "loaded") as (block, s):
        @block.sync
        def _(sync):
            for tile, dram in pairs:
                sync.dma_start(tile, dram, allow_slow_non_contiguous=True).then_inc(s.loaded, 16)
            sync.wait_ge(s.loaded, 16 * len(pairs))


def by_rows(weight):
    return weight.rearrange("(c p) n -> p c n", p=min(P, weight.shape[0]))


def on_all(bias):
    return bias.unsqueeze(0).to_broadcast([P, bias.shape[0]])


def attention_factor(nc, factor, weight, att_src, att_dst, stack):
    heads, share = att_src.shape
    n = heads * share
    sbuf, _ = tiles_of(stack, nc)
    with ExitStack() as inner:
        sbuf, _ = tiles_of(inner, nc)
        att = sbuf("att", [P, 2, n])
        each = sbuf("each", [P, 2, n])
        with phase(nc, "own", "loaded") as (block, s):
            @block.sync
            def _(sync):
                sync.dma_start(factor[:, :, 0:n], by_rows(weight)).then_inc(s.loaded, 16)
                for k, a in enumerate((att_src, att_dst)):
                    sync.dma_start(att[:, k, :], a.rearrange("h c -> (h c)").unsqueeze(0).to_broadcast([P, n])
                                   ).then_inc(s.loaded, 16)

            @block.vector
            def _(dve):
                link = linker(dve, s.own)
                dve.wait_ge(s.loaded, 48)
                for c in range(2):
                    for k in range(2):
                        link(nc.vector.tensor_tensor(each[:, c, :], factor[:, c, 0:n], att[:, k, :], ALU.mult))
                        link(nc.vector.tensor_reduce(factor[:, c, n + k * heads:n + (k + 1) * heads],
                                                     each[:, c, :].rearrange("p (h v) -> p h v", h=heads),
                                                     AXX, ALU.add))


def build_program(nc, t, output):
    nodes, features, edges = t.nodes, t.x.shape[1], t.edges
    tiles, blocks = sizes(nodes, edges)
    g = Graph()
    g.nodes, g.features, g.tiles, g.blocks = nodes, features, tiles, blocks
    padded, slots = blocks * P, tiles * P
    heads, hidden = t.L1_gnn_att_src1.shape

    def dram(name, shape):
        return nc.dram_tensor(name, shape, FP32, kind="Internal").ap()

    g.offset_dram = dram("offset_dram", [P, tiles + 2])
    g.base_float_dram = dram("base_float_dram", [1, tiles])
    g.half_offset_dram = dram("half_offset_dram", [P, tiles])
    g.half_base_float_dram = dram("half_base_float_dram", [1, tiles // HALF])
    g.source_flat, g.x_dram = t.src_flat, t.x
    support = [dram(f"support{n}", [padded + P, features]) for n in range(COPIES)]
    spare = dram("spare", [HALF, 2, P, P])
    rows1, rows2 = dram("gat_rows1", [padded, features]), dram("gat_rows2", [padded, hidden])
    logits1, logits2 = dram("gat_logits1", [padded, heads]), dram("gat_logits2", [padded, 1])
    norm2 = dram("norm2", [padded, features])
    gcn = [dram(f"gcn_rows{n}", [padded, features]) for n in range(3)]
    scratch = {n: dram(f"scratch{n}", [slots, n]) for n in (2 * heads, heads, 2, 1)}
    segment = {n: dram(f"segment{n}", [slots, n]) for n in (heads, 1)}
    planes = dram("planes", [heads, slots])

    with ExitStack() as stack:
        sbuf, _ = tiles_of(stack, nc)
        g.source = sbuf("source", [P, tiles + RING], INT32)
        g.source_chunk = sbuf("source_chunk", [P, tiles + RING], INT32)
        g.offset = sbuf("offset", [P, tiles + 2])
        g.base = sbuf("base", [1, tiles], INT32)
        g.base_float = sbuf("base_float", [1, tiles])
        g.last_window = sbuf("last_window", [1, 1], INT32)
        g.edge_values = sbuf("edge_values", [P, tiles, 3])
        g.half_base = sbuf("half_base", [1, tiles // HALF], INT32)
        g.half_base_float = sbuf("half_base_float", [1, tiles // HALF])
        g.half_last_window = sbuf("half_last_window", [1, 1], INT32)
        g.half_offset = sbuf("half_offset", [P, tiles])
        g.source_float = sbuf("source_float", [P, tiles + HALF])
        g.to_spare = sbuf("to_spare", [P, tiles + HALF])
        g.earlier = sbuf("earlier", [P, P])
        g.keep = sbuf("keep", [P, tiles])
        g.reset = sbuf("reset", [P, tiles])
        g.keep_row = sbuf("keep_row", [8, P])
        g.reset_row = sbuf("reset_row", [8, P])
        g.iota = sbuf("iota", [P, P])
        g.identity = sbuf("identity", [P, P])
        g.x = sbuf("x", [P, blocks, features])
        g.stats = sbuf("stats", [P, blocks, 6])
        g.weight_sum = sbuf("weight_sum", [P, blocks])
        g.root_degree = sbuf("root_degree", [P, blocks])
        g.nonempty = sbuf("nonempty", [P, blocks])
        g.empty = sbuf("empty", [P, blocks])
        g.first_edge = sbuf("first_edge", [P, blocks], INT32)
        g.last_edge = sbuf("last_edge", [P, blocks], INT32)
        g.self_logits = sbuf("self_logits", [P, blocks, 2 * heads])
        g.alpha_self = sbuf("alpha_self", [P, blocks, heads])
        edge_weight = g.edge_values[:, :, 0:1].rearrange("p i a -> p a i")
        gate = g.edge_values[:, :, 1:2].rearrange("p i a -> p a i")

        def scoped():
            inner = ExitStack()
            return inner, tiles_of(inner, nc)[0]

        def spec(**fields):
            base = dict(features=features, own=None, heads=0, factor=None, feature_bias=None, rectify=False,
                        columns=features, bias=None, store=None, stored_columns=features)
            base.update(fields)
            return namedtuple("Spec", list(base))(**base)

        set_up(nc, g, t)
        zero_scratch(nc, g, scratch)

        inner, part = scoped()
        with inner:
            with ExitStack() as first:
                histogram = tiles_of(first, nc)[0]("histogram", [3, padded])
                windows(nc, g, lambda first: scatter_by_source(nc, g, support, spare, histogram, first),
                        (g.half_offset, g.half_base_float, g.half_base, g.half_offset_dram,
                         g.half_base_float_dram, g.half_last_window))
                degrees(nc, g, histogram)
            top, bottom = part("top", [P, 2, features]), part("bottom", [P, 2, features])
            bias = part("bias", [P, features])
            load(nc, (top[:], by_rows(t.L0_gnn_W[0:features, :])), (bottom[:], by_rows(t.L0_gnn_W[features:, :])),
                 (bias[:], on_all(t.L0_gnn_b)))
            combine(nc, g, spec(own="x", support=support, factor=[top, bottom], bias=bias, finish="relu"))
        g.alpha = sbuf("alpha", [P, heads, tiles])

        inner, part = scoped()
        with inner as held:
            factor = part("factor", [P, 2, features + 2 * heads])
            attention_factor(nc, factor, t.L1_gnn_W1, t.L1_gnn_att_src1, t.L1_gnn_att_dst1, held)
            project(nc, g, spec(factor=factor, columns=features + 2 * heads, store=rows1, finish="logits"))
        store_edges(nc, g, [(logits1.rearrange("(b p) h -> p b h", p=P), g.self_logits[:, :, 0:heads])])
        attention(nc, g, logits1, heads, segment[heads], scratch[2 * heads], scratch[heads], planes)
        inner, part = scoped()
        with inner as held:
            g.acc = part("acc", [P, 2, padded])
            aggregate_windows(nc, g, rows1, features, g.alpha, heads)
            factor = part("factor", [P, 2, hidden + 2])
            attention_factor(nc, factor, t.L1_gnn_W2, t.L1_gnn_att_src2, t.L1_gnn_att_dst2, held)
            bias = part("bias", [P, 2])
            load(nc, *((bias[:, c:c + 1], t.L1_gnn_b1[c * P:(c + 1) * P].unsqueeze(1)) for c in range(2)))
            combine(nc, g, spec(own=rows1, heads=heads, factor=[factor], feature_bias=bias, rectify=True,
                                columns=hidden + 2, store=rows2, stored_columns=hidden, finish="logits"))

        store_edges(nc, g, [(logits2.rearrange("(b p) h -> p b h", p=P), g.self_logits[:, :, 0:1])])
        attention(nc, g, logits2, 1, segment[1], scratch[2], scratch[1], planes)
        inner, part = scoped()
        with inner:
            g.acc = part("acc", [P, 2, padded])
            aggregate_windows(nc, g, rows2, hidden, g.alpha, 1)
            factor = part("factor", [hidden, 1, features])
            feature_bias, bias = part("feature_bias", [hidden, 1]), part("bias", [P, features])
            load(nc, (factor[:], by_rows(t.L1_gnn_Wf)), (feature_bias[:], t.L1_gnn_b2.unsqueeze(1)),
                 (bias[:], on_all(t.L1_gnn_bf)))
            combine(nc, g, spec(own=rows2, features=hidden, heads=1, factor=[factor], feature_bias=feature_bias,
                                bias=bias, finish="add"))
        norm_store = [(norm2.rearrange("(b p) f -> p b f", p=P)[:, b:min(b + 10, blocks), :],
                       g.x[:, b:min(b + 10, blocks), :], min(b + 10, blocks)) for b in range(0, blocks, 10)]
        project(nc, g, spec(finish="norm", norm_stores=norm_store))

        inner, part = scoped()
        with inner:
            g.acc = part("acc", [P, 2, padded])
            aggregate_windows(nc, g, norm2, features, edge_weight, 1)
            factor, bias = part("factor", [P, 2, features]), part("bias", [P, features])
            load(nc, (factor[:], by_rows(t.L2_gnn_weight)), (bias[:], on_all(t.L2_gnn_bias)))
            combine(nc, g, spec(factor=[factor], bias=bias, finish="weight_sum"))

        inner, part = scoped()
        with inner:
            factor, bias = part("factor", [P, 2, features]), part("bias", [P, features])
            g.acc = part("acc", [P, 2, padded])
            load(nc, (factor[:], by_rows(t.L3_gnn_W1)), (bias[:], on_all(t.L3_gnn_b1)))
            project(nc, g, spec(factor=factor, bias=bias, store=gcn[0], finish="scale"))
            for n, (w, b) in enumerate(((t.L3_gnn_W2, t.L3_gnn_b2), (t.L3_gnn_W3, t.L3_gnn_b3))):
                aggregate_windows(nc, g, gcn[n], features, gate, 1)
                load(nc, (factor[:], by_rows(w)), (bias[:], on_all(b)))
                combine(nc, g, spec(own=gcn[n], factor=[factor], bias=bias, rectify=True, store=gcn[n + 1],
                                    finish="scale"))
            aggregate_windows(nc, g, gcn[2], features, gate, 1)
            combine(nc, g, spec(own=gcn[2], finish="last"))
        full, rest = nodes // P, nodes % P
        out_stores = [(output[b * P:min(b + 8, full) * P, :].rearrange("(b p) f -> p b f", p=P),
                       g.x[:, b:min(b + 8, full), :], min(b + 8, full)) for b in range(0, full, 8)]
        if rest:
            out_stores.append((output[full * P:nodes, :], g.x[0:rest, full, :], full + 1))
        project(nc, g, spec(finish="norm", norm_stores=out_stores))


def zero_scratch(nc, g, scratch):
    with ExitStack() as stack:
        sbuf, _ = tiles_of(stack, nc)
        most = max(scratch)
        zeros = sbuf("zeros", [P, g.tiles * most])
        with phase(nc, "zeroed", "stored") as (block, s):
            @block.vector
            def _(dve):
                nc.vector.memset(zeros[:], 0.0).then_inc(s.zeroed, 1)

            @block.sync
            def _(sync):
                sync.wait_ge(s.zeroed, 1)
                for n, dram in scratch.items():
                    sync.dma_start(dram.rearrange("(p i) v -> p (i v)", p=P), zeros[:, 0:g.tiles * n]
                                   ).then_inc(s.stored, 16)
                sync.wait_ge(s.stored, 16 * len(scratch))


_PLAIN = ["L0_gnn_W", "L0_gnn_b", "L1_gnn_W1", "L1_gnn_att_src1", "L1_gnn_att_dst1", "L1_gnn_b1",
          "L1_gnn_W2", "L1_gnn_att_src2", "L1_gnn_att_dst2", "L1_gnn_b2", "L1_gnn_Wf", "L1_gnn_bf",
          "L2_gnn_weight", "L2_gnn_bias", "L3_gnn_W1", "L3_gnn_b1", "L3_gnn_W2", "L3_gnn_b2", "L3_gnn_W3",
          "L3_gnn_b3", "L3_gnn_mw1", "L3_gnn_mb1", "L3_gnn_mw2", "L3_gnn_mb2"]


def lay_out(inputs):
    nodes, edges = inputs["x"].shape[0], inputs["src"].shape[0]
    tiles, blocks = sizes(nodes, edges)

    def pad(a, value, front=0):
        a = np.asarray(a).reshape(-1)
        whole = np.full(tiles * P + front, value, a.dtype)
        whole[front:front + edges] = a
        return whole[:tiles * P]

    def by_tile(a):
        return np.ascontiguousarray(a.reshape(tiles, P).T)

    src, dst = pad(inputs["src"], 0), pad(inputs["dst"], nodes)
    before = np.concatenate([np.full(1, -1, dst.dtype), dst[:-1]])
    arrays = {n: np.ascontiguousarray(inputs[n]) for n in _PLAIN}
    x = np.zeros((blocks * P, inputs["x"].shape[1]), np.float32)
    x[:nodes] = inputs["x"]
    arrays.update(x=x, src_flat=src.reshape(1, -1), src_tile=by_tile(src), src_chunk=src.reshape(P, tiles), dst_tile=by_tile(dst),
                  dst_chunk=dst.reshape(P, tiles), before_chunk=before.reshape(P, tiles),
                  weight_tile=by_tile(pad(inputs["edge_weight"], 0)),
                  attr_tile=by_tile(pad(inputs["edge_weight1"], 0)))
    return arrays


def kernel(**inputs):
    import concourse.bacc as bacc
    from concourse.bass_utils import run_bass_kernel_spmd

    arrays = lay_out(inputs)
    nc = bacc.Bacc("TRN2", target_bir_lowering=False, num_devices=1)
    t = {n: nc.dram_tensor(f"in_{n}", a.shape, mybir.dt.from_np(a.dtype), kind="ExternalInput").ap()
         for n, a in arrays.items()}
    t.update(nodes=inputs["x"].shape[0], edges=inputs["src"].shape[0])
    output = nc.dram_tensor("out", inputs["x"].shape, FP32, kind="ExternalOutput").ap()
    build_program(nc, namedtuple("Tensors", list(t))(**t), output)
    result = run_bass_kernel_spmd(nc, [{f"in_{n}": a for n, a in arrays.items()}], core_ids=[0])
    return result.results[0]["out"]
```

```python
import math
from collections import namedtuple
from contextlib import ExitStack, contextmanager

import numpy as np
import concourse.bass as bass
from concourse import mybir

P = 128
RING = 16
HALF = RING // 2
BUFS = 4
BATCH = 4
AHEAD = 1
COPIES = 4
BIG = 1e30
WIDEST = 60.0

FP32 = mybir.dt.float32
INT32 = mybir.dt.int32
ALU = mybir.AluOpType
ACT = mybir.ActivationFunctionType
AXX = mybir.AxisListType.X
ENGINES = mybir.ALL_ENGINES


def sizes(nodes, edges):
    tiles = math.ceil(edges / P / RING) * RING
    blocks = 2 * math.ceil((nodes + P) / P / 2)
    return tiles, blocks


class Graph:
    pass


@contextmanager
def phase(nc, *names):
    sems = {n: nc.alloc_semaphore(name=f"{n}_{nc.next_id()}") for n in names}
    with nc.Block() as block:
        yield block, namedtuple("Semaphores", list(sems))(**sems)
    nc.clear_and_free_semaphores(list(sems.values()))
    nc.all_engine_barrier(sem_only=True)


@contextmanager
def entered_if(nc, flag):
    value = nc.values_load(flag[0:1, 0:1], engines=ENGINES, min_val=0, max_val=1,
                           skip_runtime_bounds_check_because="0 or 1")
    with nc.If(value > 0):
        with nc.Fori(0, value):
            yield


def tiles_of(stack, nc):
    def sbuf(name, shape, dtype=FP32):
        return stack.enter_context(nc.sbuf_tensor(f"{name}_{nc.next_id()}", shape, dtype))

    def psum(name, shape=(P, 512), dtype=FP32):
        return stack.enter_context(nc.psum_tensor(f"{name}_{nc.next_id()}", list(shape), dtype))

    return sbuf, psum


def aggregate(nc, g, table, features, weights, heads, first_pass, softmax=False):
    chunks = math.ceil(features / P)
    width = features // chunks
    share = features // heads
    with ExitStack() as stack:
        sbuf, psum = tiles_of(stack, nc)
        rows = sbuf("rows", [P, RING, table.shape[1]])
        scaled_rows = sbuf("scaled_rows", [P, BUFS, features])
        if softmax:
            batches = RING // BATCH
            exponent = sbuf("exponent", [P, batches, BATCH, heads])
            bound = sbuf("bound", [P, BATCH, heads])
            edge_weight = sbuf("edge_weight", [P, batches, BATCH, heads])
        onehots = sbuf("onehots", [P, BUFS, P])
        index = sbuf("index", [P, RING], INT32)
        sums = [psum(f"sums{n}") for n in range(BUFS)]
        gathered_names = [f"gathered{k}" for k in range(RING)]
        with phase(nc, "index_ready", "issued", "scaled", "onehot_ready", "summed", "added", "own",
                   "exponent_ready", "weight_ready", *gathered_names) as (block, s):
            gathered = s[-RING:]

            @block.gpsimd
            def _(pool):
                def gather(i, k):
                    if k % HALF == 0:
                        pool.wait_ge(s.index_ready, i * 2 + (k // HALF + 1))
                    pool.wait_ge(s.scaled, i * RING + (k + 1))
                    pool.sem_inc(s.issued, 1)
                    nc.gpsimd.indirect_dma_start(
                        rows[:, k, :], None, table,
                        bass.IndirectOffsetOnAxis(ap=index[:, k:k + 1], axis=0),
                    ).then_inc(gathered[k], 16)

                with pool.Fori(0, g.tiles // RING) as i:
                    for k in range(RING):
                        gather(i, k)
                if softmax:
                    for k in range(BATCH):
                        gather(g.tiles // RING, k)

            @block.scalar
            def _(act):
                act.sem_inc(s.scaled, RING)
                for half in range(2):
                    nc.scalar.copy(index[:, half * HALF:(half + 1) * HALF],
                                   g.source[:, half * HALF:(half + 1) * HALF]
                                   ).then_inc(s.index_ready, 1)

                def exponentials(batch, before):
                    act.wait_ge(s.exponent_ready, before + 1)
                    nc.scalar.activation(edge_weight[:, batch, :, :], exponent[:, batch, :, :], ACT.Exp
                                         ).then_inc(s.weight_ready, 1)

                if softmax:
                    exponentials(0, 0)
                with act.Fori(0, g.tiles // RING) as i:
                    for k in range(RING):
                        if softmax:
                            if k % BATCH == 0:
                                act.wait_ge(s.weight_ready, i * batches + (k // BATCH + 1))
                        else:
                            act.wait_ge(gathered[k], i * 16 + 16)
                        act.wait_ge(s.summed, i * RING + (k + 1))
                        for h in range(heads):
                            part = slice(h * share, (h + 1) * share)
                            weight = (edge_weight[:, k // BATCH, k % BATCH, h:h + 1] if softmax
                                      else weights[:, h, bass.ds(i * RING + k, 1)])
                            last = nc.scalar.activation(scaled_rows[:, k % BUFS, part], rows[:, k, part],
                                                        ACT.Copy, scale=weight)
                        last.then_inc(s.scaled, 1)
                        if softmax and k % BATCH == BATCH - 1:
                            batch = k // BATCH + 1
                            exponentials(batch % batches, i * batches + batch)
                        if k % HALF == HALF - 1:
                            half = k // HALF * HALF
                            nc.scalar.copy(index[:, half:half + HALF],
                                           g.source[:, bass.ds(i * RING + (RING + half), HALF)]
                                           ).then_inc(s.index_ready, 1)

            @block.tensor
            def _(pe):
                pe.sem_inc(s.summed, BUFS)
                with pe.Fori(0, g.tiles // RING) as i:
                    for k in range(RING):
                        pe.wait_ge(s.scaled, i * RING + (RING + k + 1))
                        pe.wait_ge(s.onehot_ready, i * RING + (k + 1))
                        pe.wait_ge(s.added, i * RING + (k + 1))
                        b = k % BUFS
                        for c in range(chunks):
                            last = nc.tensor.matmul(
                                sums[b][0:width, c * P:(c + 1) * P],
                                scaled_rows[:, b, c * width:(c + 1) * width], onehots[:, b, :],
                                start=True, stop=True)
                        if softmax:
                            last = nc.tensor.matmul(
                                sums[b][0:heads, chunks * P:(chunks + 1) * P],
                                edge_weight[:, k // BATCH, k % BATCH, :], onehots[:, b, :], start=True, stop=True)
                        last.then_inc(s.summed, 1)

            @block.vector
            def _(dve):
                def onehot(slot, column):
                    nc.vector.tensor_scalar(onehots[:, slot, :], g.iota[:], column, None,
                                            ALU.is_equal).then_inc(s.onehot_ready, 1)

                def exponents(batch, tile, before, use):
                    slots = slice(batch * BATCH, (batch + 1) * BATCH)
                    for k in range(slots.start, slots.stop):
                        dve.wait_ge(gathered[k], use)
                    d = weights[:, 0:heads, bass.ds(tile, BATCH)].rearrange("p h i -> p i h")
                    to, rest = exponent[:, batch, :, :], bound[:]
                    top = g.top[:, 0:heads].unsqueeze(1).to_broadcast([P, BATCH, heads])
                    nc.vector.tensor_tensor(rest, d, top, ALU.add)
                    nc.vector.tensor_tensor(to, rows[:, slots, features:features + heads], d, ALU.add
                                            ).then_inc(s.own, 1)
                    dve.wait_ge(s.own, before * 2 + 1)
                    nc.vector.scalar_tensor_tensor(rest, rest, 0.2, rest, ALU.mult, ALU.max)
                    nc.vector.scalar_tensor_tensor(to, to, 0.2, to, ALU.mult, ALU.max).then_inc(s.own, 1)
                    dve.wait_ge(s.own, before * 2 + 2)
                    nc.vector.tensor_tensor(to, to, rest, ALU.subtract).then_inc(s.exponent_ready, 1)

                if first_pass:
                    if softmax:
                        nc.vector.memset(g.z, 0.0)
                    nc.vector.memset(g.acc[0:width, 0:chunks, :], 0.0).then_inc(s.added, BUFS)
                else:
                    dve.sem_inc(s.added, BUFS)
                for k in range(2):
                    onehot(k, g.offset[:, k:k + 1])
                if softmax:
                    exponents(0, 0, 0, 16)
                with dve.Fori(0, g.tiles // RING) as i:
                    for k in range(RING):
                        if k % HALF == 0:
                            _, bases = nc.values_load_multi_w_load_instructions(
                                g.base[0:1, bass.ds(i * RING + k, HALF)],
                                engines=[mybir.EngineType.DVE], min_val=0,
                                max_val=(g.blocks - 1) * P,
                                skip_runtime_bounds_check_because="a destination, or clamped")
                            bases = list(bases)
                        onehot((k + 2) % BUFS, g.offset[:, bass.ds(i * RING + (k + 2), 1)])
                        if softmax and k % BATCH == AHEAD:
                            batch = k // BATCH + 1
                            exponents(batch % batches, i * RING + batch * BATCH, i * batches + batch,
                                      i * 16 + 16 * (batch // batches + 1))
                        window = bass.ds(bases[k % HALF], P)
                        dve.wait_ge(s.summed, i * RING + (BUFS + k + 1))
                        dve.wait_ge(s.added, i * RING + (BUFS + k))
                        last = nc.vector.tensor_tensor(
                            g.acc[0:width, 0:chunks, window], g.acc[0:width, 0:chunks, window],
                            sums[k % BUFS][0:width, 0:chunks * P].rearrange("p (c n) -> p c n", c=chunks),
                            ALU.add)
                        if softmax:
                            last = nc.vector.tensor_tensor(
                                g.z[:, window], g.z[:, window],
                                sums[k % BUFS][0:heads, chunks * P:(chunks + 1) * P], ALU.add)
                        last.then_inc(s.added, 1)


def scatter_by_source(nc, g, support, spare, histogram, first_pass):
    with ExitStack() as stack:
        sbuf, psum = tiles_of(stack, nc)
        parts = 2 * HALF // COPIES
        zeros = sbuf("zeros", [P, (g.blocks + 1) * g.features // parts])
        x_window = sbuf("x_window", [P, 2, g.features])
        source_row = sbuf("source_row", [P, 2, HALF, P], INT32)
        values = sbuf("values", [P, 2, HALF, 3])
        onehots = sbuf("onehots", [P, BUFS, P])
        same_source = sbuf("same_source", [P, BUFS, P])
        scrap = sbuf("scrap", [P, HALF, P])
        repeats = sbuf("repeats", [P, 2, HALF])
        moved = sbuf("moved", [P, 2, HALF])
        index = sbuf("index", [P, 2, HALF], INT32)
        cross = sbuf("cross", [P, BUFS, P])
        rows = sbuf("rows", [P, HALF, g.features])
        cross_bank = [psum(f"cross_bank{n}") for n in range(2)]
        rows_bank = [psum(f"rows_bank{n}") for n in range(2)]
        counts_bank = [psum(f"counts_bank{n}") for n in range(2)]
        names = [f"scattered{k}" for k in range(HALF)]
        with phase(nc, "zeroed", "x_loaded0", "x_loaded1", "row_loaded0", "row_loaded1", "own", "index_ready",
                   "issued", "matrices", "crossed", "cross_copied", "multiplied", "rows_ready", "counted",
                   "values_ready", *names) as (block, s):
            scattered = s[-HALF:]
            x_loaded, row_loaded = [s.x_loaded0, s.x_loaded1], [s.row_loaded0, s.row_loaded1]

            @block.gpsimd
            def _(pool):
                pool.wait_ge(s.zeroed, 1)
                for slot in range(HALF):
                    for part in range(2):
                        if first_pass:
                            flat = support[slot % COPIES].rearrange("n f -> (n f)")
                            size = flat.shape[0] // parts
                            at = (2 * (slot // COPIES) + part) * size
                            target = flat[at:at + size].rearrange("(p z) -> p z", p=P)
                            pool.dma_start(target, zeros[:]).then_inc(scattered[slot], 16)
                        else:
                            pool.dma_start(spare[slot, part], zeros[:, 0:P]).then_inc(scattered[slot], 16)
                for slot in range(HALF):
                    pool.wait_ge(scattered[slot], 32)
                with pool.Fori(0, g.tiles // RING) as i:
                    for k in range(RING):
                        if k % HALF == 0:
                            pool.wait_ge(s.index_ready, i * 2 + (k // HALF + 1))
                        pool.wait_ge(s.rows_ready, i * RING + (k + 3))
                        before = (k - COPIES) % HALF
                        uses = (k - COPIES) // HALF + 1
                        pool.wait_ge(scattered[before], i * 32 + 16 * (uses + 2))
                        pool.sem_inc(s.issued, 1)
                        nc.gpsimd.indirect_dma_start(
                            support[k % COPIES],
                            bass.IndirectOffsetOnAxis(ap=index[:, k // HALF, k % HALF:k % HALF + 1], axis=0),
                            rows[:, k % HALF, :], None, compute_op=ALU.add,
                        ).then_inc(scattered[k % HALF], 16)
                for slot in range(HALF):
                    pool.wait_ge(scattered[slot], 16 * (g.tiles // HALF + 2))
                pool.wait_ge(s.index_ready, g.tiles // HALF + 1)

            @block.sync
            def _(sync):
                with sync.Fori(0, g.tiles // RING) as i:
                    for h in range(2):
                        base = sync.value_load(g.half_base[0:1, bass.ds(i * 2 + h, 1)], min_val=0,
                                               max_val=(g.blocks - 1) * P)
                        sync.wait_ge(s.multiplied, i * RING + HALF * (h + 1))
                        sync.dma_start(x_window[:, h, :], g.x_dram[bass.ds(base, P), :]).then_inc(x_loaded[h], 16)
                        sync.wait_ge(s.matrices, i * RING + HALF * (h + 1))
                        sync.dma_start(
                            source_row[:, h, :, :].rearrange("p k e -> p (k e)"),
                            g.source_flat[0:1, bass.ds((i * 2 + h) * (HALF * P), HALF * P)]
                            .to_broadcast([P, HALF * P])).then_inc(row_loaded[h], 16)
                sync.wait_ge(s.matrices, g.tiles + HALF)
                sync.dma_start(source_row[:, 0, :, :].rearrange("p k e -> p (k e)"),
                               g.source_flat[0:1, 0:HALF * P].to_broadcast([P, HALF * P])
                               ).then_inc(row_loaded[0], 16)

            @block.scalar
            def _(act):
                act.sem_inc(s.cross_copied, 2)
                act.sem_inc(s.rows_ready, 2)

                def copy_rows(i, k):
                    act.wait_ge(s.multiplied, i * RING + (RING + k + 1))
                    act.wait_ge(scattered[k % HALF], i * 32 + 16 * (k // HALF + 2))
                    nc.scalar.copy(rows[:, k % HALF, :], rows_bank[k % 2][:, 0:g.features]).then_inc(s.rows_ready, 1)

                with act.Fori(0, g.tiles // RING) as i:
                    for k in range(RING):
                        if k % HALF == 0:
                            nc.scalar.copy(values[:, k // HALF, :, :],
                                           g.edge_values[:, bass.ds(i * RING + k, HALF), :]
                                           ).then_inc(s.values_ready, 1)
                        act.wait_ge(s.crossed, i * RING + (BUFS + k + 1))
                        nc.scalar.copy(cross[:, k % BUFS, :], cross_bank[k % 2][:, 0:P]).then_inc(s.cross_copied, 1)
                        if k > 0:
                            copy_rows(i, k - 1)
                    copy_rows(i, RING - 1)

            @block.tensor
            def _(pe):
                pe.sem_inc(s.crossed, BUFS)
                pe.sem_inc(s.multiplied, RING)

                def multiply(i, k):
                    if k % HALF == 0:
                        pe.wait_ge(x_loaded[k // HALF], i * 16 + 16)
                    pe.wait_ge(s.cross_copied, i * RING + (k + 3))
                    pe.wait_ge(s.rows_ready, i * RING + (k + 1))
                    nc.tensor.matmul(rows_bank[k % 2][:, 0:g.features], cross[:, k % BUFS, :],
                                     x_window[:, k // HALF, :], start=True, stop=True).then_inc(s.multiplied, 1)

                with pe.Fori(0, g.tiles // RING) as i:
                    for k in range(RING):
                        b = k % BUFS
                        pe.wait_ge(s.matrices, i * RING + (RING + k + 1))
                        pe.wait_ge(s.cross_copied, i * RING + (k + 1))
                        nc.tensor.matmul(cross_bank[k % 2][:, 0:P], onehots[:, b, :], same_source[:, b, :],
                                         start=True, stop=True)
                        if k % HALF == 0:
                            pe.wait_ge(s.values_ready, i * 2 + (k // HALF + 1))
                            pe.wait_ge(s.counted, i * 2 + (k // HALF + 1))
                        nc.tensor.matmul(counts_bank[k // HALF][0:3, 0:P], values[:, k // HALF, k % HALF, :],
                                         onehots[:, b, :], start=(k % HALF == 0), stop=(k % HALF == HALF - 1)
                                         ).then_inc(s.crossed, 1)
                        if k > 0:
                            multiply(i, k - 1)
                    multiply(i, RING - 1)

            @block.vector
            def _(dve):
                nc.vector.memset(zeros[:], 0.0).then_inc(s.zeroed, 1)
                if first_pass:
                    nc.vector.memset(histogram[:], 0.0).then_inc(s.counted, 2)
                else:
                    dve.sem_inc(s.counted, 2)
                dve.sem_inc(s.matrices, RING)
                for slot in range(HALF):
                    dve.wait_ge(scattered[slot], 32)

                def index_half(i, h, ahead):
                    dve.wait_ge(row_loaded[h], i * 16 + 16 * (ahead + 1))
                    for k in range(HALF):
                        last = nc.vector.scalar_tensor_tensor(
                            scrap[:, k, :], source_row[:, h, k, :],
                            g.source_float[:, bass.ds(i * RING + (ahead * RING + h * HALF + k), 1)], g.earlier[:],
                            ALU.is_equal, ALU.mult, accum_out=repeats[:, h, k:k + 1])
                    last.then_inc(s.own, 1)
                    halves = 2 * ahead + h
                    dve.wait_ge(s.own, i * 4 + (2 * halves + 1))
                    here = bass.ds(i * RING + halves * HALF, HALF)
                    nc.vector.scalar_tensor_tensor(moved[:, h, :], repeats[:, h, :], 0.5, g.to_spare[:, here],
                                                   ALU.is_gt, ALU.mult).then_inc(s.own, 1)
                    dve.wait_ge(s.own, i * 4 + (2 * halves + 2))
                    for slot in range(HALF):
                        dve.wait_ge(scattered[slot], i * 32 + 16 * (halves + 1))
                    nc.vector.tensor_tensor(index[:, h, :], moved[:, h, :], g.source_float[:, here],
                                            ALU.add).then_inc(s.index_ready, 1)

                index_half(0, 0, 0)
                with dve.Fori(0, g.tiles // RING) as i:
                    for h in range(2):
                        base = dve.value_load(g.half_base[0:1, bass.ds(i * 2 + h, 1)], min_val=0,
                                              max_val=(g.blocks - 1) * P)
                        for k in range(HALF):
                            b, tile = k % BUFS, bass.ds(i * RING + (h * HALF + k), 1)
                            dve.wait_ge(s.crossed, i * RING + (h * HALF + k + 1))
                            nc.vector.tensor_scalar(onehots[:, b, :], g.iota[:], g.half_offset[:, tile], None,
                                                    ALU.is_equal)
                            nc.vector.tensor_scalar(same_source[:, b, :], source_row[:, h, k, :],
                                                    g.source_float[:, tile],
                                                    g.edge_values[:, tile, 0:1].rearrange("p a v -> p (a v)"),
                                                    ALU.is_equal, ALU.mult).then_inc(s.matrices, 1)
                        index_half(i, 1 - h, h)
                        window = bass.ds(base, P)
                        dve.wait_ge(s.crossed, i * RING + (BUFS + HALF * (h + 1)))
                        dve.wait_ge(s.counted, i * 2 + (h + 2))
                        nc.vector.tensor_tensor(histogram[:, window], histogram[:, window],
                                                counts_bank[h][0:3, 0:P], ALU.add).then_inc(s.counted, 1)


def windows(nc, g, one_pass, tables):
    one_pass(True)
    offset, base_float, base, offset_dram, base_float_dram, last_window = tables
    wide = nc.values_load(last_window[0:1, 0:1], engines=ENGINES, min_val=0, max_val=g.blocks - 1,
                          skip_runtime_bounds_check_because="destinations are below blocks * 128")
    with nc.If(wide > 0):
        with nc.Fori(1, wide + 1):
            with phase(nc, "moved") as (block, s):
                @block.vector
                def _(dve):
                    nc.vector.tensor_scalar(offset[:], offset[:], float(P), None, ALU.subtract)
                    nc.vector.tensor_scalar(base_float[:], base_float[:], float(P),
                                            float((g.blocks - 1) * P), ALU.add, ALU.min).then_inc(s.moved, 1)
                    dve.wait_ge(s.moved, 1)
                    nc.vector.tensor_copy(base[:], base_float[:])
            one_pass(False)
        load(nc, (offset[:], offset_dram[:]), (base_float[:], base_float_dram[:]))
        with phase(nc) as (block, s):
            @block.vector
            def _(dve):
                nc.vector.tensor_copy(base[:], base_float[:])


def aggregate_windows(nc, g, table, features, weights, heads, softmax=False):
    windows(nc, g, lambda first: aggregate(nc, g, table, features, weights, heads, first, softmax),
            (g.offset, g.base_float, g.base, g.offset_dram, g.base_float_dram, g.last_window))


def linker(engine, sem):
    count = [0]

    def link(instruction):
        count[0] += 1
        instruction.then_inc(sem, 1)
        engine.wait_ge(sem, count[0])

    link.count = count
    return link


def inverse_root(nc, link, value, root, scratch):
    link(nc.vector.reciprocal(root[:], root[:]))
    link(nc.vector.tensor_tensor(scratch[:], root[:], root[:], ALU.mult))
    link(nc.vector.tensor_tensor(scratch[:], scratch[:], value[:], ALU.mult))
    link(nc.vector.tensor_scalar(scratch[:], scratch[:], -0.5, 1.5, ALU.mult, ALU.add))
    link(nc.vector.tensor_tensor(root[:], root[:], scratch[:], ALU.mult))


def set_up(nc, g, t):
    with ExitStack() as stack:
        sbuf, psum = tiles_of(stack, nc)
        iota_int = sbuf("iota_int", [P, P], INT32)
        lane_int = sbuf("lane_int", [P, 1], INT32)
        lane = sbuf("lane", [P, 1])
        dst_int = sbuf("dst_int", [P, g.tiles], INT32)
        base_int = sbuf("base_int", [P, g.tiles], INT32)
        base_all = sbuf("base_all", [P, g.tiles])
        chunk_dst = sbuf("chunk_dst", [P, g.tiles], INT32)
        chunk_before = sbuf("chunk_before", [P, g.tiles], INT32)
        attribute = sbuf("attribute", [P, g.tiles])
        weight = sbuf("weight", [P, g.tiles])
        hidden = sbuf("hidden", [P, 2, g.tiles])
        gate = sbuf("gate", [P, g.tiles])
        mlp = sbuf("mlp", [P, 25])
        widest = sbuf("widest", [1, 2])
        small = sbuf("small", [P, 5])
        turned = psum("turned")
        groups = g.tiles // HALF
        hid = t.L3_gnn_mw2.shape[0]
        with phase(nc, "loaded", "x_loaded", "iota", "own", "relu", "added", "gated", "kept",
                   "turned", "wide", "stored") as (block, s):
            @block.sync
            def _(sync):
                for out, dram in ((g.source[:, 0:g.tiles], t.src_tile),
                                  (g.source_chunk[:, 0:g.tiles], t.src_chunk),
                                  (dst_int[:], t.dst_tile),
                                  (base_int[:], t.dst_tile[0:1, :].to_broadcast([P, g.tiles])),
                                  (g.base[:], t.dst_tile[0:1, :]), (chunk_dst[:], t.dst_chunk),
                                  (chunk_before[:], t.before_chunk), (attribute[:], t.attr_tile),
                                  (weight[:], t.weight_tile)):
                    sync.dma_start(out, dram).then_inc(s.loaded, 16)
                for at, param in ((0, t.L3_gnn_mw1), (hid, t.L3_gnn_mb1), (2 * hid, t.L3_gnn_mw2),
                                  (3 * hid, t.L3_gnn_mb2)):
                    n = hid if at < 3 * hid else 1
                    sync.dma_start(mlp[:, at:at + n], param.rearrange("a b -> (a b)").unsqueeze(0).to_broadcast([P, n])
                                   if len(param.shape) == 2 else param.unsqueeze(0).to_broadcast([P, n])
                                   ).then_inc(s.loaded, 16)
                sync.dma_start(g.x[:], t.x.rearrange("(b p) f -> p b f", p=P)).then_inc(s.x_loaded, 16)
                sync.wait_ge(s.x_loaded, 16)
                sync.wait_ge(s.kept, 1)
                sync.dma_start(g.offset_dram[:], g.offset[:]).then_inc(s.stored, 16)
                sync.dma_start(g.base_float_dram[:], g.base_float[:]).then_inc(s.stored, 16)
                sync.dma_start(g.half_offset_dram[:], g.half_offset[:]).then_inc(s.stored, 16)
                sync.dma_start(g.half_base_float_dram[:], g.half_base_float[:]).then_inc(s.stored, 16)
                sync.wait_ge(s.stored, 64)

            @block.gpsimd
            def _(pool):
                nc.gpsimd.iota(iota_int[:], [[1, P]], base=0, channel_multiplier=0).then_inc(s.iota, 1)
                nc.gpsimd.iota(lane_int[:], [[0, 1]], base=0, channel_multiplier=1).then_inc(s.iota, 1)

            @block.scalar
            def _(act):
                act.wait_ge(s.loaded, 16 * 13)
                for k in range(hid):
                    if k >= 2:
                        act.wait_ge(s.added, k - 1)
                    nc.scalar.activation(hidden[:, k % 2, :], attribute[:], ACT.Relu,
                                         bias=mlp[:, hid + k:hid + k + 1],
                                         scale=mlp[:, k:k + 1]).then_inc(s.relu, 1)
                act.wait_ge(s.added, hid)
                nc.scalar.activation(g.edge_values[:, :, 1], gate[:], ACT.Sigmoid,
                                     bias=mlp[:, 3 * hid:3 * hid + 1]).then_inc(s.gated, 1)
                act.wait_ge(s.gated, 1)

            @block.tensor
            def _(pe):
                pe.wait_ge(s.kept, 1)
                nc.tensor.matmul(turned[0:1, 0:P], small[:, 0:1], g.identity[:], start=True, stop=True)
                nc.tensor.matmul(turned[0:1, 3 * P:4 * P], small[:, 4:5], g.identity[:], start=True, stop=True)
                nc.tensor.matmul(turned[0:8, P:2 * P], small[:, 1:2].to_broadcast([P, 8]), g.identity[:],
                                 start=True, stop=True)
                nc.tensor.matmul(turned[0:8, 2 * P:3 * P], small[:, 2:3].to_broadcast([P, 8]), g.identity[:],
                                 start=True, stop=True).then_inc(s.turned, 1)

            @block.vector
            def _(dve):
                link = linker(dve, s.own)
                nc.vector.memset(g.source[:, g.tiles:], 0)
                nc.vector.memset(g.source_chunk[:, g.tiles:], 0)
                nc.vector.memset(g.offset[:, g.tiles:], -1.0)
                nc.vector.memset(g.edge_values[:, :, 2], 1.0)
                dve.wait_ge(s.iota, 2)
                nc.vector.tensor_copy(lane[:], lane_int[:])
                link(nc.vector.tensor_copy(g.iota[:], iota_int[:]))
                nc.vector.tensor_scalar(g.identity[:], g.iota[:], lane[:], None, ALU.is_equal)
                nc.vector.tensor_scalar(g.earlier[:], g.iota[:], lane[:], None, ALU.is_lt)
                link(nc.vector.tensor_scalar(small[:, 3:4], lane[:], float(g.blocks * P), None, ALU.add))
                dve.wait_ge(s.loaded, 16 * 13)
                nc.vector.tensor_copy(g.offset[:, 0:g.tiles], dst_int[:])
                nc.vector.tensor_copy(g.base_float[:], base_int[0:1, :])
                nc.vector.tensor_copy(g.half_base_float[:], base_int[0:1, ::HALF])
                nc.vector.tensor_copy(g.half_base[:], base_int[0:1, ::HALF])
                link(nc.vector.tensor_copy(g.source_float[:], g.source[:, 0:g.tiles + HALF]))
                nc.vector.tensor_scalar(g.to_spare[:], g.source_float[:], small[:, 3:4], -1.0,
                                        ALU.subtract, ALU.mult)
                link(nc.vector.tensor_copy(base_all[:], base_int[:]))
                link(nc.vector.tensor_tensor(
                    g.half_offset[:].rearrange("p (n k) -> p n k", k=HALF),
                    g.offset[:, 0:g.tiles].rearrange("p (n k) -> p n k", k=HALF),
                    base_all[:].rearrange("p (n k) -> p n k", k=HALF)[:, :, 0:1].to_broadcast([P, groups, HALF]),
                    ALU.subtract))
                link(nc.vector.tensor_tensor(g.offset[:, 0:g.tiles], g.offset[:, 0:g.tiles], base_all[:], ALU.subtract))
                nc.vector.tensor_copy(g.edge_values[:, :, 0], weight[:])
                link(nc.vector.tensor_tensor(g.keep[:], chunk_dst[:], chunk_before[:], ALU.is_equal))
                link(nc.vector.tensor_scalar(g.reset[:], g.keep[:], 1.0, BIG, ALU.subtract, ALU.mult))
                nc.vector.tensor_reduce(small[:, 0:1], g.offset[:, 0:g.tiles], AXX, ALU.max)
                nc.vector.tensor_reduce(small[:, 4:5], g.half_offset[:], AXX, ALU.max)
                nc.vector.tensor_reduce(small[:, 1:2], g.keep[:], AXX, ALU.min)
                nc.vector.tensor_reduce(small[:, 2:3], g.reset[:], AXX, ALU.min).then_inc(s.kept, 1)
                dve.wait_ge(s.turned, 1)
                nc.vector.tensor_copy(g.keep_row[:], turned[0:8, P:2 * P])
                nc.vector.tensor_copy(g.reset_row[:], turned[0:8, 2 * P:3 * P])
                nc.vector.tensor_reduce(widest[:, 0:1], turned[0:1, 0:P], AXX, ALU.max)
                link(nc.vector.tensor_reduce(widest[:, 1:2], turned[0:1, 3 * P:4 * P], AXX, ALU.max))
                link(nc.vector.tensor_scalar(widest[:], widest[:], 1.0 / P, 0.5 / P - 0.5, ALU.mult, ALU.add))
                nc.vector.tensor_copy(g.last_window[:], widest[:, 0:1])
                nc.vector.tensor_copy(g.half_last_window[:], widest[:, 1:2])
                for k in range(hid):
                    dve.wait_ge(s.relu, k + 1)
                    if k == 0:
                        nc.vector.tensor_scalar(gate[:], hidden[:, 0, :], mlp[:, 2 * hid:2 * hid + 1], None,
                                                ALU.mult).then_inc(s.added, 1)
                    else:
                        dve.wait_ge(s.added, k)
                        nc.vector.scalar_tensor_tensor(
                            gate[:], hidden[:, k % 2, :], mlp[:, 2 * hid + k:2 * hid + k + 1], gate[:],
                            ALU.mult, ALU.add).then_inc(s.added, 1)


def degrees(nc, g, histogram):
    with ExitStack() as stack:
        sbuf, psum = tiles_of(stack, nc)
        running = sbuf("running", [3, g.blocks * P])
        one = sbuf("one", [3, 1])
        counts = sbuf("counts", [P, g.blocks, 2])
        degree = sbuf("degree", [P, g.blocks])
        scratch = sbuf("scratch", [P, g.blocks])
        values = psum("values")[:, 0:3 * g.blocks].rearrange("p (b v) -> p b v", v=3)
        ends = psum("ends")[:, 0:3 * g.blocks].rearrange("p (b v) -> p b v", v=3)
        with phase(nc, "own", "counted", "turned", "rooted", "degree") as (block, s):
            @block.tensor
            def _(pe):
                pe.wait_ge(s.counted, 1)
                for b in range(g.blocks):
                    nc.tensor.matmul(values[:, b, :], histogram[:, b * P:(b + 1) * P],
                                     g.identity[0:3, 0:3], start=True, stop=True)
                    last = nc.tensor.matmul(ends[:, b, :], running[:, b * P:(b + 1) * P],
                                            g.identity[0:3, 0:3], start=True, stop=True)
                last.then_inc(s.turned, 1)

            @block.scalar
            def _(act):
                act.wait_ge(s.degree, 1)
                nc.scalar.activation(g.root_degree[:], degree[:], ACT.Sqrt).then_inc(s.rooted, 1)

            @block.vector
            def _(dve):
                link = linker(dve, s.own)
                link(nc.vector.memset(one[:], 1.0))
                nc.vector.tensor_tensor_scan(running[:], one[:].to_broadcast([3, g.blocks * P]), histogram[:],
                                             0.0, ALU.mult, ALU.add).then_inc(s.counted, 1)
                dve.wait_ge(s.turned, 1)
                nc.vector.tensor_copy(g.weight_sum[:], values[:, :, 0])
                nc.vector.tensor_scalar(degree[:], values[:, :, 1], 1.0, None, ALU.add).then_inc(s.degree, 1)
                nc.vector.tensor_copy(counts[:, :, 0], values[:, :, 2])
                link(nc.vector.tensor_copy(counts[:, :, 1], ends[:, :, 2]))
                link(nc.vector.tensor_scalar(g.nonempty[:], counts[:, :, 0], 0.5, None, ALU.is_gt))
                nc.vector.tensor_scalar(g.empty[:], counts[:, :, 0], 0.5, None, ALU.is_lt)
                link(nc.vector.tensor_tensor(counts[:, :, 0], counts[:, :, 1], counts[:, :, 0], ALU.subtract))
                link(nc.vector.tensor_scalar(counts[:, :, 1], counts[:, :, 1], 1.0, None, ALU.subtract))
                link(nc.vector.tensor_tensor(counts[:, :, 1], counts[:, :, 1], g.nonempty[:], ALU.mult))
                nc.vector.tensor_copy(g.last_edge[:], counts[:, :, 1])
                link(nc.vector.scalar_tensor_tensor(counts[:, :, 0], g.empty[:], float(2 * g.tiles * P),
                                                    counts[:, :, 0], ALU.mult, ALU.add))
                nc.vector.tensor_copy(g.first_edge[:], counts[:, :, 0])
                dve.wait_ge(s.rooted, 1)
                inverse_root(nc, link, degree, g.root_degree, scratch)


def segmented_scan(nc, g, values, out, columns, largest):
    start = -BIG if largest else 0.0
    first, op0, op1 = (g.reset, ALU.add, ALU.max) if largest else (g.keep, ALU.mult, ALU.add)
    row_first = g.reset_row if largest else g.keep_row
    with ExitStack() as stack:
        sbuf, psum = tiles_of(stack, nc)
        ends = sbuf("ends", [P, columns])
        row = sbuf("row", [columns, P + 1])
        carry = sbuf("carry", [P, columns])
        turned = psum("turned")
        with phase(nc, "own", "ended", "turned", "carried", "returned") as (block, s):
            @block.tensor
            def _(pe):
                pe.wait_ge(s.ended, 1)
                nc.tensor.matmul(turned[0:columns, 0:P], ends[:], g.identity[:], start=True,
                                 stop=True).then_inc(s.turned, 1)
                pe.wait_ge(s.carried, 1)
                nc.tensor.matmul(turned[:, P:P + columns], row[:, 0:P], g.identity[0:columns, 0:columns],
                                 start=True, stop=True).then_inc(s.returned, 1)

            @block.vector
            def _(dve):
                link = linker(dve, s.own)
                nc.vector.memset(row[:, 0:1], start)
                for c in range(columns):
                    last = nc.vector.tensor_tensor_scan(out[:, :, c], first[:], values[:, :, c], start, op0, op1)
                link(last)
                nc.vector.tensor_copy(ends[:], out[:, g.tiles - 1, :]).then_inc(s.ended, 1)
                dve.wait_ge(s.turned, 1)
                nc.vector.tensor_tensor_scan(row[:, 1:P + 1], row_first[0:columns, :], turned[0:columns, 0:P],
                                             start, op0, op1).then_inc(s.carried, 1)
                dve.wait_ge(s.returned, 1)
                link(nc.vector.tensor_copy(carry[:], turned[:, P:P + columns]))
                for c in range(columns):
                    nc.vector.tensor_tensor_scan(out[:, :, c], first[:], values[:, :, c], carry[:, c:c + 1], op0, op1)


def gather_logits(nc, g, table, heads, out):
    with ExitStack() as stack:
        sbuf, _ = tiles_of(stack, nc)
        rows = sbuf("rows", [P, RING, heads])
        index = sbuf("index", [P, RING], INT32)
        with phase(nc, "index_ready", "issued", "copied", "gathered0", "gathered1") as (block, s):
            gathered = [s.gathered0, s.gathered1]

            @block.gpsimd
            def _(pool):
                with pool.Fori(0, g.tiles // RING) as i:
                    for k in range(RING):
                        if k % HALF == 0:
                            pool.wait_ge(s.index_ready, i * 2 + (k // HALF + 1))
                            pool.sem_inc(s.issued, 1)
                        nc.gpsimd.indirect_dma_start(
                            rows[:, k, :], None, table,
                            bass.IndirectOffsetOnAxis(ap=index[:, k:k + 1], axis=0),
                        ).then_inc(gathered[k // HALF], 16)

            @block.vector
            def _(dve):
                for half in range(2):
                    nc.vector.tensor_copy(index[:, half * HALF:(half + 1) * HALF],
                                          g.source_chunk[:, half * HALF:(half + 1) * HALF]
                                          ).then_inc(s.index_ready, 1)
                with dve.Fori(0, g.tiles // RING) as i:
                    for half in range(2):
                        at = half * HALF
                        dve.wait_ge(gathered[half], i * (16 * HALF) + 16 * HALF)
                        nc.vector.tensor_copy(out[:, bass.ds(i * RING + at, HALF), :],
                                              rows[:, at:at + HALF, :])
                        nc.vector.tensor_copy(index[:, at:at + HALF],
                                              g.source_chunk[:, bass.ds(i * RING + (RING + at), HALF)]
                                              ).then_inc(s.index_ready, 1)


def store_edges(nc, g, pairs):
    with phase(nc, "stored") as (block, s):
        @block.sync
        def _(sync):
            for dram, tile in pairs:
                sync.dma_start(dram, tile, allow_slow_non_contiguous=True).then_inc(s.stored, 16)
            sync.wait_ge(s.stored, 16 * len(pairs))


def at_last_edges(nc, g, edges, out, heads):
    with phase(nc, "gathered") as (block, s):
        @block.gpsimd
        def _(pool):
            for b in range(g.blocks):
                nc.gpsimd.indirect_dma_start(
                    out[:, b, :], None, edges,
                    bass.IndirectOffsetOnAxis(ap=g.last_edge[:, b:b + 1], axis=0)).then_inc(s.gathered, 16)
            pool.wait_ge(s.gathered, 16 * g.blocks)


def to_edges(nc, g, values, columns, scratch, spread, out):
    with phase(nc, "scattered", "loaded") as (block, s):
        @block.gpsimd
        def _(pool):
            for b in range(g.blocks):
                nc.gpsimd.indirect_dma_start(
                    scratch, bass.IndirectOffsetOnAxis(ap=g.first_edge[:, b:b + 1], axis=0),
                    values[:, b, :], None, bounds_check=g.tiles * P - 1, oob_is_err=False,
                ).then_inc(s.scattered, 16)
            pool.wait_ge(s.scattered, 16 * g.blocks)
            pool.dma_start(spread[:], scratch.rearrange("(p i) v -> p i v", p=P)).then_inc(s.loaded, 16)
            pool.wait_ge(s.loaded, 16)
    segmented_scan(nc, g, spread, out, columns, False)


def attention_bound(nc, g, heads):
    with ExitStack() as stack:
        sbuf, psum = tiles_of(stack, nc)
        extremes = sbuf("extremes", [P, 2 * heads])
        extreme = sbuf("extreme", [2 * heads, 1])
        on_lanes = sbuf("on_lanes", [2 * heads, P])
        ranges = sbuf("ranges", [P, heads])
        flags = sbuf("flags", [1, 3])
        turned = psum("turned")
        a_src = g.self_logits[:, :, 0:heads].rearrange("p b h -> p h b")
        with phase(nc, "own", "reduced", "turned", "spread_out", "returned") as (block, s):
            @block.tensor
            def _(pe):
                pe.wait_ge(s.reduced, 1)
                nc.tensor.matmul(turned[0:2 * heads, 0:P], extremes[:], g.identity[:], start=True,
                                 stop=True).then_inc(s.turned, 1)
                pe.wait_ge(s.spread_out, 1)
                nc.tensor.matmul(turned[:, P:P + 2 * heads], on_lanes[:], g.identity[0:2 * heads, 0:2 * heads],
                                 start=True, stop=True).then_inc(s.returned, 1)

            @block.vector
            def _(dve):
                link = linker(dve, s.own)
                nc.vector.tensor_reduce(extremes[:, 0:heads], a_src, AXX, ALU.max)
                link(nc.vector.tensor_reduce(extremes[:, heads:2 * heads], a_src, AXX, ALU.min))
                nc.vector.tensor_scalar(extremes[:, heads:2 * heads], extremes[:, heads:2 * heads], -1.0, None,
                                        ALU.mult).then_inc(s.reduced, 1)
                dve.wait_ge(s.turned, 1)
                link(nc.vector.tensor_reduce(extreme[:], turned[0:2 * heads, 0:P], AXX, ALU.max))
                nc.vector.tensor_copy(on_lanes[:], extreme[:].to_broadcast([2 * heads, P])
                                      ).then_inc(s.spread_out, 1)
                dve.wait_ge(s.returned, 1)
                link(nc.vector.tensor_copy(g.top[:, 0:heads], turned[:, P:P + heads]))
                link(nc.vector.tensor_tensor(ranges[:], g.top[:, 0:heads], turned[:, P + heads:P + 2 * heads],
                                             ALU.add))
                link(nc.vector.tensor_reduce(flags[:, 0:1], ranges[0:1, :], AXX, ALU.max))
                link(nc.vector.tensor_scalar(flags[:, 1:2], flags[:, 0:1], WIDEST, None, ALU.is_gt))
                link(nc.vector.tensor_scalar(flags[:, 2:3], flags[:, 1:2], 0.5, None, ALU.is_lt))
                link(nc.vector.tensor_copy(g.wide_range[:], flags[:, 1:2]))
                link(nc.vector.tensor_copy(g.narrow_range[:], flags[:, 2:3]))


def attend(nc, g, table, logits, features, heads, segment, scratch, planes):
    attention_bound(nc, g, heads)
    with entered_if(nc, g.wide_range):
        store_edges(nc, g, [(logits.rearrange("(b p) h -> p b h", p=P), g.self_logits[:, :, 0:heads])])
        attention(nc, g, logits, heads, segment, scratch[2 * heads], scratch[heads], planes)
        aggregate_windows(nc, g, table, features, g.alpha, heads)
        with phase(nc) as (block, s):
            @block.vector
            def _(dve):
                nc.vector.memset(g.z, 1.0)
    with entered_if(nc, g.narrow_range):
        with ExitStack() as stack:
            sbuf, _ = tiles_of(stack, nc)
            own_bound = sbuf("own_bound", [P, g.blocks, heads])
            a_dst = sbuf("a_dst", [P, g.blocks, heads])
            spread = sbuf("spread", [P, g.tiles, heads])
            filled = sbuf("filled", [P, g.tiles, heads])
            with phase(nc, "own", "exponents") as (block, s):
                @block.vector
                def _(dve):
                    link = linker(dve, s.own)
                    own, dst = g.alpha_self[:, :, 0:heads], g.self_logits[:, :, heads:2 * heads]
                    top = g.top[:, 0:heads].unsqueeze(1).to_broadcast([P, g.blocks, heads])
                    nc.vector.tensor_copy(a_dst[:], dst)
                    nc.vector.tensor_tensor(own, g.self_logits[:, :, 0:heads], dst, ALU.add)
                    link(nc.vector.tensor_tensor(own_bound[:], dst, top, ALU.add))
                    nc.vector.scalar_tensor_tensor(own, own, 0.2, own, ALU.mult, ALU.max)
                    link(nc.vector.scalar_tensor_tensor(own_bound[:], own_bound[:], 0.2, own_bound[:],
                                                        ALU.mult, ALU.max))
                    nc.vector.tensor_tensor(own, own, own_bound[:], ALU.subtract).then_inc(s.exponents, 1)

                @block.scalar
                def _(act):
                    act.wait_ge(s.exponents, 1)
                    own = g.alpha_self[:, :, 0:heads]
                    nc.scalar.activation(own, own, ACT.Exp)
            to_edges(nc, g, a_dst, heads, scratch[heads], spread, filled)
            lay_out_weights(nc, g, filled, None, spread, heads, planes)
        aggregate_windows(nc, g, table, features, g.alpha, heads, softmax=True)
        normalisers(nc, g, heads)


def normalisers(nc, g, heads):
    banks, per_bank = 4, 4
    with ExitStack() as stack:
        _, psum = tiles_of(stack, nc)
        turned = [psum(f"turned{n}") for n in range(banks)]
        groups = [range(b, min(b + per_bank, g.blocks)) for b in range(0, g.blocks, per_bank)]
        with phase(nc, "turned", "added") as (block, s):
            @block.tensor
            def _(pe):
                for n, group in enumerate(groups):
                    if n >= banks:
                        pe.wait_ge(s.added, n - banks + 1)
                    for k, b in enumerate(group):
                        last = nc.tensor.matmul(turned[n % banks][0:heads, k * P:(k + 1) * P],
                                                g.alpha_self[:, b, 0:heads], g.identity[:], start=True, stop=True)
                    last.then_inc(s.turned, 1)

            @block.vector
            def _(dve):
                for n, group in enumerate(groups):
                    here = slice(group[0] * P, (group[-1] + 1) * P)
                    dve.wait_ge(s.turned, n + 1)
                    nc.vector.tensor_tensor(g.z[:, here], g.z[:, here], turned[n % banks][0:heads, 0:len(group) * P],
                                            ALU.add).then_inc(s.added, 1)
                dve.wait_ge(s.added, len(groups))
                nc.vector.reciprocal(g.z, g.z)


def attention(nc, g, table, heads, scratch_sums, scratch_pair, scratch_one, scratch_planes):
    both = 2 * heads
    with ExitStack() as stack:
        sbuf, psum = tiles_of(stack, nc)
        logit = sbuf("logit", [P, g.tiles, heads])
        best = sbuf("best", [P, g.tiles, heads])
        whole, size = g.acc[:].rearrange("p c n -> p (c n)"), g.tiles * both
        spread = whole[:, 0:size].rearrange("p (i v) -> p i v", v=both)
        pair = whole[:, size:2 * size].rearrange("p (i v) -> p i v", v=both)
        node = sbuf("node", [P, g.blocks, heads])
        node_self = sbuf("node_self", [P, g.blocks, heads])
        node_pair = sbuf("node_pair", [P, g.blocks, both])
        node_one = sbuf("node_one", [P, g.blocks, heads])
        mask = g.nonempty[:].unsqueeze(2).to_broadcast([P, g.blocks, heads])
        mask_empty = g.empty[:].unsqueeze(2).to_broadcast([P, g.blocks, heads])
        a_src, a_dst = g.self_logits[:, :, 0:heads], g.self_logits[:, :, heads:both]
        d_node, m_node = node_pair[:, :, 0:heads], node_pair[:, :, heads:both]

        gather_logits(nc, g, table, heads, logit)
        segmented_scan(nc, g, logit, best, heads, True)
        store_edges(nc, g, [(scratch_sums.rearrange("(p i) v -> p i v", p=P), best[:])])
        at_last_edges(nc, g, scratch_sums, node, heads)
        with phase(nc, "own") as (block, s):
            @block.vector
            def _(dve):
                link = linker(dve, s.own)
                link(nc.vector.tensor_tensor(node[:], node[:], mask, ALU.mult))
                link(nc.vector.tensor_tensor(node_self[:], a_src, mask_empty, ALU.mult))
                link(nc.vector.tensor_tensor(node[:], node[:], node_self[:], ALU.add))
                link(nc.vector.tensor_tensor(node[:], node[:], a_src, ALU.max))
                link(nc.vector.tensor_tensor(node[:], node[:], a_dst, ALU.add))
                nc.vector.tensor_copy(d_node, a_dst)
                link(nc.vector.scalar_tensor_tensor(m_node, node[:], 0.2, node[:], ALU.mult, ALU.max))
                link(nc.vector.tensor_tensor(node_self[:], a_src, a_dst, ALU.add))
                link(nc.vector.scalar_tensor_tensor(node_self[:], node_self[:], 0.2, node_self[:], ALU.mult, ALU.max))
                link(nc.vector.tensor_tensor(node_self[:], node_self[:], m_node, ALU.subtract))
        to_edges(nc, g, node_pair, both, scratch_pair, spread, pair)
        with phase(nc, "own", "logits", "exponents") as (block, s):
            @block.vector
            def _(dve):
                link = linker(dve, s.own)
                link(nc.vector.tensor_tensor(logit[:], logit[:], pair[:, :, 0:heads], ALU.add))
                link(nc.vector.scalar_tensor_tensor(logit[:], logit[:], 0.2, logit[:], ALU.mult, ALU.max))
                nc.vector.tensor_tensor(logit[:], logit[:], pair[:, :, heads:both], ALU.subtract
                                        ).then_inc(s.logits, 1)

            @block.scalar
            def _(act):
                nc.scalar.activation(node_self[:], node_self[:], ACT.Exp)
                act.wait_ge(s.logits, 1)
                nc.scalar.activation(logit[:], logit[:], ACT.Exp).then_inc(s.exponents, 1)
        segmented_scan(nc, g, logit, best, heads, False)
        store_edges(nc, g, [(scratch_sums.rearrange("(p i) v -> p i v", p=P), best[:])])
        at_last_edges(nc, g, scratch_sums, node, heads)
        with phase(nc, "own") as (block, s):
            @block.vector
            def _(dve):
                link = linker(dve, s.own)
                link(nc.vector.tensor_tensor(node[:], node[:], mask, ALU.mult))
                link(nc.vector.tensor_tensor(node[:], node[:], node_self[:], ALU.add))
                link(nc.vector.reciprocal(node_one[:], node[:]))
                link(nc.vector.tensor_tensor(g.alpha_self[:, :, 0:heads], node_self[:], node_one[:], ALU.mult))
        to_edges(nc, g, node_one, heads, scratch_one, best, pair[:, :, 0:heads])
        lay_out_weights(nc, g, logit, pair[:, :, 0:heads], spread, heads, scratch_planes)


def lay_out_weights(nc, g, exponents, inverse, spare, heads, planes):
    rows = max(r for r in range(1, P + 1) if g.tiles % r == 0)
    groups = g.tiles // rows
    spare = spare[:].rearrange("p i v -> p (i v)")
    product = spare[:, 0:heads * g.tiles].rearrange("p (h i) -> p h i", h=heads)
    with ExitStack() as stack:
        sbuf, psum = tiles_of(stack, nc)
        by_tile = sbuf("by_tile", [rows, heads, groups, P])
        turned = [psum(f"turned{n}") for n in range(BUFS)]
        with phase(nc, "product", "stored", "loaded", "turned", "copied") as (block, s):
            jobs = [(h, n) for h in range(heads) for n in range(groups)]

            @block.sync
            def _(sync):
                sync.wait_ge(s.product, 1)
                for h in range(heads):
                    sync.dma_start(planes[h].rearrange("(p i) -> p i", p=P), product[:, h, :]).then_inc(s.stored, 16)
                sync.wait_ge(s.stored, 16 * heads)
                for h in range(heads):
                    sync.dma_start(by_tile[:, h, :, :],
                                   planes[h].rearrange("(n r p) -> r n p", r=rows, p=P)).then_inc(s.loaded, 16)

            @block.tensor
            def _(pe):
                pe.wait_ge(s.loaded, 16 * heads)
                for n, (h, k) in enumerate(jobs):
                    if n >= BUFS:
                        pe.wait_ge(s.copied, n - BUFS + 1)
                    nc.tensor.matmul(turned[n % BUFS][:, 0:rows], by_tile[:, h, k, :],
                                     g.identity[0:rows, 0:rows], start=True, stop=True).then_inc(s.turned, 1)

            @block.vector
            def _(dve):
                if inverse is None:
                    nc.vector.tensor_copy(product, exponents[:].rearrange("p i h -> p h i")).then_inc(s.product, 1)
                else:
                    nc.vector.tensor_tensor(product, exponents[:].rearrange("p i h -> p h i"),
                                            inverse.rearrange("p i h -> p h i"), ALU.mult).then_inc(s.product, 1)
                for n, (h, k) in enumerate(jobs):
                    dve.wait_ge(s.turned, n + 1)
                    nc.vector.tensor_copy(g.alpha[:, h, k * rows:(k + 1) * rows],
                                          turned[n % BUFS][:, 0:rows]).then_inc(s.copied, 1)


def steps(blocks):
    return max(n for n in range(2, 12, 2) if blocks % n == 0)


def ring_of(body):
    depth = max(2, body // 2)
    return depth, min(2, depth - 1)


def combine(nc, g, spec):
    chunks = math.ceil(spec.features / P)
    width = spec.features // chunks
    both = spec.own == "x"
    own_rows = spec.own is not None and not both
    turn = spec.own is not None and spec.finish != "last"
    residual = spec.finish in ("relu", "add", "weight_sum", "last")
    columns = spec.columns
    body = steps(g.blocks)
    group = body // 2
    depth, ahead = ring_of(body)

    def nodes(i, j, count=1):
        return bass.ds(i * (body * P) + j * P, count * P)

    def blk(i, j):
        return bass.ds(i * body + j, 1)

    with ExitStack() as stack:
        sbuf, psum = tiles_of(stack, nc)
        if both:
            support_rows = sbuf("support_rows", [P, 2, group, COPIES, spec.features])
            two_sums = sbuf("two_sums", [P, depth, 2, spec.features])
            support_sum = sbuf("support_sum", [P, depth, spec.features])
            x_rows = sbuf("x_rows", [P, depth, spec.features])
        if own_rows:
            rows = sbuf("rows", [P, body, spec.features])
        if spec.heads:
            own_scaled = sbuf("own_scaled", [P, depth, spec.features])
            unscaled = sbuf("unscaled", [width, depth, chunks, P])
            selector = sbuf("selector", [spec.heads, chunks, P])
        if turn and not both:
            sums = sbuf("sums", [width, depth, chunks, P])
        if turn:
            left = sbuf("left", [width, depth, chunks, P])
        if both or not turn:
            aggregate_left = sbuf("aggregate_left", [width, depth, chunks, P])
        out = sbuf("out", [P, body, columns])
        turned = [psum(f"turned{n}") for n in range(depth)]
        product = [psum(f"product{n}") for n in range(2)]

        def view(tile):
            return tile[0:width, 0:chunks * P].rearrange("p (c n) -> p c n", c=chunks)

        def second_view(tile):
            return tile[0:width, chunks * P:2 * chunks * P].rearrange("p (c n) -> p c n", c=chunks)

        with phase(nc, "issued", "product_used", "added", "loaded0", "loaded1", "scaled", "copied", "turned", "summed", "left_ready",
                   "pairs_added", "selector_zeroed", "selector_ready", "own_added", "support_summed", "support_turned", "multiplied", "finished", "out_free",
                   "stored0", "stored1") as (block, s):
            loaded, stored = [s.loaded0, s.loaded1], [s.stored0, s.stored1]
            transfers = COPIES if both else 1

            if both or own_rows:
                @block.sync
                def _(sync):
                    with sync.Fori(0, g.blocks // body) as i:
                        for h in range(2):
                            sync.wait_ge(s.finished, i * body + (h + 1) * group)
                            for q in range(transfers):
                                table = spec.support[q] if both else spec.own
                                to = (support_rows[:, h, :, q, :] if both
                                      else rows[:, h * group:(h + 1) * group, :])
                                sync.dma_start(to, table[nodes(i, h * group, group), 0:spec.features]
                                               .rearrange("(b p) f -> p b f", p=P)).then_inc(loaded[h], 16)

            if not residual:
                @block.gpsimd
                def _(pool):
                    pool.sem_inc(s.out_free, body)
                    with pool.Fori(0, g.blocks // body) as i:
                        for h in range(2):
                            pool.wait_ge(s.finished, i * body + (body + (h + 1) * group))
                            pool.dma_start(
                                spec.store[nodes(i, h * group, group), :].rearrange("(b p) f -> p b f", p=P),
                                out[:, h * group:(h + 1) * group, 0:spec.stored_columns]
                            ).then_inc(stored[h], 16)
                        for h in range(2):
                            pool.wait_ge(stored[h], i * 16 + 16)
                            pool.sem_inc(s.out_free, group)

            def wait_loaded(engine, i, j):
                if j % group == 0:
                    engine.wait_ge(loaded[j // group], i * (16 * transfers) + 16 * transfers)

            @block.scalar
            def _(act):
                act.sem_inc(s.left_ready, depth)
                act.sem_inc(s.copied, depth)

                def first_stage(i, j):
                    b = j % depth
                    if both:
                        act.wait_ge(s.turned, i * body + (j + 1))
                        nc.scalar.copy(x_rows[:, b, :], g.x[:, blk(i, j), :].rearrange("p a f -> p (a f)")
                                       ).then_inc(s.scaled, 1)
                    elif not turn:
                        act.wait_ge(s.multiplied, i * body + (j + 1))
                        nc.scalar.copy(aggregate_left[:, b, :, :], g.acc[0:width, 0:chunks, nodes(i, j)]
                                       ).then_inc(s.copied, 1)
                    elif spec.heads:
                        share = spec.features // spec.heads
                        wait_loaded(act, i, j)
                        act.wait_ge(s.turned, i * body + (j + 1))
                        for h in range(spec.heads):
                            part = slice(h * share, (h + 1) * share)
                            last = nc.scalar.activation(
                                own_scaled[:, b, part], rows[:, j, part], ACT.Copy,
                                scale=g.alpha_self[:, blk(i, j), h:h + 1].rearrange("p a b -> p (a b)"))
                        last.then_inc(s.scaled, 1)

                def second_stage(i, j):
                    b = j % depth
                    if both:
                        act.wait_ge(s.support_turned, i * body + (j + 1))
                        act.wait_ge(s.multiplied, i * body + (j + 1))
                        nc.scalar.copy(left[:, b, :, :], view(turned[b])).then_inc(s.left_ready, 1)
                        nc.scalar.copy(aggregate_left[:, b, :, :], second_view(turned[b])).then_inc(s.copied, 1)
                    elif turn:
                        act.wait_ge(s.summed, i * body + (j + 1 + depth))
                        act.wait_ge(s.multiplied, i * body + (j + 1))
                        for c in range(chunks):
                            bias = spec.feature_bias[:, c:c + 1] if spec.feature_bias is not None else 0.0
                            last = nc.scalar.activation(left[:, b, c, :], sums[:, b, c, :],
                                                        ACT.Relu if spec.rectify else ACT.Identity, bias=bias)
                        last.then_inc(s.left_ready, 1)

                with act.Fori(0, g.blocks // body) as i:
                    for j in range(ahead):
                        first_stage(i, j)
                    for j in range(body):
                        if j + ahead < body:
                            first_stage(i, j + ahead)
                        second_stage(i, j)

            @block.tensor
            def _(pe):
                pe.sem_inc(s.turned, depth)
                pe.sem_inc(s.multiplied, depth)

                def turn_rows(i, j):
                    b = j % depth
                    if not turn:
                        return
                    if spec.heads or both:
                        pe.wait_ge(s.scaled, i * body + (j + 1))
                    else:
                        wait_loaded(pe, i, j)
                    if both:
                        pe.wait_ge(s.left_ready, i * body + (j + 1))
                        pe.wait_ge(s.copied, i * body + (j + 1))
                    else:
                        pe.wait_ge(s.summed, i * body + (j + 1))
                    for c in range(chunks):
                        part = slice(c * width, (c + 1) * width)
                        if both:
                            source = x_rows[:, b, part]
                        else:
                            source = own_scaled[:, b, part] if spec.heads else rows[:, j, part]
                        last = nc.tensor.matmul(turned[b][0:width, c * P:(c + 1) * P], source,
                                                g.identity[:], start=True, stop=True)
                    if spec.heads:
                        for c in range(chunks):
                            last = nc.tensor.matmul(turned[b][:, (chunks + c) * P:(chunks + c + 1) * P],
                                                    selector[:, c, :], g.z[:, nodes(i, j)],
                                                    start=True, stop=True)
                    last.then_inc(s.turned, 1)
                    if both:
                        pe.wait_ge(s.support_summed, i * body + (j + 1 + depth))
                        for c in range(chunks):
                            last = nc.tensor.matmul(turned[b][:, (chunks + c) * P:(chunks + c + 1) * P],
                                                    support_sum[:, b, c * P:(c + 1) * P], g.identity[:],
                                                    start=True, stop=True)
                        last.then_inc(s.support_turned, 1)

                def multiply(i, j):
                    b = j % depth
                    if turn:
                        pe.wait_ge(s.left_ready, i * body + (j + 1 + depth))
                    if both or not turn:
                        pe.wait_ge(s.copied, i * body + (j + 1 + depth))
                    if spec.finish == "logits":
                        pe.wait_ge(s.finished, i * body + (body + j - 1))
                    else:
                        pe.wait_ge(s.product_used, i * body + (j + 1))
                    if spec.finish == "last":
                        for c in range(chunks):
                            last = nc.tensor.matmul(product[j % 2][:, c * P:(c + 1) * P],
                                                    aggregate_left[:, b, c, :], g.identity[:],
                                                    start=True, stop=True)
                    else:
                        factors = []
                        if turn:
                            factors += [(left[:, b, c, :], spec.factor[0], c) for c in range(chunks)]
                        if both or not turn:
                            factors += [(aggregate_left[:, b, c, :], spec.factor[-1], c)
                                        for c in range(chunks)]
                        for n, (lhs, matrix, c) in enumerate(factors):
                            last = nc.tensor.matmul(product[j % 2][:, 0:columns], lhs, matrix[:, c, 0:columns],
                                                    start=(n == 0), stop=(n == len(factors) - 1))
                    last.then_inc(s.multiplied, 1)

                if spec.heads:
                    pe.wait_ge(s.selector_ready, 1)
                with pe.Fori(0, g.blocks // body) as i:
                    for j in range(ahead):
                        turn_rows(i, j)
                    for j in range(body):
                        if j + ahead < body:
                            turn_rows(i, j + ahead)
                        multiply(i, j)

            @block.vector
            def _(dve):
                if spec.heads:
                    share, per_chunk = spec.features // spec.heads, width * spec.heads // spec.features
                    nc.vector.memset(selector[:], 0.0).then_inc(s.selector_zeroed, 1)
                    dve.wait_ge(s.selector_zeroed, 1)
                    for c in range(chunks):
                        own_heads = g.identity[0:spec.heads, c * per_chunk:(c + 1) * per_chunk]
                        last = nc.vector.tensor_copy(
                            selector[:, c, 0:width].rearrange("h (a v) -> h a v", a=per_chunk),
                            own_heads.unsqueeze(2).to_broadcast([spec.heads, per_chunk, share]))
                    last.then_inc(s.selector_ready, 1)
                dve.sem_inc(s.finished, body)
                dve.sem_inc(s.product_used, 2)
                dve.sem_inc(s.summed, depth)
                dve.sem_inc(s.support_summed, depth)

                def add_own(i, j):
                    b = j % depth
                    if both:
                        wait_loaded(dve, i, j)
                        here = support_rows[:, j // group, j % group, :, :]
                        nc.vector.tensor_tensor(two_sums[:, b, :, :], here[:, 0:2, :], here[:, 2:4, :], ALU.add
                                                ).then_inc(s.pairs_added, 1)
                        dve.wait_ge(s.pairs_added, i * body + (j + 1))
                        dve.wait_ge(s.multiplied, i * body + (j + 1))
                        nc.vector.tensor_tensor(support_sum[:, b, :], two_sums[:, b, 0, :], two_sums[:, b, 1, :],
                                                ALU.add).then_inc(s.support_summed, 1)
                    elif turn:
                        dve.wait_ge(s.turned, i * body + (j + 1 + depth))
                        dve.wait_ge(s.left_ready, i * body + (j + 1))
                        if spec.heads:
                            nc.vector.tensor_tensor(unscaled[:, b, :, :], g.acc[0:width, 0:chunks, nodes(i, j)],
                                                    view(turned[b]), ALU.add).then_inc(s.own_added, 1)
                            dve.wait_ge(s.own_added, i * body + (j + 1))
                            nc.vector.tensor_tensor(
                                sums[:, b, :, :], unscaled[:, b, :, :],
                                second_view(turned[b]),
                                ALU.mult).then_inc(s.summed, 1)
                        else:
                            nc.vector.tensor_tensor(sums[:, b, :, :], g.acc[0:width, 0:chunks, nodes(i, j)],
                                                    view(turned[b]), ALU.add).then_inc(s.summed, 1)

                def use_product(i, j):
                    if spec.finish == "last":
                        wait_loaded(dve, i, j)
                    dve.wait_ge(s.multiplied, i * body + (j + 1 + depth))
                    if not residual and j % group == 0:
                        dve.wait_ge(s.out_free, i * body + (j + group))
                    got, to = product[j % 2][:, 0:columns], out[:, j, :]
                    if spec.finish in ("relu", "add"):
                        first = nc.vector.tensor_tensor(to, got, spec.bias[:], ALU.add)
                    elif spec.finish == "weight_sum":
                        first = nc.vector.scalar_tensor_tensor(to, spec.bias[:], g.weight_sum[:, blk(i, j)],
                                                               got, ALU.mult, ALU.add)
                    elif spec.finish == "last":
                        first = nc.vector.tensor_tensor(to, got, rows[:, j, :], ALU.add)
                    elif spec.finish == "scale":
                        first = nc.vector.scalar_tensor_tensor(to, got, g.root_degree[:, blk(i, j)],
                                                               spec.bias[:], ALU.mult, ALU.add)
                    else:
                        n = 2 * spec.stored_columns - columns
                        nc.vector.tensor_copy(
                            g.self_logits[:, blk(i, j), 0:columns - n].rearrange("p a v -> p (a v)"), got[:, n:])
                        n = spec.stored_columns
                        nc.vector.tensor_copy(to[:, 0:n], got[:, 0:n]).then_inc(s.finished, 1)
                        return
                    first.then_inc(s.product_used, 1)

                def end_or_add(i, j):
                    to, x = out[:, j, :], g.x[:, blk(i, j), :].rearrange("p a f -> p (a f)")
                    dve.wait_ge(s.product_used, i * body + (j + 3))
                    if spec.finish == "scale":
                        nc.vector.tensor_scalar(to, to, g.root_degree[:, blk(i, j)], None, ALU.mult
                                                ).then_inc(s.finished, 1)
                    elif spec.finish == "relu":
                        nc.vector.scalar_tensor_tensor(x, to, 0.0, x, ALU.max, ALU.add).then_inc(s.added, 1)
                    elif spec.finish == "last":
                        nc.vector.scalar_tensor_tensor(x, to, g.root_degree[:, blk(i, j)], x,
                                                       ALU.mult, ALU.add).then_inc(s.added, 1)
                    else:
                        nc.vector.tensor_tensor(x, x, to, ALU.add).then_inc(s.added, 1)

                def statistics(i, j):
                    dve.wait_ge(s.added, i * body + (j + 1))
                    dve.sem_inc(s.issued, 1)
                    nc.vector.bn_stats(g.stats[:, blk(i, j), :].rearrange("p a v -> p (a v)"),
                                       g.x[:, blk(i, j), :].rearrange("p a f -> p (a f)")
                                       ).then_inc(s.finished, 1)

                with dve.Fori(0, g.blocks // body) as i:
                    for j in range(ahead):
                        add_own(i, j)
                    for j in range(body + 2):
                        if j + ahead < body:
                            add_own(i, j + ahead)
                        if j < body:
                            use_product(i, j)
                        if spec.finish != "logits" and 1 <= j <= body:
                            end_or_add(i, j - 1)
                        if residual and j >= 2:
                            statistics(i, j - 2)


def project(nc, g, spec):
    chunks = g.features // P
    columns = spec.columns
    product_of = spec.finish != "norm"
    body = steps(g.blocks)
    group = body // 2
    depth, ahead = ring_of(body)
    further = min(ahead + 1, depth - 1)

    def nodes(i, j, count=1):
        return bass.ds(i * (body * P) + j * P, count * P)

    def blk(i, j):
        return bass.ds(i * body + j, 1)

    with ExitStack() as stack:
        sbuf, psum = tiles_of(stack, nc)
        if product_of:
            left = sbuf("left", [P, depth, chunks, P])
            normal = sbuf("normal", [P, depth, g.features])
            out = sbuf("out", [P, body, columns])
        mean = sbuf("mean", [P, g.blocks])
        variance = sbuf("variance", [P, g.blocks])
        spread = sbuf("spread", [P, g.blocks])
        root = sbuf("root", [P, g.blocks])
        turned = [psum(f"turned{n}") for n in range(depth)]
        product = [psum(f"product{n}") for n in range(2)]
        with phase(nc, "own", "variance_ready", "root_ready", "normed", "kept", "turned", "left_ready",
                   "multiplied", "biased", "finished", "out_free", "stored0", "stored1") as (block, s):
            stored = [s.stored0, s.stored1]

            @block.sync
            def _(sync):
                if not product_of:
                    for n, (dram, tile, b) in enumerate(spec.norm_stores):
                        sync.wait_ge(s.normed, b)
                        sync.dma_start(dram, tile).then_inc(stored[0], 16)
                    sync.wait_ge(stored[0], 16 * len(spec.norm_stores))
                    return
                sync.sem_inc(s.out_free, body)
                with sync.Fori(0, g.blocks // body) as i:
                    for h in range(2):
                        sync.wait_ge(s.finished, i * body + ((h + 1) * group + depth))
                        sync.dma_start(
                            spec.store[nodes(i, h * group, group), :].rearrange("(b p) f -> p b f", p=P),
                            out[:, h * group:(h + 1) * group, 0:spec.stored_columns]).then_inc(stored[h], 16)
                    for h in range(2):
                        sync.wait_ge(stored[h], i * 16 + 16)
                        sync.sem_inc(s.out_free, group)

            @block.scalar
            def _(act):
                act.wait_ge(s.variance_ready, 1)
                nc.scalar.activation(root[:], variance[:], ACT.Sqrt).then_inc(s.root_ready, 1)
                if not product_of:
                    return
                act.sem_inc(s.left_ready, depth)
                act.sem_inc(s.kept, depth)

                def keep(i, j):
                    act.wait_ge(s.normed, i * body + (j + 1))
                    nc.scalar.copy(g.x[:, blk(i, j), :].rearrange("p a f -> p (a f)"), normal[:, j % depth, :]
                                   ).then_inc(s.kept, 1)

                with act.Fori(0, g.blocks // body) as i:
                    for j in range(ahead):
                        keep(i, j)
                    for j in range(body):
                        if j + ahead < body:
                            keep(i, j + ahead)
                        act.wait_ge(s.turned, i * body + (j + 1 + depth))
                        act.wait_ge(s.multiplied, i * body + (j + 1))
                        nc.scalar.copy(left[:, j % depth, :, :],
                                       turned[j % depth][:, 0:chunks * P].rearrange("p (c n) -> p c n", c=chunks)
                                       ).then_inc(s.left_ready, 1)

            if product_of:
                @block.tensor
                def _(pe):
                    pe.sem_inc(s.turned, depth)
                    pe.sem_inc(s.multiplied, depth)

                    def turn_rows(i, j):
                        pe.wait_ge(s.normed, i * body + (j + 1))
                        pe.wait_ge(s.left_ready, i * body + (j + 1))
                        for c in range(chunks):
                            last = nc.tensor.matmul(turned[j % depth][:, c * P:(c + 1) * P],
                                                    normal[:, j % depth, c * P:(c + 1) * P],
                                                    g.identity[:], start=True, stop=True)
                        last.then_inc(s.turned, 1)

                    with pe.Fori(0, g.blocks // body) as i:
                        for j in range(ahead):
                            turn_rows(i, j)
                        for j in range(body):
                            if j + ahead < body:
                                turn_rows(i, j + ahead)
                            pe.wait_ge(s.left_ready, i * body + (j + 1 + depth))
                            pe.wait_ge(s.finished, i * body + (depth + j - 1))
                            for c in range(chunks):
                                last = nc.tensor.matmul(product[j % 2][:, 0:columns], left[:, j % depth, c, :],
                                                        spec.factor[:, c, 0:columns],
                                                        start=(c == 0), stop=(c == chunks - 1))
                            last.then_inc(s.multiplied, 1)

            @block.vector
            def _(dve):
                link = linker(dve, s.own)
                mean_even, mean_odd = g.stats[:, :, 1], g.stats[:, :, 4]
                link(nc.vector.tensor_tensor(mean[:], mean_even, mean_odd, ALU.add))
                link(nc.vector.tensor_scalar(mean[:], mean[:], 0.5, None, ALU.mult))
                link(nc.vector.tensor_tensor(spread[:], mean_even, mean_odd, ALU.subtract))
                link(nc.vector.scalar_tensor_tensor(spread[:], spread[:], 0.25, spread[:], ALU.mult, ALU.mult))
                link(nc.vector.tensor_tensor(variance[:], g.stats[:, :, 2], g.stats[:, :, 5], ALU.add))
                link(nc.vector.scalar_tensor_tensor(variance[:], variance[:], 1.0 / g.features, spread[:],
                                                    ALU.mult, ALU.add))
                link(nc.vector.tensor_scalar(variance[:], variance[:], 1e-5, None, ALU.add))
                dve.sem_inc(s.variance_ready, 1)
                dve.wait_ge(s.root_ready, 1)
                inverse_root(nc, link, variance, root, spread)
                dve.sem_inc(s.finished, depth)

                def normalise(i, j):
                    x = g.x[:, blk(i, j), :].rearrange("p a f -> p (a f)")
                    if product_of:
                        dve.wait_ge(s.kept, i * body + (j + 1))
                        dve.wait_ge(s.turned, i * body + (j + 1))
                    nc.vector.tensor_scalar(normal[:, j % depth, :] if product_of else x, x, mean[:, blk(i, j)],
                                            root[:, blk(i, j)], ALU.subtract, ALU.mult).then_inc(s.normed, 1)

                with dve.Fori(0, g.blocks // body) as i:
                    for j in range(further):
                        normalise(i, j)
                    for j in range(body):
                        if j + further < body:
                            normalise(i, j + further)
                        if not product_of:
                            continue
                        dve.wait_ge(s.multiplied, i * body + (j + 1 + depth))
                        if j % group == 0:
                            dve.wait_ge(s.out_free, i * body + (j + group))
                        got, to = product[j % 2][:, 0:columns], out[:, j, :]
                        if spec.finish == "scale":
                            nc.vector.tensor_tensor(to, got, spec.bias[:], ALU.add).then_inc(s.biased, 1)
                            dve.wait_ge(s.biased, i * body + (j + 1))
                            nc.vector.tensor_scalar(to, to, g.root_degree[:, blk(i, j)], None, ALU.mult
                                                    ).then_inc(s.finished, 1)
                        else:
                            n = 2 * spec.stored_columns - columns
                            nc.vector.tensor_copy(
                                g.self_logits[:, blk(i, j), 0:columns - n].rearrange("p a v -> p (a v)"), got[:, n:])
                            n = spec.stored_columns
                            nc.vector.tensor_copy(to[:, 0:n], got[:, 0:n]).then_inc(s.finished, 1)


def load(nc, *pairs):
    with phase(nc, "loaded") as (block, s):
        @block.sync
        def _(sync):
            for tile, dram in pairs:
                sync.dma_start(tile, dram, allow_slow_non_contiguous=True).then_inc(s.loaded, 16)
            sync.wait_ge(s.loaded, 16 * len(pairs))


def by_rows(weight):
    return weight.rearrange("(c p) n -> p c n", p=min(P, weight.shape[0]))


def on_all(bias):
    return bias.unsqueeze(0).to_broadcast([P, bias.shape[0]])


def attention_factor(nc, factor, weight, att_src, att_dst, stack):
    heads, share = att_src.shape
    n = heads * share
    sbuf, _ = tiles_of(stack, nc)
    with ExitStack() as inner:
        sbuf, _ = tiles_of(inner, nc)
        att = sbuf("att", [P, 2, n])
        each = sbuf("each", [P, 2, n])
        with phase(nc, "own", "loaded") as (block, s):
            @block.sync
            def _(sync):
                sync.dma_start(factor[:, :, 0:n], by_rows(weight)).then_inc(s.loaded, 16)
                for k, a in enumerate((att_src, att_dst)):
                    sync.dma_start(att[:, k, :], a.rearrange("h c -> (h c)").unsqueeze(0).to_broadcast([P, n])
                                   ).then_inc(s.loaded, 16)

            @block.vector
            def _(dve):
                link = linker(dve, s.own)
                dve.wait_ge(s.loaded, 48)
                for c in range(2):
                    for k in range(2):
                        link(nc.vector.tensor_tensor(each[:, c, :], factor[:, c, 0:n], att[:, k, :], ALU.mult))
                        link(nc.vector.tensor_reduce(factor[:, c, n + k * heads:n + (k + 1) * heads],
                                                     each[:, c, :].rearrange("p (h v) -> p h v", h=heads),
                                                     AXX, ALU.add))


def build_program(nc, t, output):
    nodes, features, edges = t.nodes, t.x.shape[1], t.edges
    tiles, blocks = sizes(nodes, edges)
    g = Graph()
    g.nodes, g.features, g.tiles, g.blocks = nodes, features, tiles, blocks
    padded, slots = blocks * P, tiles * P
    heads, hidden = t.L1_gnn_att_src1.shape

    def dram(name, shape):
        return nc.dram_tensor(name, shape, FP32, kind="Internal").ap()

    g.offset_dram = dram("offset_dram", [P, tiles + 2])
    g.base_float_dram = dram("base_float_dram", [1, tiles])
    g.half_offset_dram = dram("half_offset_dram", [P, tiles])
    g.half_base_float_dram = dram("half_base_float_dram", [1, tiles // HALF])
    g.source_flat, g.x_dram = t.src_flat, t.x
    support = [dram(f"support{n}", [padded + P, features]) for n in range(COPIES)]
    spare = dram("spare", [HALF, 2, P, P])
    rows1, rows2 = dram("gat_rows1", [padded, features + heads]), dram("gat_rows2", [padded, hidden + 1])
    x_part = dram("x_part", [heads, blocks, features])
    logits1, logits2 = dram("gat_logits1", [padded, heads]), dram("gat_logits2", [padded, 1])
    norm2 = dram("norm2", [padded, features])
    gcn = [dram(f"gcn_rows{n}", [padded, features]) for n in range(3)]
    scratch = {n: dram(f"scratch{n}", [slots, n]) for n in (2 * heads, heads, 2, 1)}
    segment = {n: dram(f"segment{n}", [slots, n]) for n in (heads, 1)}
    planes = dram("planes", [heads, slots])

    with ExitStack() as stack:
        sbuf, _ = tiles_of(stack, nc)
        g.source = sbuf("source", [P, tiles + RING], INT32)
        g.source_chunk = sbuf("source_chunk", [P, tiles + RING], INT32)
        g.offset = sbuf("offset", [P, tiles + 2])
        g.base = sbuf("base", [1, tiles], INT32)
        g.base_float = sbuf("base_float", [1, tiles])
        g.last_window = sbuf("last_window", [1, 1], INT32)
        g.edge_values = sbuf("edge_values", [P, tiles, 3])
        g.half_base = sbuf("half_base", [1, tiles // HALF], INT32)
        g.half_base_float = sbuf("half_base_float", [1, tiles // HALF])
        g.half_last_window = sbuf("half_last_window", [1, 1], INT32)
        g.half_offset = sbuf("half_offset", [P, tiles])
        g.source_float = sbuf("source_float", [P, tiles + HALF])
        g.to_spare = sbuf("to_spare", [P, tiles + HALF])
        g.earlier = sbuf("earlier", [P, P])
        g.keep = sbuf("keep", [P, tiles])
        g.reset = sbuf("reset", [P, tiles])
        g.keep_row = sbuf("keep_row", [8, P])
        g.reset_row = sbuf("reset_row", [8, P])
        g.iota = sbuf("iota", [P, P])
        g.identity = sbuf("identity", [P, P])
        g.x = sbuf("x", [P, blocks, features])
        g.stats = sbuf("stats", [P, blocks, 6])
        g.weight_sum = sbuf("weight_sum", [P, blocks])
        g.root_degree = sbuf("root_degree", [P, blocks])
        g.nonempty = sbuf("nonempty", [P, blocks])
        g.empty = sbuf("empty", [P, blocks])
        g.first_edge = sbuf("first_edge", [P, blocks], INT32)
        g.last_edge = sbuf("last_edge", [P, blocks], INT32)
        g.self_logits = sbuf("self_logits", [P, blocks, 2 * heads])
        g.alpha_self = sbuf("alpha_self", [P, blocks, heads])
        edge_weight = g.edge_values[:, :, 0:1].rearrange("p i a -> p a i")
        gate = g.edge_values[:, :, 1:2].rearrange("p i a -> p a i")

        def scoped():
            inner = ExitStack()
            return inner, tiles_of(inner, nc)[0]

        def spec(**fields):
            base = dict(features=features, own=None, heads=0, factor=None, feature_bias=None, rectify=False,
                        columns=features, bias=None, store=None, stored_columns=features)
            base.update(fields)
            return namedtuple("Spec", list(base))(**base)

        set_up(nc, g, t)
        zero_scratch(nc, g, scratch)

        inner, part = scoped()
        with inner:
            with ExitStack() as first:
                histogram = tiles_of(first, nc)[0]("histogram", [3, padded])
                windows(nc, g, lambda first: scatter_by_source(nc, g, support, spare, histogram, first),
                        (g.half_offset, g.half_base_float, g.half_base, g.half_offset_dram,
                         g.half_base_float_dram, g.half_last_window))
                degrees(nc, g, histogram)
            top, bottom = part("top", [P, 2, features]), part("bottom", [P, 2, features])
            bias = part("bias", [P, features])
            load(nc, (top[:], by_rows(t.L0_gnn_W[0:features, :])), (bottom[:], by_rows(t.L0_gnn_W[features:, :])),
                 (bias[:], on_all(t.L0_gnn_b)))
            combine(nc, g, spec(own="x", support=support, factor=[top, bottom], bias=bias, finish="relu"))
        g.alpha = sbuf("alpha", [P, heads, tiles + BATCH])
        g.top = sbuf("top", [P, heads])
        g.wide_range = sbuf("wide_range", [1, 1], INT32)
        g.narrow_range = sbuf("narrow_range", [1, 1], INT32)
        with phase(nc) as (block, s):
            @block.vector
            def _(dve):
                nc.vector.memset(g.alpha[:, :, tiles:tiles + BATCH], 0.0)

        inner, part = scoped()
        with inner as held:
            factor = part("factor", [P, 2, features + 2 * heads])
            attention_factor(nc, factor, t.L1_gnn_W1, t.L1_gnn_att_src1, t.L1_gnn_att_dst1, held)
            project(nc, g, spec(factor=factor, columns=features + 2 * heads, store=rows1,
                                stored_columns=features + heads, finish="logits"))
        store_edges(nc, g, [(x_part[:], g.x[0:heads])])
        g.z = g.x[0:heads].rearrange("h b f -> h (b f)")[:, 0:padded]
        inner, part = scoped()
        with inner as held:
            g.acc = part("acc", [P, 2, padded])
            attend(nc, g, rows1, logits1, features, heads, segment[heads], scratch, planes)
            factor = part("factor", [P, 2, hidden + 2])
            attention_factor(nc, factor, t.L1_gnn_W2, t.L1_gnn_att_src2, t.L1_gnn_att_dst2, held)
            bias = part("bias", [P, 2])
            load(nc, *((bias[:, c:c + 1], t.L1_gnn_b1[c * P:(c + 1) * P].unsqueeze(1)) for c in range(2)))
            combine(nc, g, spec(own=rows1, heads=heads, factor=[factor], feature_bias=bias, rectify=True,
                                columns=hidden + 2, store=rows2, stored_columns=hidden + 1, finish="logits"))
        load(nc, (g.x[0:heads], x_part[:]))

        inner, part = scoped()
        with inner:
            g.acc = part("acc", [P, 2, padded])
            g.z = g.acc[0:1, 1, :]
            attend(nc, g, rows2, logits2, hidden, 1, segment[1], scratch, planes)
            factor = part("factor", [hidden, 1, features])
            feature_bias, bias = part("feature_bias", [hidden, 1]), part("bias", [P, features])
            load(nc, (factor[:], by_rows(t.L1_gnn_Wf)), (feature_bias[:], t.L1_gnn_b2.unsqueeze(1)),
                 (bias[:], on_all(t.L1_gnn_bf)))
            combine(nc, g, spec(own=rows2, features=hidden, heads=1, factor=[factor], feature_bias=feature_bias,
                                bias=bias, finish="add"))
        norm_store = [(norm2.rearrange("(b p) f -> p b f", p=P)[:, b:min(b + 10, blocks), :],
                       g.x[:, b:min(b + 10, blocks), :], min(b + 10, blocks)) for b in range(0, blocks, 10)]
        project(nc, g, spec(finish="norm", norm_stores=norm_store))

        inner, part = scoped()
        with inner:
            g.acc = part("acc", [P, 2, padded])
            aggregate_windows(nc, g, norm2, features, edge_weight, 1)
            factor, bias = part("factor", [P, 2, features]), part("bias", [P, features])
            load(nc, (factor[:], by_rows(t.L2_gnn_weight)), (bias[:], on_all(t.L2_gnn_bias)))
            combine(nc, g, spec(factor=[factor], bias=bias, finish="weight_sum"))

        inner, part = scoped()
        with inner:
            factor, bias = part("factor", [P, 2, features]), part("bias", [P, features])
            g.acc = part("acc", [P, 2, padded])
            load(nc, (factor[:], by_rows(t.L3_gnn_W1)), (bias[:], on_all(t.L3_gnn_b1)))
            project(nc, g, spec(factor=factor, bias=bias, store=gcn[0], finish="scale"))
            for n, (w, b) in enumerate(((t.L3_gnn_W2, t.L3_gnn_b2), (t.L3_gnn_W3, t.L3_gnn_b3))):
                aggregate_windows(nc, g, gcn[n], features, gate, 1)
                load(nc, (factor[:], by_rows(w)), (bias[:], on_all(b)))
                combine(nc, g, spec(own=gcn[n], factor=[factor], bias=bias, rectify=True, store=gcn[n + 1],
                                    finish="scale"))
            aggregate_windows(nc, g, gcn[2], features, gate, 1)
            combine(nc, g, spec(own=gcn[2], finish="last"))
        full, rest = nodes // P, nodes % P
        out_stores = [(output[b * P:min(b + 8, full) * P, :].rearrange("(b p) f -> p b f", p=P),
                       g.x[:, b:min(b + 8, full), :], min(b + 8, full)) for b in range(0, full, 8)]
        if rest:
            out_stores.append((output[full * P:nodes, :], g.x[0:rest, full, :], full + 1))
        project(nc, g, spec(finish="norm", norm_stores=out_stores))


def zero_scratch(nc, g, scratch):
    with ExitStack() as stack:
        sbuf, _ = tiles_of(stack, nc)
        most = max(scratch)
        zeros = sbuf("zeros", [P, g.tiles * most])
        with phase(nc, "zeroed", "stored") as (block, s):
            @block.vector
            def _(dve):
                nc.vector.memset(zeros[:], 0.0).then_inc(s.zeroed, 1)

            @block.sync
            def _(sync):
                sync.wait_ge(s.zeroed, 1)
                for n, dram in scratch.items():
                    sync.dma_start(dram.rearrange("(p i) v -> p (i v)", p=P), zeros[:, 0:g.tiles * n]
                                   ).then_inc(s.stored, 16)
                sync.wait_ge(s.stored, 16 * len(scratch))


_PLAIN = ["L0_gnn_W", "L0_gnn_b", "L1_gnn_W1", "L1_gnn_att_src1", "L1_gnn_att_dst1", "L1_gnn_b1",
          "L1_gnn_W2", "L1_gnn_att_src2", "L1_gnn_att_dst2", "L1_gnn_b2", "L1_gnn_Wf", "L1_gnn_bf",
          "L2_gnn_weight", "L2_gnn_bias", "L3_gnn_W1", "L3_gnn_b1", "L3_gnn_W2", "L3_gnn_b2", "L3_gnn_W3",
          "L3_gnn_b3", "L3_gnn_mw1", "L3_gnn_mb1", "L3_gnn_mw2", "L3_gnn_mb2"]


def lay_out(inputs):
    nodes, edges = inputs["x"].shape[0], inputs["src"].shape[0]
    tiles, blocks = sizes(nodes, edges)

    def pad(a, value, front=0):
        a = np.asarray(a).reshape(-1)
        whole = np.full(tiles * P + front, value, a.dtype)
        whole[front:front + edges] = a
        return whole[:tiles * P]

    def by_tile(a):
        return np.ascontiguousarray(a.reshape(tiles, P).T)

    src, dst = pad(inputs["src"], 0), pad(inputs["dst"], nodes)
    before = np.concatenate([np.full(1, -1, dst.dtype), dst[:-1]])
    arrays = {n: np.ascontiguousarray(inputs[n]) for n in _PLAIN}
    x = np.zeros((blocks * P, inputs["x"].shape[1]), np.float32)
    x[:nodes] = inputs["x"]
    arrays.update(x=x, src_flat=src.reshape(1, -1), src_tile=by_tile(src), src_chunk=src.reshape(P, tiles), dst_tile=by_tile(dst),
                  dst_chunk=dst.reshape(P, tiles), before_chunk=before.reshape(P, tiles),
                  weight_tile=by_tile(pad(inputs["edge_weight"], 0)),
                  attr_tile=by_tile(pad(inputs["edge_weight1"], 0)))
    return arrays


def kernel(**inputs):
    import concourse.bacc as bacc
    from concourse.bass_utils import run_bass_kernel_spmd

    arrays = lay_out(inputs)
    nc = bacc.Bacc("TRN2", target_bir_lowering=False, num_devices=1)
    t = {n: nc.dram_tensor(f"in_{n}", a.shape, mybir.dt.from_np(a.dtype), kind="ExternalInput").ap()
         for n, a in arrays.items()}
    t.update(nodes=inputs["x"].shape[0], edges=inputs["src"].shape[0])
    output = nc.dram_tensor("out", inputs["x"].shape, FP32, kind="ExternalOutput").ap()
    build_program(nc, namedtuple("Tensors", list(t))(**t), output)
    result = run_bass_kernel_spmd(nc, [{f"in_{n}": a for n, a in arrays.items()}], core_ids=[0])
    return result.results[0]["out"]
```
